# Optimizing a Trainium2 kernel written in Bass

```python
import numpy as np
import jax
import jax.numpy as jnp

def _softmax(x, axis=-1):
    return jax.nn.softmax(x, axis=axis)

def _gelu(x):
    return jax.nn.gelu(x, approximate=True)

def _silu(x):
    return jax.nn.silu(x)

def _sigmoid(x):
    return jax.nn.sigmoid(x)

def _layernorm(x, axis=-1, eps=1e-05):
    m = jnp.mean(x, axis=axis, keepdims=True)
    v = jnp.var(x, axis=axis, keepdims=True)
    return (x - m) / jnp.sqrt(v + eps)

def _scatter_add(tgt, idx, src, axis=0):
    return tgt.at[idx].add(src)

def _segment_sum(src, seg, n):
    return jax.ops.segment_sum(src, seg, n)
kernel_name = 'mk_gnn_resnorm_d4_gnn_r32_94e601'

def setup_inputs(seed: int=0):
    np.random.seed(seed)
    _w = jnp.asarray

    def _rec_inputs():
        import jax
        import jax.numpy as jnp
        _gk = jax.random.key(seed)
        x = -0.0006008 + 1.001 * jax.random.normal(jax.random.fold_in(_gk, 1), (50000, 256), jnp.float32)
        src = jax.random.randint(jax.random.fold_in(_gk, 2), (25000,), 0, 50000, jnp.int32)
        dst = jax.random.randint(jax.random.fold_in(_gk, 3), (25000,), 0, 50000, jnp.int32)
        _o = jnp.argsort(dst, stable=True)
        src = src[_o]
        dst = dst[_o]
        edge_attr_64 = 0.000151818 + 1.00006 * jax.random.normal(jax.random.fold_in(_gk, 12), (25000, 64), jnp.float32)
        edge_weight = jax.random.uniform(jax.random.fold_in(_gk, 14), (25000,), jnp.float32, 0.0, 0.999998)
        return (x, src, dst, edge_attr_64, edge_weight)
    x, src, dst, edge_attr_64, edge_weight = _rec_inputs()

    def _L0_gnn_setup():
        import jax, jax.numpy as jnp
        import numpy as np
        import math
        HIDDEN = 256
        NUM_GAUSSIANS = 64
        NUM_FILTERS = 256
        CUTOFF = 1.0
        COSINE_OFFSET = 0.0
        N_NODES = 10000
        N_EDGES = 10000

        def ssp(x):
            return jax.nn.softplus(x) - jnp.log(2.0).astype(x.dtype)
        key = jax.random.key(seed)
        ks = jax.random.split(key, 12)

        def xavier(k, fan_out, fan_in):
            a = math.sqrt(6.0 / (fan_in + fan_out))
            return jax.random.uniform(k, (fan_out, fan_in), jnp.float32, -a, a)
        x = jax.random.normal(ks[0], (N_NODES, HIDDEN), jnp.float32)
        ji_pairs = jax.random.randint(ks[1], (2, N_EDGES), 0, N_NODES, jnp.int64)
        e_ji = jax.random.uniform(ks[2], (N_EDGES,), jnp.float32)
        e_ji_basis = jax.random.normal(ks[3], (N_EDGES, NUM_GAUSSIANS), jnp.float32)
        return {'x': x, 'ji_pairs': ji_pairs, 'e_ji': e_ji, 'e_ji_basis': e_ji_basis, 'fw1': xavier(ks[4], NUM_FILTERS, NUM_GAUSSIANS), 'fb1': jnp.zeros((NUM_FILTERS,), jnp.float32), 'fw2': xavier(ks[5], NUM_FILTERS, NUM_FILTERS), 'fb2': jnp.zeros((NUM_FILTERS,), jnp.float32), 'w1': xavier(ks[6], NUM_FILTERS, HIDDEN), 'w2': xavier(ks[7], HIDDEN, NUM_FILTERS), 'b2': jnp.zeros((HIDDEN,), jnp.float32), 'w3': xavier(ks[8], HIDDEN, HIDDEN), 'b3': jnp.zeros((HIDDEN,), jnp.float32)}
    _L0_gnn_all = _L0_gnn_setup()
    _L0_gnn_in = {k: v for k, v in _L0_gnn_all.items() if k in ('fw1', 'fb1', 'fw2', 'fb2', 'w1', 'w2', 'b2', 'w3', 'b3')}
    del _L0_gnn_all

    def _L1_gnn_setup():
        import jax, jax.numpy as jnp
        import numpy as np
        N_NODES = 3125
        N_EDGES = 50000
        D_FEAT = 256
        LAYERS = 3
        EPS = 1e-12

        def _spmm(vals, row, col, h, n_nodes):
            msgs = vals[:, None] * h[col]
            return jax.ops.segment_sum(msgs, row, num_segments=n_nodes, indices_are_sorted=True)

        def _l2_normalize(h):
            norm = jnp.sqrt(jnp.sum(h * h, axis=-1, keepdims=True))
            return h / jnp.maximum(norm, EPS)
        key = jax.random.key(seed)
        k1, k2, k3, k4 = jax.random.split(key, 4)
        x = jax.random.normal(k1, (N_NODES, D_FEAT), dtype=jnp.float32)
        vals = jax.random.uniform(k2, (N_EDGES,), dtype=jnp.float32)
        row = jnp.sort(jax.random.randint(k3, (N_EDGES,), 0, N_NODES, dtype=jnp.int32))
        col = jax.random.randint(k4, (N_EDGES,), 0, N_NODES, dtype=jnp.int32)
        return {'x': x, 'vals': vals, 'row': row, 'col': col}
    _L1_gnn_all = _L1_gnn_setup()
    _L1_gnn_in = {k: v for k, v in _L1_gnn_all.items() if k in ()}
    del _L1_gnn_all

    def _L2_gnn_setup():
        import jax, jax.numpy as jnp
        import numpy as np
        HEADS = 4
        OUT_CH = 64
        NEG_SLOPE = 0.2
        key = jax.random.key(seed)
        k1, k2, k3, k4, k5 = jax.random.split(key, 5)
        N, E, IN = (50000, 50000, 256)
        x = jax.random.normal(k1, (N, IN), dtype=jnp.float32)
        edge_index = jax.random.randint(k2, (2, E), 0, N, dtype=jnp.int32)
        W = jax.random.normal(k3, (IN, HEADS * OUT_CH), dtype=jnp.float32) * (1.0 / np.sqrt(IN))
        att_src = jax.random.normal(k4, (HEADS, OUT_CH), dtype=jnp.float32) * 0.1
        att_dst = jax.random.normal(k5, (HEADS, OUT_CH), dtype=jnp.float32) * 0.1
        bias = jnp.zeros((HEADS * OUT_CH,), dtype=jnp.float32)
        return {'x': x, 'edge_index': edge_index, 'W': W, 'att_src': att_src, 'att_dst': att_dst, 'bias': bias}
    _L2_gnn_all = _L2_gnn_setup()
    _L2_gnn_in = {k: v for k, v in _L2_gnn_all.items() if k in ('W', 'att_src', 'att_dst', 'bias')}
    del _L2_gnn_all

    def _L3_gnn_setup():
        import jax, jax.numpy as jnp
        import numpy as np
        N_NODES = 50000
        N_EDGES = 25000
        DIM = 256
        NUM_HEADS = 8
        key = jax.random.key(seed)
        k_x, k_wu, k_bu, k_wv, k_src, k_dst = jax.random.split(key, 6)
        x = jax.random.normal(k_x, (N_NODES, DIM), dtype=jnp.float32)
        W_u = jax.random.normal(k_wu, (NUM_HEADS, DIM), dtype=jnp.float32) * (1.0 / np.sqrt(DIM))
        b_u = jax.random.normal(k_bu, (NUM_HEADS,), dtype=jnp.float32) * 0.01
        W_v = jax.random.normal(k_wv, (NUM_HEADS, DIM), dtype=jnp.float32) * (1.0 / np.sqrt(DIM))
        src = jax.random.randint(k_src, (N_EDGES,), 0, N_NODES, dtype=jnp.int32)
        dst = jax.random.randint(k_dst, (N_EDGES,), 0, N_NODES, dtype=jnp.int32)
        return {'x': x, 'W_u': W_u, 'b_u': b_u, 'W_v': W_v, 'src': src, 'dst': dst}
    _L3_gnn_all = _L3_gnn_setup()
    _L3_gnn_in = {k: v for k, v in _L3_gnn_all.items() if k in ('W_u', 'b_u', 'W_v')}
    del _L3_gnn_all
    return {'x': x, 'src': src, 'dst': dst, 'edge_attr_64': edge_attr_64, 'edge_weight': edge_weight, 'L0_gnn_fw1': _L0_gnn_in['fw1'], 'L0_gnn_fb1': _L0_gnn_in['fb1'], 'L0_gnn_fw2': _L0_gnn_in['fw2'], 'L0_gnn_fb2': _L0_gnn_in['fb2'], 'L0_gnn_w1': _L0_gnn_in['w1'], 'L0_gnn_w2': _L0_gnn_in['w2'], 'L0_gnn_b2': _L0_gnn_in['b2'], 'L0_gnn_w3': _L0_gnn_in['w3'], 'L0_gnn_b3': _L0_gnn_in['b3'], 'L2_gnn_W': _L2_gnn_in['W'], 'L2_gnn_att_src': _L2_gnn_in['att_src'], 'L2_gnn_att_dst': _L2_gnn_in['att_dst'], 'L2_gnn_bias': _L2_gnn_in['bias'], 'L3_gnn_W_u': _L3_gnn_in['W_u'], 'L3_gnn_b_u': _L3_gnn_in['b_u'], 'L3_gnn_W_v': _L3_gnn_in['W_v']}

def reference(x, src, dst, edge_attr_64, edge_weight, L0_gnn_fw1, L0_gnn_fb1, L0_gnn_fw2, L0_gnn_fb2, L0_gnn_w1, L0_gnn_w2, L0_gnn_b2, L0_gnn_w3, L0_gnn_b3, L2_gnn_W, L2_gnn_att_src, L2_gnn_att_dst, L2_gnn_bias, L3_gnn_W_u, L3_gnn_b_u, L3_gnn_W_v):
    import jax
    import jax.numpy as jnp

    def _L0_gnn_ref(x, ji_pairs, e_ji, e_ji_basis, fw1, fb1, fw2, fb2, w1, w2, b2, w3, b3):
        import jax, jax.numpy as jnp
        import numpy as np
        import math
        HIDDEN = 256
        NUM_GAUSSIANS = 64
        NUM_FILTERS = 256
        CUTOFF = 1.0
        COSINE_OFFSET = 0.0
        N_NODES = 10000
        N_EDGES = 10000

        def ssp(x):
            return jax.nn.softplus(x) - jnp.log(2.0).astype(x.dtype)
        pi = jnp.asarray(math.pi, x.dtype)
        C = 0.25 * (jnp.cos((e_ji - COSINE_OFFSET) * pi / (CUTOFF - COSINE_OFFSET)) + 1.0)
        W = ssp(e_ji_basis @ fw1.T + fb1) @ fw2.T + fb2
        W = W * C[:, None]
        h = x @ w1.T
        src, dst = (ji_pairs[0], ji_pairs[1])
        msg = h[src] * W
        agg = jax.ops.segment_sum(msg, dst, num_segments=x.shape[0])
        out = agg @ w2.T + b2
        out = ssp(out) @ w3.T + b3
        return out

    def _L1_gnn_ref(x, vals, row, col):
        import jax, jax.numpy as jnp
        import numpy as np
        N_NODES = 3125
        N_EDGES = 50000
        D_FEAT = 256
        LAYERS = 3
        EPS = 1e-12

        def _spmm(vals, row, col, h, n_nodes):
            msgs = vals[:, None] * h[col]
            return jax.ops.segment_sum(msgs, row, num_segments=n_nodes, indices_are_sorted=True)

        def _l2_normalize(h):
            norm = jnp.sqrt(jnp.sum(h * h, axis=-1, keepdims=True))
            return h / jnp.maximum(norm, EPS)
        n_nodes = x.shape[0]
        h = x
        acc = x
        for _ in range(LAYERS):
            h = _spmm(vals, row, col, h, n_nodes)
            h = _l2_normalize(h)
            acc = acc + h
        return acc / (LAYERS + 1)

    def _L2_gnn_ref(x, edge_index, W, att_src, att_dst, bias):
        import jax, jax.numpy as jnp
        import numpy as np
        HEADS = 4
        OUT_CH = 64
        NEG_SLOPE = 0.2
        N = x.shape[0]
        loop = jnp.arange(N, dtype=edge_index.dtype)
        src = jnp.concatenate([edge_index[0], loop])
        dst = jnp.concatenate([edge_index[1], loop])
        h = (x @ W).reshape(N, HEADS, OUT_CH)
        a_src = jnp.einsum('nhc,hc->nh', h, att_src)
        a_dst = jnp.einsum('nhc,hc->nh', h, att_dst)
        e = a_src[src] + a_dst[dst]
        e = jnp.where(e >= 0, e, NEG_SLOPE * e)
        e_max = jax.ops.segment_max(e, dst, num_segments=N)
        e_exp = jnp.exp(e - e_max[dst])
        denom = jax.ops.segment_sum(e_exp, dst, num_segments=N)
        alpha = e_exp / denom[dst]
        msgs = h[src] * alpha[:, :, None]
        out = jax.ops.segment_sum(msgs, dst, num_segments=N)
        out = out.reshape(N, HEADS * OUT_CH) + bias
        out = jax.nn.relu(out)
        norm = jnp.sqrt(jnp.sum(out * out, axis=-1, keepdims=True))
        out = out / jnp.maximum(norm, 1e-12)
        return out

    def _L3_gnn_ref(x, W_u, b_u, W_v, src, dst):
        import jax, jax.numpy as jnp
        import numpy as np
        N_NODES = 50000
        N_EDGES = 25000
        DIM = 256
        NUM_HEADS = 8
        n_nodes, dim = x.shape
        num_heads = W_u.shape[0]
        head_dim = dim // num_heads
        s_u = x @ W_u.T + b_u
        s_v = x @ W_v.T
        e = s_u[src] + s_v[dst]
        e = jnp.where(e >= 0, e, 0.2 * e)
        m = jax.ops.segment_max(e, dst, num_segments=n_nodes)
        e_exp = jnp.exp(e - m[dst])
        denom = jax.ops.segment_sum(e_exp, dst, num_segments=n_nodes)
        probs = e_exp / denom[dst]
        xh = x.reshape(n_nodes, head_dim, num_heads)
        msg = xh[src] * probs[:, None, :]
        out = jax.ops.segment_sum(msg, dst, num_segments=n_nodes)
        return out.reshape(n_nodes, dim)
    edge_index = jnp.stack([src, dst])
    x = _layernorm(x + _L0_gnn_ref(x, edge_index, edge_weight, edge_attr_64, L0_gnn_fw1, L0_gnn_fb1, L0_gnn_fw2, L0_gnn_fb2, L0_gnn_w1, L0_gnn_w2, L0_gnn_b2, L0_gnn_w3, L0_gnn_b3), axis=-1)
    x = _layernorm(x + _L1_gnn_ref(x, edge_weight, src, dst), axis=-1)
    x = _layernorm(x + _L2_gnn_ref(x, edge_index, L2_gnn_W, L2_gnn_att_src, L2_gnn_att_dst, L2_gnn_bias), axis=-1)
    x = _layernorm(x + _L3_gnn_ref(x, L3_gnn_W_u, L3_gnn_b_u, L3_gnn_W_v, src, dst), axis=-1)
    return x

_drawn_inputs = setup_inputs


def setup_inputs(seed=0):
    import zlib

    import numpy as np

    out = dict(_drawn_inputs(seed))
    spreads = {'L0_gnn_fb1': (0.0, 0.8),
     'L0_gnn_fb2': (0.0, 0.8),
     'L0_gnn_b2': (0.0, 0.1),
     'L0_gnn_b3': (0.0, 0.1),
     'L2_gnn_bias': (0.0, 0.8)}
    factors = {'edge_weight': 3.022, 'L2_gnn_att_src': 6.063, 'L2_gnn_att_dst': 8.0, 'L3_gnn_b_u': 8.0}
    for name, (base, spread) in spreads.items():
        noise = np.random.default_rng([zlib.crc32(name.encode()), seed]).standard_normal(out[name].shape)
        drawn = base * np.exp(spread * noise) if base else spread * noise
        out[name] = jnp.asarray(drawn.astype(out[name].dtype))
    for name, factor in factors.items():
        out[name] = (out[name] * factor).astype(out[name].dtype)
    return out
```

```python
from contextlib import ExitStack, contextmanager
import math

import concourse.bass as bass
from concourse import mybir

F32 = mybir.dt.float32
BF16 = mybir.dt.bfloat16
I32 = mybir.dt.int32
ALU = mybir.AluOpType
ACT = mybir.ActivationFunctionType

P = 128
N, D = 50000, 256
E = 25000
BASIS = 64
K4 = 4
ROWS = K4 * P
GROUPS = 50
T = GROUPS * K4
EP = T * P
EDGE_PARTS = E // T
HALVES = ((0, 26), (26, 24))
NG = -(-N // ROWS)
PAD_KEY = 65535
FAR = 100000.0
LOW = -1.0e30
LN_EPS = 1e-5
NORM_EPS2 = 1e-24
NORM_SCALE = 2.0 ** 20
H2, H3 = 4, 8


def steps(eng, n, body, start=0):
    a, b = start // 2, (start + n) // 2 - 1
    body(2 * a, 0, a)
    body(2 * a + 1, 1, a)
    with eng.Fori(a + 1, b) as r:
        body(r * 2, 0, r)
        body(r * 2 + 1, 1, r)
    body(2 * b, 0, b)
    body(2 * b + 1, 1, b)


def early(step, n):
    return isinstance(step, int) and step < n


def node_base(g):
    return N - ROWS if isinstance(g, int) and g == NG - 1 else g * ROWS


def node_rows(dram, g):
    return dram[bass.ds(node_base(g), ROWS), :].rearrange("(p k) d -> p k d", k=K4)


def edge_rows(dram, g, width=D):
    return dram[bass.ds(g * ROWS, ROWS), :].rearrange("(k p) d -> p k d", p=P)


class Core:

    def __init__(self, nc, ctx):
        self.nc, self.ctx = nc, ctx

    def sb(self, name, shape, dt=F32, ctx=None):
        t = (ctx or self.ctx).enter_context(self.nc.sbuf_tensor(name, shape, dt))
        return t

    def ps(self, name, shape, dt=F32, ctx=None):
        return (ctx or self.ctx).enter_context(self.nc.psum_tensor(name, shape, dt))

    def sem(self, name):
        self.phase_sems.append(self.nc.alloc_semaphore(name))
        return self.phase_sems[-1]

    @contextmanager
    def phase(self):
        self.phase_sems = []
        with ExitStack() as ctx:
            yield ctx
        self.nc.clear_and_free_semaphores(self.phase_sems)
        self.nc.all_engine_barrier()


def setup_phase(c, a):
    nc = c.nc
    with c.phase() as ctx:
        nat = {n: c.sb("nat_" + n, [P, 2, D], ctx=ctx) for n in ("fw2", "w1", "w2", "w3")}
        nat["fw1"] = c.sb("nat_fw1", [P, 2, BASIS], ctx=ctx)
        heads = c.sb("heads", [16, D], ctx=ctx)
        att = c.sb("att", [P, 2, 2], ctx=ctx)
        blocks = c.sb("blocks", [P, 2, 2 * H2], ctx=ctx)
        wgT = c.sb("wgT", [P, 2, D], ctx=ctx)
        b2s = c.sb("b2s", [P, 4, 2], ctx=ctx)
        tp = [c.ps(f"tp{i}", [P, 512], ctx=ctx) for i in range(4)]
        loaded, masks, blocked = c.sem("w_loaded"), c.sem("w_masks"), c.sem("w_blocks")
        turned, copied = c.sem("w_turned"), c.sem("w_copied")
        soft, soft2, base = c.sem("w_soft"), c.sem("w_soft2"), c.sem("w_base")
        init, zeroed = c.sem("w_init"), c.sem("w_zeroed")
        block = ctx.enter_context(nc.Block())
        loads = [(nat[n][:, :, :], a[n].rearrange("(c p) i -> p c i", p=P)) for n in nat]
        loads += [(c.wg[:, :, 0:D], a["W"].rearrange("(c p) i -> p c i", p=P)),
                  (heads[0:8, :], a["W_u"]), (heads[8:16, :], a["W_v"]),
                  (c.fb1[:, :], a["fb1"].rearrange("(c p) -> p c", p=P)),
                  (c.b2[:, :], a["b2"].rearrange("(c p) -> p c", p=P)),
                  (att[:, :, 0], a["att_src"].rearrange("(c h) d -> (h d) c", h=2)),
                  (att[:, :, 1], a["att_dst"].rearrange("(c h) d -> (h d) c", h=2)),
                  (c.fb2[:, :], a["fb2"].rearrange("(o d) -> o d", o=1).to_broadcast([P, D])),
                  (c.b3[:, :], a["b3"].rearrange("(o d) -> o d", o=1).to_broadcast([P, D])),
                  (c.bias[:, :], a["bias"].rearrange("(o d) -> o d", o=1).to_broadcast([P, D])),
                  (c.bu[:, :], a["b_u"].rearrange("(o d) -> o d", o=1).to_broadcast([P, H3]))]
        turns = []
        for n, to in (("fw2", c.fw2T), ("w1", c.w1T), ("w2", c.w2T), ("w3", c.w3T)):
            for i in range(2):
                turns.append(([nat[n][:, o, i * P:(i + 1) * P] for o in range(2)], P, to[:, i, :], P))
        for i in range(2):
            turns.append(([c.wg[:, o, i * P:(i + 1) * P] for o in range(2)], P, wgT[:, i, :], P))
        turns.append(([nat["fw1"][:, o, :] for o in range(2)], P, c.fw1T[:, :], BASIS))
        for i in range(2):
            turns.append(([heads[:, i * P:(i + 1) * P]], 16, c.wuv[:, i, :], P))

        @block.sync
        def _(sp):
            for to, frm in loads:
                sp.dma_start(to, frm, allow_slow_non_contiguous=True).then_inc(loaded, 16)
            sp.wait_ge(zeroed, 3)
            sp.dma_start(c.h1_dram[EP:EP + 1, :], c.zero_row[0:1, :]).then_inc(init, 16)
            sp.dma_start(c.h2_dram[EP:EP + 1, :], c.zero_row[0:1, :]).then_inc(init, 16)
            sp.dma_start(c.place_dram.rearrange("(p j) o -> p (j o)", p=125), c.absent[0:125, :]).then_inc(init, 16)
            sp.wait_ge(init, 48)

        @block.gpsimd
        def _(pool):
            pool.memset(c.ident[:, :], 0.0).then_inc(masks, 1)
            pool.memset(c.ltri[:, :], 1.0).then_inc(masks, 1)
            pool.memset(c.window[:, :], 0.0).then_inc(masks, 1)
            pool.memset(c.ones[:, :], 1.0).then_inc(masks, 1)
            pool.memset(c.first[:, :], 0.0).then_inc(masks, 1)
            pool.memset(c.end[:, :], 0.0).then_inc(masks, 1)
            pool.memset(c.zero_row[:, :], 0.0).then_inc(zeroed, 1)
            pool.memset(c.absent[:, :], EP).then_inc(zeroed, 1)
            pool.iota(c.digits_i[:, :], pattern=[[1, 256]], base=0, channel_multiplier=0).then_inc(zeroed, 1)
            pool.wait_ge(masks, 6)
            pool.affine_select(out=c.ident[:, :], in_=c.ident[:, :], compare_op=ALU.not_equal, fill=1.0,
                               base=0, pattern=[[-1, P]], channel_multiplier=1).then_inc(masks, 1)
            pool.affine_select(out=c.ltri[:, :], in_=c.ltri[:, :], compare_op=ALU.is_gt, fill=0.0,
                               base=0, pattern=[[1, P]], channel_multiplier=-1).then_inc(masks, 1)
            pool.memset(c.window[:, P:P + 1], 1.0).then_inc(masks, 1)
            pool.memset(c.first[0:1, :], 1.0).then_inc(masks, 1)
            pool.affine_select(out=c.end[:, :], in_=c.end[:, :], compare_op=ALU.not_equal, fill=1.0,
                               base=-(P - 1), pattern=[[0, 1]], channel_multiplier=1).then_inc(masks, 1)
            pool.wait_ge(masks, 11)
            pool.tensor_copy(c.identb[:, :], c.ident[:, :]).then_inc(masks, 1)

        @block.vector
        def _(dve):
            dve.memset(blocks[:, :, :], 0.0).then_inc(blocked, 1)
            dve.memset(c.consts[:, 0:1], LN_EPS).then_inc(blocked, 1)
            dve.memset(c.consts[:, 1:2], math.log(1.25)).then_inc(blocked, 1)
            dve.memset(c.consts[:, 2:3], 0.5 * math.log(NORM_SCALE)).then_inc(blocked, 1)
            dve.memset(c.consts[:, 3:4], math.pi / 2).then_inc(blocked, 1)
            dve.memset(c.consts[:, 4:5], 0.5)
            dve.memset(c.consts[:, 5:6], 0.5 * math.log(NORM_SCALE) + math.log(0.25)).then_inc(blocked, 1)
            dve.wait_ge(zeroed, 3)
            dve.tensor_copy(c.digits[:, :], c.digits_i[:, :]).then_inc(blocked, 1)
            dve.wait_ge(loaded, 16 * len(loads))
            dve.wait_ge(blocked, 7)
            for which in range(2):
                for h in range(H2):
                    r = slice(64 * (h % 2), 64 * (h % 2) + 64)
                    dve.tensor_copy(blocks[r, h // 2, which * H2 + h:which * H2 + h + 1],
                                    att[r, h // 2, which:which + 1]).then_inc(blocked, 1)
            for n, (parts, wide, to, rows) in enumerate(turns):
                dve.wait_ge(turned, n + 1)
                dve.tensor_copy(to, tp[n % 4][0:rows, 0:wide * len(parts)]).then_inc(copied, 1)
            n = len(turns)
            for i in range(2):
                dve.wait_ge(turned, n + i + 1)
                dve.tensor_copy(c.wg[:, i, D:D + 2 * H2], tp[(n + i) % 4][:, 0:2 * H2]).then_inc(copied, 1)
            dve.tensor_scalar(b2s[:, 0, :], c.b2[:, :], 0.0, None, ALU.max).then_inc(soft2, 1)
            dve.wait_ge(soft2, 1)
            dve.wait_ge(soft, 3)
            dve.tensor_tensor(b2s[:, 0, :], b2s[:, 0, :], b2s[:, 3, :], ALU.add).then_inc(soft2, 1)
            dve.wait_ge(base, 1)
            dve.tensor_tensor(c.c0[:, :], tp[(n + 2) % 4][:, 0:D], c.b3[:, :], ALU.add).then_inc(base, 1)

        @block.scalar
        def _(act):
            act.wait_ge(loaded, 16 * len(loads))
            act.wait_ge(blocked, 6)
            act.activation(b2s[:, 1, :], c.b2[:, :], ACT.Abs).then_inc(soft, 1)
            act.wait_ge(soft, 1)
            act.activation(b2s[:, 2, :], b2s[:, 1, :], ACT.Exp, scale=-1.0).then_inc(soft, 1)
            act.wait_ge(soft, 2)
            act.activation(b2s[:, 3, :], b2s[:, 2, :], ACT.Ln, bias=c.consts[:, 4:5], scale=0.5).then_inc(soft, 1)

        @block.tensor
        def _(pe):
            pe.wait_ge(masks, 12)
            pe.wait_ge(loaded, 16 * len(loads))
            for n, (parts, wide, to, rows) in enumerate(turns):
                if n >= 4:
                    pe.wait_ge(copied, n - 3)
                for o, part in enumerate(parts):
                    last = pe.transpose(tp[n % 4][0:rows, o * wide:(o + 1) * wide], part, c.ident[0:wide, 0:wide])
                last.then_inc(turned, 1)
            n = len(turns)
            pe.wait_ge(copied, n)
            pe.wait_ge(blocked, 7 + 2 * H2)
            for i in range(2):
                for o in range(2):
                    last = pe.matmul(tp[(n + i) % 4][:, 0:2 * H2], wgT[:, o, i * P:(i + 1) * P], blocks[:, o, :],
                                     start=(o == 0), stop=(o == 1))
                last.then_inc(turned, 1)
            pe.wait_ge(soft2, 2)
            for o in range(2):
                last = pe.matmul(tp[(n + 2) % 4][:, 0:D], b2s[:, 0, o:o + 1].to_broadcast([P, P]), c.w3T[:, o, :],
                                 start=(o == 0), stop=(o == 1))
            last.then_inc(base, 1)


def payload_phase(c, a):
    nc = c.nc
    with c.phase() as ctx:
        dst = c.sb("pl_dst", [P, T], I32, ctx=ctx)
        src = c.sb("pl_src", [P, T], I32, ctx=ctx)
        w = c.sb("pl_w", [P, T], ctx=ctx)
        num = c.sb("pl_num", [P, T], I32, ctx=ctx)
        pad = c.sb("pl_pad", [P, 1], ctx=ctx)
        ready, loaded, made, numbered = c.sem("pl_ready"), c.sem("pl_loaded"), c.sem("pl_made"), c.sem("pl_numbered")
        block = ctx.enter_context(nc.Block())

        @block.sync
        def _(sp):
            sp.wait_ge(ready, 3)
            sp.dma_start(dst[0:EDGE_PARTS, :], a["dst"].rearrange("(p t) -> p t", t=T)).then_inc(loaded, 16)
            sp.dma_start(src[0:EDGE_PARTS, :], a["src"].rearrange("(p t) -> p t", t=T)).then_inc(loaded, 16)
            sp.dma_start(w[0:EDGE_PARTS, :], a["ew"].rearrange("(p t) -> p t", t=T)).then_inc(loaded, 16)

        @block.gpsimd
        def _(pool):
            pool.iota(num[:, :], pattern=[[1, T]], base=0, channel_multiplier=T).then_inc(numbered, 1)
            pool.memset(pad[:, :], float(PAD_KEY)).then_inc(numbered, 1)
            pool.wait_ge(numbered, 2)
            pool.affine_select(out=pad[:, :], in_=pad[:, :], compare_op=ALU.is_ge, fill=0.0,
                               base=-EDGE_PARTS, pattern=[[0, 1]], channel_multiplier=1).then_inc(numbered, 1)

        @block.vector
        def _(dve):
            dve.memset(dst[:, :], 0).then_inc(ready, 1)
            dve.memset(src[:, :], 0).then_inc(ready, 1)
            dve.memset(w[:, :], 0.0).then_inc(ready, 1)
            dve.wait_ge(numbered, 3)
            dve.tensor_scalar(num[:, :], num[:, :], float(E - 1), None, ALU.min).then_inc(made, 1)
            dve.wait_ge(loaded, 48)
            dve.wait_ge(made, 1)
            for table, key, other in ((c.pay_d, dst, src), (c.pay_s, src, dst)):
                dve.tensor_scalar(table[:, :, 0], key[:, :], pad[:, 0:1], None, ALU.max)
                dve.tensor_copy(table[:, :, 1], other[:, :])
                dve.tensor_copy(table[:, :, :].bitcast(F32)[:, :, 2], w[:, :])
                dve.tensor_copy(table[:, :, 3], num[:, :]).then_inc(made, 1)


def sort_pass(c, name, pay, shift, out_dram):
    nc = c.nc
    with c.phase() as ctx:
        digit_i = c.sb(name + "digit_i", [P, T], I32, ctx=ctx)
        digit = c.sb(name + "digit", [P, T], ctx=ctx)
        hot = c.sb(name + "hot", [P, 2 * K4, 256], BF16, ctx=ctx)
        junk = c.sb(name + "junk", [P, 2 * K4, 256], BF16, ctx=ctx)
        counts = c.sb(name + "counts", [P, 2, 256], BF16, ctx=ctx)
        zeros = c.sb(name + "zeros", [P, 256], ctx=ctx)
        total = c.sb(name + "total", [P, 256], ctx=ctx)
        base = c.sb(name + "base", [P, 256], ctx=ctx)
        ahead = c.sb(name + "ahead", [P, 2, 256], ctx=ctx)
        ahead_hi = c.sb(name + "ahead_hi", [P, 2, 256], BF16, ctx=ctx)
        ahead_lo = c.sb(name + "ahead_lo", [P, 2, 256], BF16, ctx=ctx)
        place = c.sb(name + "place", [P, T], ctx=ctx)
        place_i = c.sb(name + "place_i", [P, T], I32, ctx=ctx)
        at = c.sb(name + "at", [P, 2, K4], I32, ctx=ctx)
        rows = c.sb(name + "rows", [P, 2, K4, 4], I32, ctx=ctx)
        tab = c.ps(name + "tab", [P, 2, 512], ctx=ctx)
        rank = c.ps(name + "rank", [P, 2 * K4, 256], ctx=ctx)
        digits_ready, hot_made, hot_counted = c.sem(name + "digits"), c.sem(name + "hot_made"), c.sem(name + "hot_counted")
        tables = c.sem(name + "tables")
        sums, heads, ranked, read = c.sem(name + "sums"), c.sem(name + "heads"), c.sem(name + "ranked"), c.sem(name + "read")
        placed, copied, back = c.sem(name + "placed"), c.sem(name + "copied"), c.sem(name + "back")
        issuing = c.sem(name + "issuing")
        hot2, sent = c.sem(name + "hot2"), [c.sem(f"{name}sent{u}") for u in range(2)]
        block = ctx.enter_context(nc.Block())

        def make_hot(dve, g, u, made):
            for k in range(K4):
                last = dve.tensor_scalar(hot[:, u * K4 + k, :], c.digits[:, :], digit[:, bass.ds(g * K4 + k, 1)], None,
                                         ALU.is_equal)
            last.then_inc(made, 1)

        @block.vector
        def _(dve):
            dve.memset(zeros[:, :], 0.0).then_inc(digits_ready, 1)
            dve.tensor_scalar(digit_i[:, :], pay[:, :, 0], shift, 255, ALU.logical_shift_right, ALU.bitwise_and)\
               .then_inc(digits_ready, 1)
            dve.wait_ge(digits_ready, 2)
            dve.tensor_copy(digit[:, :], digit_i[:, :]).then_inc(digits_ready, 1)
            dve.wait_ge(digits_ready, 3)

            def count(g, u, i):
                if not early(g, 2):
                    dve.wait_ge(hot_counted, g - 1)
                make_hot(dve, g, u, hot_made)
            for start, n in HALVES:
                steps(dve, n, count, start)
            dve.wait_ge(tables, 1)
            dve.tensor_copy(counts[:, :, :], tab[:, :, 0:256]).then_inc(tables, 1)
            dve.wait_ge(sums, 1)
            dve.tensor_copy(total[:, :], rank[:, 0, :]).then_inc(heads, 1)
            dve.wait_ge(heads, 1)
            dve.tensor_tensor_scan(base[:, :], total[:, :], zeros[:, :], 0.0, ALU.add, ALU.add).then_inc(heads, 1)
            dve.wait_ge(heads, 2)
            dve.tensor_tensor(base[:, :], base[:, :], total[:, :], ALU.subtract).then_inc(heads, 1)
            dve.wait_ge(heads, 3)
            dve.wait_ge(sums, 2)
            for h in range(2):
                dve.tensor_tensor(ahead[:, h, :], rank[:, 2 + 2 * h, :], base[:, :], ALU.add).then_inc(heads, 1)
            dve.wait_ge(heads, 5)
            dve.tensor_copy(ahead_hi[:, :, :], ahead[:, :, :]).then_inc(heads, 1)
            dve.wait_ge(heads, 6)
            dve.tensor_tensor(ahead_lo[:, :, :], ahead[:, :, :], ahead_hi[:, :, :], ALU.subtract).then_inc(heads, 1)

            def positions(g, u):
                dve.wait_ge(ranked, g + 1)
                for k in range(K4):
                    last = dve.scalar_tensor_tensor(
                        out=junk[:, u * K4 + k, :], in0=hot[:, u * K4 + k, :], scalar=1.0, in1=rank[:, u * K4 + k, :],
                        op0=ALU.mult, op1=ALU.mult, accum_out=place[:, bass.ds(g * K4 + k, 1)])
                last.then_inc(read, 1)

            def place_step(g, u, i):
                if not early(g, 2):
                    dve.wait_ge(read, g - 1)
                make_hot(dve, g, u, hot2)
                if not early(g, 1):
                    positions(g - 1, 1 - u)
            dve.wait_ge(hot_counted, GROUPS)
            for start, n in HALVES:
                steps(dve, n, place_step, start)
            positions(GROUPS - 1, 1)
            dve.wait_ge(read, GROUPS)
            dve.tensor_copy(place_i[:, :], place[:, :]).then_inc(placed, 1)

        @block.tensor
        def _(pe):
            for h, (start, n) in enumerate(HALVES):
                pe.matmul(tab[:, h, 0:256], c.window[:, 0:P], c.window[:, 0:256], start=True, stop=False)

                def count(g, u, i):
                    pe.wait_ge(hot_made, g + 1)
                    for k in range(K4):
                        last = pe.matmul(tab[:, h, 0:256], c.window[:, bass.ds((g - start) * (-K4) + P - k, P)],
                                         hot[:, u * K4 + k, :], start=False, stop=False)
                    last.then_inc(hot_counted, 1)
                steps(pe, n, count, start)
                last = pe.matmul(tab[:, h, 0:256], c.window[:, 0:P], c.window[:, 0:256], start=False, stop=True)
            last.then_inc(tables, 1)
            pe.wait_ge(tables, 2)
            for h in range(2):
                last = pe.matmul(rank[:, 0, :], c.ones[:, :], counts[:, h, :], start=(h == 0), stop=(h == 1))
            last.then_inc(sums, 1)
            pe.matmul(rank[:, 2, :], c.ltri[:, :], counts[:, 0, :], start=True, stop=True)
            pe.matmul(rank[:, 4, :], c.ltri[:, :], counts[:, 1, :], start=True, stop=False)
            pe.matmul(rank[:, 4, :], c.ones[:, :], counts[:, 0, :], start=False, stop=True).then_inc(sums, 1)
            pe.wait_ge(heads, 7)
            for h, (start, n) in enumerate(HALVES):
                def rank_step(g, u, i):
                    pe.wait_ge(hot2, g + 1)
                    if not early(g, 2):
                        pe.wait_ge(read, g - 1)
                    for k in range(K4):
                        out = rank[:, u * K4 + k, :]
                        pick = c.identb[:, bass.ds((g - start) * K4 + k, 1)].to_broadcast([P, P])
                        pe.matmul(out, c.ltri[:, :], hot[:, u * K4 + k, :], start=True, stop=False)
                        pe.matmul(out, pick, ahead_hi[:, h, :], start=False, stop=False)
                        last = pe.matmul(out, pick, ahead_lo[:, h, :], start=False, stop=True)
                    last.then_inc(ranked, 1)
                steps(pe, n, rank_step, start)

        @block.gpsimd
        def _(pool):
            pool.wait_ge(placed, 1)

            def send(g, u, i):
                if not early(g, 2):
                    pool.wait_ge(sent[u], i * 16 * K4)
                pool.tensor_copy(at[:, u, :], place_i[:, bass.ds(g * K4, K4)]).then_inc(copied, 1)
                pool.tensor_copy(rows[:, u, :, :], pay[:, bass.ds(g * K4, K4), :]).then_inc(copied, 1)
                pool.wait_ge(copied, g * 2 + 2)
                pool.sem_inc(issuing, 1)
                for k in range(K4):
                    pool.indirect_dma_start(out_dram[:, :], bass.IndirectOffsetOnAxis(ap=at[:, u, k:k + 1], axis=0),
                                            rows[:, u, k, :], None).then_inc(sent[u], 16)
            steps(pool, GROUPS, send)

        @block.sync
        def _(sp):
            for u in range(2):
                sp.wait_ge(sent[u], GROUPS // 2 * 16 * K4)
            sp.dma_start(pay[:, :, :], out_dram.rearrange("(t p) c -> p t c", p=P)).then_inc(back, 16)
            sp.wait_ge(back, 16)


def index_phase(c, name, side):
    nc = c.nc
    pay, key, last_at, keys_dram = side["pay"], side["key"], side["last_at"], side["keys"]
    with c.phase() as ctx:
        keyT = c.sb(name + "keyT", [P, 2, P], ctx=ctx)
        nextT = c.sb(name + "nextT", [P, 2, P], ctx=ctx)
        sentinels = c.sb(name + "sentinels", [1, 2], ctx=ctx)
        turn = c.ps(name + "turn", [P, 2, 512], ctx=ctx)
        turn2 = c.ps(name + "turn2", [P, 2, 512], ctx=ctx)
        keyed, turned, keyedT, stored = c.sem(name + "keyed"), c.sem(name + "turned"), c.sem(name + "keyedT"), c.sem(name + "stored")
        cuts = c.sb(name + "cuts", [P, 2, P], ctx=ctx)
        loaded, marked, back = c.sem(name + "loaded"), c.sem(name + "marked"), c.sem(name + "ix_back")
        block = ctx.enter_context(nc.Block())
        half = T // 2

        @block.vector
        def _(dve):
            dve.memset(sentinels[0:1, 0:1], -1.0).then_inc(keyed, 1)
            dve.memset(sentinels[0:1, 1:2], -2.0).then_inc(keyed, 1)
            dve.memset(key[:, 0:1], -1.0).then_inc(keyed, 1)
            dve.tensor_copy(key[:, 1:T + 1], pay[:, :, 0]).then_inc(keyed, 1)
            for to, col, top in side["columns"]:
                dve.tensor_scalar(to[:, :], pay[:, :, col], float(top), None, ALU.min)
            dve.tensor_copy(side["w"][:, :], pay[:, :, :].bitcast(F32)[:, :, 2])
            dve.tensor_scalar(side["w8"][:, :], pay[:, :, :].bitcast(F32)[:, :, 2], 0.8, None, ALU.mult)
            dve.wait_ge(turned, 1)
            dve.tensor_copy(keyT[0:half, :, :], turn[0:half, :, 0:P]).then_inc(keyedT, 1)
            dve.wait_ge(loaded, 16)
            dve.tensor_tensor(nextT[0:half, :, :], nextT[0:half, :, :], keyT[0:half, :, :], ALU.is_equal).then_inc(marked, 1)
            dve.wait_ge(marked, 1)
            dve.tensor_scalar(cuts[0:half, :, :], nextT[0:half, :, :], -LOW, LOW, ALU.mult, ALU.add).then_inc(marked, 1)
            dve.wait_ge(marked, 2)
            dve.scalar_tensor_tensor(out=nextT[0:half, :, :], in0=nextT[0:half, :, :], scalar=FAR, in1=keyT[0:half, :, :],
                                     op0=ALU.mult, op1=ALU.add).then_inc(marked, 1)
            dve.wait_ge(back, 1)
            dve.tensor_copy(last_at[:, :].rearrange("p (h t) -> p h t", h=2), turn2[:, :, 0:half])

        @block.tensor
        def _(pe):
            pe.wait_ge(keyed, 4)
            for h in range(2):
                last = pe.transpose(turn[0:half, h, 0:P], key[:, 1 + h * half:1 + (h + 1) * half], c.ident[:, :])
            last.then_inc(turned, 1)
            pe.wait_ge(marked, 3)
            for h in range(2):
                last = pe.transpose(turn2[:, h, 0:half], nextT[0:half, h, :], c.ident[0:half, 0:half])
            last.then_inc(back, 1)

        @block.sync
        def _(sp):
            sp.wait_ge(keyedT, 1)
            sp.dma_start(keys_dram[1:EP + 1].rearrange("(h t p) -> t h p", h=2, p=P), keyT[0:half, :, :]).then_inc(stored, 16)
            sp.dma_start(keys_dram[0:1].rearrange("(o n) -> o n", o=1), sentinels[0:1, 0:1]).then_inc(stored, 16)
            sp.dma_start(keys_dram[EP + 1:EP + 2].rearrange("(o n) -> o n", o=1), sentinels[0:1, 1:2]).then_inc(stored, 16)
            sp.wait_ge(stored, 48)
            sp.dma_start(nextT[0:half, :, :], keys_dram[2:EP + 2].rearrange("(h t p) -> t h p", h=2, p=P)).then_inc(loaded, 16)
            sp.wait_ge(marked, 2)
            sp.dma_start(side["cuts"][1:EP + 1].rearrange("(h t p) -> t h p", h=2, p=P), cuts[0:half, :, :]).then_inc(stored, 16)
            sp.dma_start(side["cuts"][0:1].rearrange("(o n) -> o n", o=1), sentinels[0:1, 0:1]).then_inc(stored, 16)
            sp.wait_ge(stored, 80)


def signals(c, prefix):
    made = {}

    def get(name):
        if name not in made:
            made[name] = c.sem(prefix + name)
        return made[name]
    return get


def row_stats(dve, x, stats, mv, n, s, what, g):
    for k in range(n):
        last = dve.bn_stats(stats[:, k, :], x[:, k, :])
    last.then_inc(s(what + "_stats"), 1)
    dve.wait_ge(s(what + "_stats"), g + 1)
    dve.sem_inc(s(what + "_held"), 1)
    for k in range(n):
        last = dve.bn_aggr(mv[:, k, :], stats[:, k, :])
    last.then_inc(s(what + "_var"), 1)


def row_scale(act, c, mv, rs, s, what, g, bias=0.0):
    act.wait_ge(s(what + "_var"), g + 1)
    act.activation(rs[:, :], mv[:, :, 1], ACT.Ln, bias=c.consts[:, 0:1]).then_inc(s(what + "_log"), 1)
    act.wait_ge(s(what + "_log"), g + 1)
    act.activation(rs[:, :], rs[:, :], ACT.Exp, bias=bias, scale=-0.5).then_inc(s(what + "_scale"), 1)


def row_apply(dve, out, x, mv, rs, n, s, what, g, done):
    dve.wait_ge(s(what + "_scale"), g + 1)
    for k in range(n):
        last = dve.tensor_scalar(out[:, k, :], x[:, k, :], mv[:, k, 0:1], rs[:, k:k + 1], ALU.subtract, ALU.mult)
    last.then_inc(s(done), 1)


def node_pass_one(c, a):
    nc = c.nc
    with c.phase() as ctx:
        x = c.sb("n1_x", [P, 2, K4, D], ctx=ctx)
        y = c.sb("n1_y", [P, 2, K4, D], ctx=ctx)
        stats, mv, rs = (c.sb("n1_" + n, [P, 2, K4] + m, ctx=ctx) for n, m in (("stats", [6]), ("mv", [2]), ("rs", [])))
        s = signals(c, "n1_")
        loaded, stored = [s("loaded0"), s("loaded1")], [s("stored0"), s("stored1")]
        block = ctx.enter_context(nc.Block())

        @block.sync
        def _(sp):
            def store(g, u, i):
                sp.wait_ge(s("y_done"), g + 1)
                if isinstance(g, int) and g == NG - 1:
                    sp.wait_ge(stored[1 - u], 16 * (i + 1))
                sp.dma_start(node_rows(c.a_dram, g), y[:, u, :, :]).then_inc(stored[u], 16)

            def step(g, u, i):
                if not early(g, 2):
                    sp.wait_ge(s("y_done"), g - 1)
                sp.dma_start(x[:, u, :, :], node_rows(a["x"], g)).then_inc(loaded[u], 16)
                if not early(g, 1):
                    store(g - 1, 1 - u, i - 1 if u == 0 else i)
            steps(sp, NG, step)
            store(NG - 1, 1, NG // 2 - 1)
            for u in range(2):
                sp.wait_ge(stored[u], 16 * (NG // 2))

        @block.vector
        def _(dve):
            def back(g, u, i):
                if not early(g, 2):
                    dve.wait_ge(stored[u], 16 * i)
                row_apply(dve, y[:, u], x[:, u], mv[:, u], rs[:, u], K4, s, "x", g, "y_done")

            def step(g, u, i):
                dve.wait_ge(loaded[u], 16 * (i + 1))
                dve.tensor_tensor(x[:, u, :, :], x[:, u, :, :], c.c0[:, :].rearrange("p (o d) -> p o d", o=1)
                                  .to_broadcast([P, K4, D]), ALU.add).then_inc(s("shifted"), 1)
                dve.wait_ge(s("shifted"), g + 1)
                row_stats(dve, x[:, u], stats[:, u], mv[:, u], K4, s, "x", g)
                if not early(g, 1):
                    back(g - 1, 1 - u, i - 1 if u == 0 else i)
            steps(dve, NG, step)
            back(NG - 1, 1, NG // 2 - 1)

        @block.scalar
        def _(act):
            steps(act, NG, lambda g, u, i: row_scale(act, c, mv[:, u], rs[:, u], s, "x", g, c.consts[:, 1:2]))


def cosine_phase(c):
    nc = c.nc
    with c.phase() as ctx:
        half = c.sb("co_half", [P, T], ctx=ctx)
        s = signals(c, "co_")
        block = ctx.enter_context(nc.Block())
        rounder = 1.5 * 2.0 ** 23
        w = c.d["w"]

        @block.vector
        def _(dve):
            dve.tensor_scalar(half[:, :], w[:, :], 0.5, rounder, ALU.mult, ALU.add).then_inc(s("step"), 1)
            dve.wait_ge(s("step"), 1)
            dve.tensor_scalar(half[:, :], half[:, :], rounder, -2.0, ALU.subtract, ALU.mult).then_inc(s("step"), 1)
            dve.wait_ge(s("step"), 2)
            dve.tensor_tensor(half[:, :], half[:, :], w[:, :], ALU.add).then_inc(s("reduced"), 1)
            dve.wait_ge(s("sine"), 1)
            dve.tensor_scalar(c.cutoff[:, :], half[:, :], 1.0, 0.25, ALU.add, ALU.mult)

        @block.scalar
        def _(act):
            act.wait_ge(s("reduced"), 1)
            act.activation(half[:, :], half[:, :], ACT.Abs).then_inc(s("abs"), 1)
            act.wait_ge(s("abs"), 1)
            act.activation(half[:, :], half[:, :], ACT.Sin, bias=c.consts[:, 3:4], scale=-math.pi).then_inc(s("sine"), 1)


def filter_layer(c, a):
    nc = c.nc
    side = c.d
    with c.phase() as ctx:
        sb = lambda n, shape, dt=F32: c.sb("l0_" + n, shape, dt, ctx=ctx)
        xs, xd = sb("xs", [P, 2, K4, D]), sb("xd", [P, 2, K4, D])
        ea, keys = sb("ea", [P, 2, K4, BASIS]), sb("keys", [P, 2, ROWS + 1])
        at = sb("at", [P, 2, 4, K4], I32)
        eaT, xsT = sb("eaT", [BASIS, ROWS]), sb("xsT", [P, 2, ROWS])
        pre, soft, log = sb("pre", [P, 2, ROWS]), sb("soft", [P, 2, ROWS]), sb("log", [P, 2, ROWS])
        filt, msg = sb("filt", [P, K4, D]), sb("msg", [P, K4, D])
        same, cont = sb("same", [P, K4, P]), sb("cont", [P, K4, P])
        agg, y = sb("agg", [P, 2, ROWS]), sb("y", [P, 2, K4, D])
        stats, mv, rs = sb("stats", [P, K4, 6]), sb("mv", [P, K4, 2]), sb("rs", [P, K4])
        pe_ea = c.ps("l0_pe", [P, 512], ctx=ctx)
        pe_x = c.ps("l0_px", [P, 2, 512], ctx=ctx)
        pe_z = c.ps("l0_pz", [P, 2, 512], ctx=ctx)
        pe_a = c.ps("l0_pa", [P, 2, 512], ctx=ctx)
        tiles_of = lambda t: t[:, :, :].rearrange("p b (j d) -> p (b j) d", d=D)
        s = signals(c, "l0_")
        got_s, got_e, got_d, keyed, sent = ([s(f"{n}{u}") for u in range(2)] for n in ("got_s", "got_e", "got_d", "keyed", "sent"))
        block = ctx.enter_context(nc.Block())

        @block.gpsimd
        def _(pool):
            def scatter(g, u):
                pool.wait_ge(s("y_done"), g + 1)
                pool.sem_inc(s("issuing"), 1)
                for k in range(K4):
                    pool.indirect_dma_start(c.a_dram[:, :], bass.IndirectOffsetOnAxis(ap=at[:, u, 3, k:k + 1], axis=0),
                                            y[:, u, k, :], None, bounds_check=N - 1, oob_is_err=False).then_inc(sent[u], 16)

            def step(g, u, i):
                if not early(g, 2):
                    pool.wait_ge(sent[u], i * 16 * K4)
                    pool.wait_ge(s("xsT"), g - 1)
                    pool.wait_ge(s("eaT"), g - 1)
                    pool.wait_ge(s("summed"), g - 1)
                for n, col in enumerate((side["other"], c.edge_of, side["own"], side["last_at"])):
                    pool.tensor_copy(at[:, u, n, :], col[:, bass.ds(g * K4, K4)]).then_inc(s("at"), 1)
                pool.wait_ge(s("at"), g * 4 + 4)
                pool.sem_inc(s("issuing"), 1)
                for n, (to, frm, got) in enumerate(((xs, a["x"], got_s), (ea, a["ea"], got_e), (xd, a["x"], got_d))):
                    for k in range(K4):
                        pool.indirect_dma_start(to[:, u, k, :], None, frm[:, :],
                                                bass.IndirectOffsetOnAxis(ap=at[:, u, n, k:k + 1], axis=0)).then_inc(got[u], 16)
                if not early(g, 1):
                    scatter(g - 1, 1 - u)
            steps(pool, GROUPS, step)
            scatter(GROUPS - 1, 1)
            for u in range(2):
                pool.wait_ge(sent[u], GROUPS // 2 * 16 * K4)

        @block.sync
        def _(sp):
            def step(g, u, i):
                if not early(g, 2):
                    sp.wait_ge(s("masked"), g - 1)
                sp.dma_start(keys[:, u, :], side["keys"][bass.ds(g * ROWS, ROWS + 1)].rearrange("(o n) -> o n", o=1)
                             .to_broadcast([P, ROWS + 1])).then_inc(keyed[u], 16)
            steps(sp, GROUPS, step)

        @block.tensor
        def _(pe):
            def step(g, u, i):
                pe.wait_ge(got_e[u], (i + 1) * 16 * K4)
                pe.sem_inc(s("held"), 1)
                for k in range(K4):
                    last = pe.transpose(pe_ea[0:BASIS, k * P:(k + 1) * P], ea[:, u, k, :], c.ident[:, :])
                last.then_inc(s("eaT"), 1)
                pe.wait_ge(got_s[u], (i + 1) * 16 * K4)
                pe.wait_ge(s("msg"), g)
                for f in range(2):
                    for k in range(K4):
                        last = pe.transpose(pe_x[:, f, k * P:(k + 1) * P], xs[:, u, k, f * P:(f + 1) * P], c.ident[:, :])
                last.then_inc(s("xsT"), 1)
                pe.wait_ge(s("eaT_sb"), g + 1)
                for f in range(2):
                    last = pe.matmul(pe_z[:, f, :], c.fw1T[:, f * P:(f + 1) * P], eaT[:, :], start=True, stop=True)
                last.then_inc(s("hidden"), 1)
                pe.wait_ge(s("soft"), 2 * g + 1)
                for k in range(K4):
                    for f in range(2):
                        last = pe.matmul(tiles_of(pe_z)[:, k, :], soft[:, f, k * P:(k + 1) * P], c.fw2T[:, f, :],
                                         start=(f == 0), stop=(f == 1))
                last.then_inc(s("filter"), 1)
                pe.wait_ge(s("xsT_sb"), g + 1)
                for k in range(K4):
                    for f in range(2):
                        last = pe.matmul(tiles_of(pe_x)[:, k, :], xsT[:, f, k * P:(k + 1) * P], c.w1T[:, f, :],
                                         start=(f == 0), stop=(f == 1))
                last.then_inc(s("h"), 1)
                pe.wait_ge(s("msg"), g + 1)
                pe.wait_ge(s("masked"), g + 1)
                for f in range(2):
                    for k in range(K4):
                        last = pe.matmul(pe_a[:, f, k * P:(k + 1) * P], msg[:, k, f * P:(f + 1) * P], same[:, k, :],
                                         start=True, stop=True)
                last.then_inc(s("runs"), 1)
                pe.wait_ge(s("agg"), (g + 1) * K4)
                for o in range(2):
                    for f in range(2):
                        last = pe.matmul(pe_z[:, o, :], c.w2T[:, f, o * P:(o + 1) * P], agg[:, f, :],
                                         start=(f == 0), stop=(f == 1))
                last.then_inc(s("o1"), 1)
                pe.wait_ge(s("soft"), 2 * g + 2)
                for k in range(K4):
                    for o in range(2):
                        last = pe.matmul(tiles_of(pe_a)[:, k, :], soft[:, o, k * P:(k + 1) * P], c.w3T[:, o, :],
                                         start=(o == 0), stop=(o == 1))
                last.then_inc(s("o2"), 1)
            steps(pe, GROUPS, step)

        @block.scalar
        def _(act):
            def softplus(g, n, ready, bias):
                act.wait_ge(s(ready), g + 1)
                for f in range(2):
                    last = act.activation(pre[:, f, :], pe_z[:, f, :], ACT.Identity, bias=bias[:, f:f + 1])
                last.then_inc(s("pre"), 1)
                act.wait_ge(s("pre"), 2 * g + n + 1)
                act.activation(log[:, :, :], pre[:, :, :], ACT.Abs).then_inc(s("soft_abs"), 1)
                act.wait_ge(s("soft_abs"), 2 * g + n + 1)
                act.activation(log[:, :, :], log[:, :, :], ACT.Exp, scale=-1.0).then_inc(s("soft_exp"), 1)
                act.wait_ge(s("soft_exp"), 2 * g + n + 1)
                act.activation(log[:, :, :], log[:, :, :], ACT.Ln, bias=c.consts[:, 4:5], scale=0.5).then_inc(s("soft_log"), 1)

            def step(g, u, i):
                act.wait_ge(s("eaT"), g + 1)
                act.activation(eaT[:, :], pe_ea[0:BASIS, :], ACT.Copy).then_inc(s("eaT_sb"), 1)
                act.wait_ge(s("xsT"), g + 1)
                act.activation(xsT[:, :, :], pe_x[:, :, :], ACT.Copy).then_inc(s("xsT_sb"), 1)
                softplus(g, 0, "hidden", c.fb1)
                softplus(g, 1, "o1", c.b2)
                row_scale(act, c, mv, rs, s, "x", g, c.consts[:, 1:2])
            steps(act, GROUPS, step)

        @block.vector
        def _(dve):
            dve.memset(agg[:, :, :], 0.0).then_inc(s("agg_clear"), 1)

            def softplus(g, n):
                dve.wait_ge(s("soft_log"), 2 * g + n + 1)
                dve.scalar_tensor_tensor(out=soft[:, :, :], in0=pre[:, :, :], scalar=0.0, in1=log[:, :, :],
                                         op0=ALU.max, op1=ALU.add).then_inc(s("soft"), 1)

            def step(g, u, i):
                dve.wait_ge(keyed[u], 16 * (i + 1))
                dve.wait_ge(s("runs"), g)
                for k in range(K4):
                    row = keys[:, u, 1 + k * P:1 + (k + 1) * P]
                    dve.tensor_scalar(same[:, k, :], row, side["key"][:, bass.ds(g * K4 + k + 1, 1)], None, ALU.is_equal)
                    last = dve.tensor_scalar(cont[:, k, :], row, keys[:, u, k * P:k * P + 1], None, ALU.is_equal)
                last.then_inc(s("masked"), 1)
                dve.wait_ge(got_d[u], (i + 1) * 16 * K4)
                dve.tensor_tensor(xd[:, u, :, :], xd[:, u, :, :], c.b3[:, :].rearrange("p (o d) -> p o d", o=1)
                                  .to_broadcast([P, K4, D]), ALU.add).then_inc(s("xd"), 1)
                softplus(g, 0)
                dve.wait_ge(s("filter"), g + 1)
                dve.tensor_tensor(filt[:, :, :], tiles_of(pe_z), c.fb2[:, :].rearrange("p (o d) -> p o d", o=1)
                                  .to_broadcast([P, K4, D]), ALU.add).then_inc(s("filt"), 1)
                dve.wait_ge(s("filt"), g + 1)
                dve.wait_ge(s("h"), g + 1)
                for k in range(K4):
                    last = dve.scalar_tensor_tensor(out=msg[:, k, :], in0=filt[:, k, :], scalar=c.cutoff[:, bass.ds(g * K4 + k, 1)],
                                                    in1=tiles_of(pe_x)[:, k, :], op0=ALU.mult, op1=ALU.mult)
                last.then_inc(s("msg"), 1)
                dve.wait_ge(s("runs"), g + 1)
                for k in range(K4):
                    if early(g, 1) and k == 0:
                        dve.wait_ge(s("agg_clear"), 1)
                    else:
                        dve.wait_ge(s("agg"), g * K4 + k)
                    before = (k * P - 1) % ROWS
                    for f in range(2):
                        last = dve.scalar_tensor_tensor(
                            out=agg[:, f, k * P:(k + 1) * P], in0=cont[:, k, :], scalar=agg[:, f, before:before + 1],
                            in1=pe_a[:, f, k * P:(k + 1) * P], op0=ALU.mult, op1=ALU.add)
                    last.then_inc(s("agg"), 1)
                softplus(g, 1)
                dve.wait_ge(s("o2"), g + 1)
                if not early(g, 2):
                    dve.wait_ge(sent[u], i * 16 * K4)
                dve.tensor_tensor(y[:, u, :, :], tiles_of(pe_a), xd[:, u, :, :], ALU.add).then_inc(s("summed"), 1)
                dve.wait_ge(s("summed"), g + 1)
                row_stats(dve, y[:, u], stats, mv, K4, s, "x", g)
                row_apply(dve, y[:, u], y[:, u], mv, rs, K4, s, "x", g, "y_done")
            steps(dve, GROUPS, step)


def place_phase(c):
    nc = c.nc
    side = c.s
    with c.phase() as ctx:
        pos = c.sb("pp_pos", [P, T], I32, ctx=ctx)
        at, row = c.sb("pp_at", [P, 2, K4], I32, ctx=ctx), c.sb("pp_row", [P, 2, K4], I32, ctx=ctx)
        s = signals(c, "pp_")
        moved = [s("moved0"), s("moved1")]
        block = ctx.enter_context(nc.Block())

        @block.gpsimd
        def _(pool):
            pool.iota(pos[:, :], pattern=[[P, T]], base=0, channel_multiplier=1).then_inc(s("pos"), 1)
            pool.wait_ge(s("pos"), 1)

            def send(g, u, i):
                if not early(g, 2):
                    pool.wait_ge(moved[u], i * 16 * K4)
                pool.tensor_copy(at[:, u, :], side["last_at"][:, bass.ds(g * K4, K4)]).then_inc(s("at"), 1)
                pool.tensor_copy(row[:, u, :], pos[:, bass.ds(g * K4, K4)]).then_inc(s("at"), 1)
                pool.wait_ge(s("at"), g * 2 + 2)
                pool.sem_inc(s("issuing"), 1)
                for k in range(K4):
                    pool.indirect_dma_start(c.place_dram[:, :], bass.IndirectOffsetOnAxis(ap=at[:, u, k:k + 1], axis=0),
                                            row[:, u, k:k + 1], None, bounds_check=N - 1, oob_is_err=False).then_inc(moved[u], 16)
            steps(pool, GROUPS, send)
            half = GROUPS // 2 * 16 * K4
            for u in range(2):
                pool.wait_ge(moved[u], half)

            def keep(g, u, i):
                pool.wait_ge(moved[u], half + (i + 1) * 16 * K4)
                pool.sem_inc(s("issuing"), 1)
                pool.tensor_copy(c.s_place[:, bass.ds(g * K4, K4)], row[:, u, :]).then_inc(s("kept"), 1)

            def look(g, u, i):
                if not early(g, 2):
                    pool.wait_ge(s("kept"), g - 1)
                    pool.sem_inc(s("issuing"), 1)
                pool.tensor_copy(at[:, u, :], side["other"][:, bass.ds(g * K4, K4)]).then_inc(s("at"), 1)
                pool.wait_ge(s("at"), g + (2 * GROUPS + 1))
                pool.sem_inc(s("issuing"), 1)
                for k in range(K4):
                    pool.indirect_dma_start(row[:, u, k:k + 1], None, c.place_dram[:, :],
                                            bass.IndirectOffsetOnAxis(ap=at[:, u, k:k + 1], axis=0)).then_inc(moved[u], 16)
                if not early(g, 1):
                    keep(g - 1, 1 - u, i - 1 if u == 0 else i)
            steps(pool, GROUPS, look)
            keep(GROUPS - 1, 1, GROUPS // 2 - 1)


def propagation_round(c, n):
    nc = c.nc
    side = c.s
    table = (c.a_dram, c.h1_dram, c.h2_dram)[n - 1]
    place = side["other"] if n == 1 else c.s_place
    weight = side["w8"] if n == 1 else side["w"]
    with c.phase() as ctx:
        pre = f"l1{n}_"
        sb = lambda m, shape, dt=F32: c.sb(pre + m, shape, dt, ctx=ctx)
        x, keys, at = sb("x", [P, 2, K4, D]), sb("keys", [P, 2, ROWS]), sb("at", [P, 2, 2, K4], I32)
        same, cont = sb("same", [P, 2, K4, P]), sb("cont", [P, 2, K4, P])
        total, h, square = sb("total", [P, K4, D]), sb("h", [P, 2, K4, D]), sb("square", [P, K4, D])
        ss, rn = sb("ss", [P, K4]), sb("rn", [P, K4])
        old = sb("old", [P, 2, 2, K4, D]) if n == 3 else None
        acc = c.ps(pre + "acc", [P, 2 * K4, 512], ctx=ctx)
        s = signals(c, pre)
        got, keyed, sent, older = ([s(f"{m}{u}") for u in range(2)] for m in ("got", "keyed", "sent", "older"))
        per_send = 16 * K4 if n == 3 else 16
        block = ctx.enter_context(nc.Block())

        @block.gpsimd
        def _(pool):
            def scatter(g, u):
                pool.wait_ge(s("h_done"), g + 1)
                pool.sem_inc(s("issuing"), 1)
                for k in range(K4):
                    pool.indirect_dma_start(c.a_dram[:, :], bass.IndirectOffsetOnAxis(ap=at[:, u, 1, k:k + 1], axis=0),
                                            h[:, u, k, :], None, bounds_check=N - 1, oob_is_err=False,
                                            compute_op=ALU.add).then_inc(sent[u], 16)

            def step(g, u, i):
                if not early(g, 2):
                    pool.wait_ge(s("summed"), g - 1)
                    if n == 3:
                        pool.wait_ge(sent[u], i * per_send)
                pool.tensor_copy(at[:, u, 0, :], place[:, bass.ds(g * K4, K4)]).then_inc(s("at"), 1)
                pool.tensor_copy(at[:, u, 1, :], side["last_at"][:, bass.ds(g * K4, K4)]).then_inc(s("at"), 1)
                pool.wait_ge(s("at"), g * 2 + 2)
                pool.sem_inc(s("issuing"), 1)
                for k in range(K4):
                    pool.indirect_dma_start(x[:, u, k, :], None, table[:, :],
                                            bass.IndirectOffsetOnAxis(ap=at[:, u, 0, k:k + 1], axis=0)).then_inc(got[u], 16)
                if n == 3 and not early(g, 1):
                    scatter(g - 1, 1 - u)
            steps(pool, GROUPS, step)
            if n == 3:
                scatter(GROUPS - 1, 1)
                for u in range(2):
                    pool.wait_ge(sent[u], GROUPS // 2 * per_send)

        @block.sync
        def _(sp):
            def store(g, u):
                sp.wait_ge(s("h_done"), g + 1)
                sp.dma_start(edge_rows((c.h1_dram, c.h2_dram)[n - 1], g), h[:, u, :, :]).then_inc(sent[u], 16)

            def step(g, u, i):
                if not early(g, 2):
                    sp.wait_ge(s("masked"), g - 1)
                sp.dma_start(keys[:, u, :], side["keys"][bass.ds(g * ROWS + 1, ROWS)].rearrange("(o n) -> o n", o=1)
                             .to_broadcast([P, ROWS])).then_inc(keyed[u], 16)
                if n == 3:
                    if not early(g, 2):
                        sp.wait_ge(s("h_done"), g - 1)
                    sp.dma_start(old[:, u, 0, :, :], edge_rows(c.h1_dram, g)).then_inc(older[u], 16)
                    sp.dma_start(old[:, u, 1, :, :], edge_rows(c.h2_dram, g)).then_inc(older[u], 16)
                elif not early(g, 1):
                    store(g - 1, 1 - u)
            steps(sp, GROUPS, step)
            if n < 3:
                store(GROUPS - 1, 1)
                for u in range(2):
                    sp.wait_ge(sent[u], GROUPS // 2 * per_send)

        @block.tensor
        def _(pe):
            def step(g, u, i):
                pe.wait_ge(got[u], (i + 1) * 16 * K4)
                pe.wait_ge(s("masked"), g + 1)
                if not early(g, 2):
                    pe.wait_ge(s("total"), (g - 1) * K4)
                for k in range(K4):
                    last = pe.matmul(acc[:, u * K4 + k, 0:D], same[:, u, k, :], x[:, u, k, :], start=True, stop=False)
                last.then_inc(s("summed"), 1)
                for k in range(K4):
                    if early(g, 1) and k == 0:
                        pe.wait_ge(s("total_clear"), 1)
                    else:
                        pe.wait_ge(s("total"), g * K4 + k)
                    pe.matmul(acc[:, u * K4 + k, 0:D], cont[96:P, u, k, :], total[96:P, (k - 1) % K4, :],
                              start=False, stop=True).then_inc(s("acc"), 1)
            steps(pe, GROUPS, step)

        @block.vector
        def _(dve):
            dve.memset(total[:, K4 - 1, :], 0.0).then_inc(s("total_clear"), 1)
            dve.wait_ge(s("total_clear"), 1)

            def masks(g, u, i):
                dve.wait_ge(keyed[u], 16 * (i + 1))
                if not early(g, 2):
                    dve.wait_ge(s("acc"), (g - 1) * K4)
                for k in range(K4):
                    row = keys[:, u, k * P:(k + 1) * P]
                    dve.tensor_scalar(same[:, u, k, :], row, side["key"][:, bass.ds(g * K4 + k + 1, 1)],
                                      weight[:, bass.ds(g * K4 + k, 1)], ALU.is_equal, ALU.mult)
                    last = dve.tensor_scalar(cont[96:P, u, k, :], row[96:P, :], side["key"][96:P, bass.ds(g * K4 + k, 1)],
                                             c.end[96:P, 0:1], ALU.is_equal, ALU.mult)
                last.then_inc(s("masked"), 1)

            def step(g, u, i):
                masks(g, u, i)
                for k in range(K4):
                    dve.wait_ge(s("acc"), g * K4 + k + 1)
                    if not early(g, 1):
                        dve.wait_ge(s("squared"), g)
                    dve.tensor_copy(total[:, k, :], acc[:, u * K4 + k, 0:D]).then_inc(s("total"), 1)
                dve.wait_ge(s("squared"), g + 1)
                dve.tensor_scalar(ss[:, :], ss[:, :], NORM_EPS2, None, ALU.max).then_inc(s("guarded"), 1)
                dve.wait_ge(s("rn"), g + 1)
                if not early(g, 2):
                    dve.wait_ge(sent[u], i * per_send)
                for k in range(K4):
                    last = dve.tensor_scalar(h[:, u, k, :], total[:, k, :], rn[:, k:k + 1], None, ALU.mult)
                if n < 3:
                    last.then_inc(s("h_done"), 1)
                    return
                last.then_inc(s("h_own"), 1)
                dve.wait_ge(older[u], (i + 1) * 32)
                for m in range(2):
                    dve.wait_ge(s("h_own"), 2 * g + m + 1)
                    last = dve.scalar_tensor_tensor(out=h[:, u, :, :], in0=old[:, u, m, :, :], scalar=0.25, in1=h[:, u, :, :],
                                                    op0=ALU.mult, op1=ALU.add)
                    last.then_inc(s(("h_own", "h_done")[m]), 1)
            steps(dve, GROUPS, step)

        @block.scalar
        def _(act):
            def step(g, u, i):
                act.wait_ge(s("guarded"), g)
                for k in range(K4):
                    act.wait_ge(s("total"), g * K4 + k + 1)
                    last = act.activation(square[:, k, :], total[:, k, :], ACT.Square, accum_out=ss[:, k:k + 1])
                last.then_inc(s("squared"), 1)
                act.wait_ge(s("guarded"), g + 1)
                act.activation(rn[:, :], ss[:, :], ACT.Ln, scale=NORM_SCALE).then_inc(s("rn_log"), 1)
                act.wait_ge(s("rn_log"), g + 1)
                act.activation(rn[:, :], rn[:, :], ACT.Exp, scale=-0.5,
                               bias=c.consts[:, 5:6] if n == 3 else c.consts[:, 2:3]).then_inc(s("rn"), 1)
            steps(act, GROUPS, step)


def node_pass_two(c):
    nc = c.nc
    with c.phase() as ctx:
        sb = lambda n, shape, dt=F32: c.sb("n2_" + n, shape, dt, ctx=ctx)
        x, x3, y = sb("x", [P, 2, K4, D]), sb("x3", [P, 2, K4, D]), sb("y", [P, 2, K4, D])
        xT, h, square = sb("xT", [P, 2, ROWS]), sb("h", [P, K4, D]), sb("square", [P, K4, D])
        stats, mv, rs = sb("stats", [P, 3, K4, 6]), sb("mv", [P, 3, K4, 2]), sb("rs", [P, 3, K4])
        ss, rn = sb("ss", [P, K4]), sb("rn", [P, K4])
        turn = c.ps("n2_turn", [P, 2, 512], ctx=ctx)
        prod = c.ps("n2_prod", [P, K4, D], ctx=ctx)
        s = signals(c, "n2_")
        loaded, sent3, senty = ([s(f"{n}{u}") for u in range(2)] for n in ("loaded", "sent3", "senty"))
        block = ctx.enter_context(nc.Block())

        @block.sync
        def _(sp):
            def store(g, u, i):
                if isinstance(g, int) and g == NG - 1:
                    sp.wait_ge(sent3[1 - u], 16 * (i + 1))
                    sp.wait_ge(senty[1 - u], 16 * (i + 1))
                sp.wait_ge(s("x3_done"), g + 1)
                sp.dma_start(node_rows(c.x3_dram, g), x3[:, u, :, :]).then_inc(sent3[u], 16)
                sp.wait_ge(s("y_done"), g + 1)
                sp.dma_start(node_rows(c.out, g), y[:, u, :, :]).then_inc(senty[u], 16)

            def step(g, u, i):
                if not early(g, 2):
                    sp.wait_ge(s("x3_sum"), g - 1)
                sp.dma_start(x[:, u, :, :], node_rows(c.a_dram, g)).then_inc(loaded[u], 16)
                if not early(g, 1):
                    store(g - 1, 1 - u, i - 1 if u == 0 else i)
            steps(sp, NG, step)
            store(NG - 1, 1, NG // 2 - 1)
            for u in range(2):
                sp.wait_ge(sent3[u], 16 * (NG // 2))
                sp.wait_ge(senty[u], 16 * (NG // 2))

        @block.vector
        def _(dve):
            def step(g, u, i):
                dve.wait_ge(loaded[u], 16 * (i + 1))
                row_stats(dve, x[:, u], stats[:, 0], mv[:, 0], K4, s, "a", g)
                row_apply(dve, x[:, u], x[:, u], mv[:, 0], rs[:, 0], K4, s, "a", g, "x2")
                dve.wait_ge(s("prod"), g + 1)
                dve.tensor_tensor(h[:, :, :], prod[:, :, :], c.bias[:, :].rearrange("p (o d) -> p o d", o=1)
                                  .to_broadcast([P, K4, D]), ALU.add).then_inc(s("biased"), 1)
                dve.wait_ge(s("squared"), g + 1)
                dve.tensor_scalar(ss[:, :], ss[:, :], NORM_EPS2, None, ALU.max).then_inc(s("guarded"), 1)
                dve.wait_ge(s("rn"), g + 1)
                if not early(g, 2):
                    dve.wait_ge(sent3[u], 16 * i)
                for k in range(K4):
                    last = dve.scalar_tensor_tensor(out=x3[:, u, k, :], in0=h[:, k, :], scalar=rn[:, k:k + 1], in1=x[:, u, k, :],
                                                    op0=ALU.mult, op1=ALU.add)
                last.then_inc(s("x3_sum"), 1)
                dve.wait_ge(s("x3_sum"), g + 1)
                row_stats(dve, x3[:, u], stats[:, 1], mv[:, 1], K4, s, "b", g)
                row_apply(dve, x3[:, u], x3[:, u], mv[:, 1], rs[:, 1], K4, s, "b", g, "x3_done")
                dve.wait_ge(s("x3_done"), g + 1)
                row_stats(dve, x3[:, u], stats[:, 2], mv[:, 2], K4, s, "c", g)
                if not early(g, 2):
                    dve.wait_ge(senty[u], 16 * i)
                row_apply(dve, y[:, u], x3[:, u], mv[:, 2], rs[:, 2], K4, s, "c", g, "y_done")
            steps(dve, NG, step)

        @block.scalar
        def _(act):
            def step(g, u, i):
                row_scale(act, c, mv[:, 0], rs[:, 0], s, "a", g)
                act.wait_ge(s("xT"), g + 1)
                act.activation(xT[:, :, :], turn[:, :, :], ACT.Copy).then_inc(s("xT_sb"), 1)
                act.wait_ge(s("biased"), g + 1)
                act.activation(h[:, :, :], h[:, :, :], ACT.Relu).then_inc(s("relu"), 1)
                act.wait_ge(s("relu"), g + 1)
                for k in range(K4):
                    last = act.activation(square[:, k, :], h[:, k, :], ACT.Square, accum_out=ss[:, k:k + 1])
                last.then_inc(s("squared"), 1)
                act.wait_ge(s("guarded"), g + 1)
                act.activation(rn[:, :], ss[:, :], ACT.Ln, scale=NORM_SCALE).then_inc(s("rn_log"), 1)
                act.wait_ge(s("rn_log"), g + 1)
                act.activation(rn[:, :], rn[:, :], ACT.Exp, scale=-0.5, bias=c.consts[:, 2:3]).then_inc(s("rn"), 1)
                row_scale(act, c, mv[:, 1], rs[:, 1], s, "b", g)
                row_scale(act, c, mv[:, 2], rs[:, 2], s, "c", g)
            steps(act, NG, step)

        @block.tensor
        def _(pe):
            def step(g, u, i):
                pe.wait_ge(s("x2"), g + 1)
                pe.wait_ge(s("xT_sb"), g)
                for f in range(2):
                    for k in range(K4):
                        last = pe.transpose(turn[:, f, k * P:(k + 1) * P], x[:, u, k, f * P:(f + 1) * P], c.ident[:, :])
                last.then_inc(s("xT"), 1)
                pe.wait_ge(s("xT_sb"), g + 1)
                pe.wait_ge(s("biased"), g)
                for k in range(K4):
                    for f in range(2):
                        last = pe.matmul(prod[:, k, :], xT[:, f, k * P:(k + 1) * P], c.wg[:, f, 0:D], start=(f == 0), stop=(f == 1))
                last.then_inc(s("prod"), 1)
            steps(pe, NG, step)


def attention_layer(c, layer):
    nc = c.nc
    side = c.d
    two = layer == 2
    H = H2 if two else H3
    W = D + H
    kinds = 2 if two else 1
    source = c.a_dram if two else c.x3_dram
    target = c.x3_dram if two else c.out
    with c.phase() as ctx:
        pre = f"l{layer}_"
        sb = lambda n, shape, dt=F32: c.sb(pre + n, shape, dt, ctx=ctx)
        x, at = sb("x", [P, 2, 2 * K4, D]), sb("at", [P, 2, 3, K4], I32)
        keys, cuts = sb("keys", [P, 2, ROWS + 1]), sb("cuts", [H3, 2, ROWS + 1])
        same, cont = sb("same", [P, K4, P]), sb("cont", [P, K4, P])
        xT = sb("xT", [P, 2, 2, ROWS])
        hh = sb("hh", [P, 2, K4, D]) if two else None
        score, e = sb("score", [P, 2, K4, 2 * H2]), sb("e", [P, 2, K4, H])
        esc, top = sb("esc", [P, K4, H]), sb("top", [P, 2, K4, H])
        run_max, seg_max = sb("run_max", [H3, 2, ROWS]), sb("seg_max", [H3, ROWS])
        prob, fade = sb("prob", [P, 2, K4, H]), sb("fade", [P, H])
        msg, total, carry = sb("msg", [P, K4, W]), sb("total", [P, K4, W]), sb("carry", [P, W])
        den = sb("den", [P, K4, H])
        r, y = sb("r", [P, K4, D]), sb("y", [P, 2, K4, D])
        square = sb("square", [P, K4, D]) if two else None
        stats, mv, rs = sb("stats", [P, 2 * K4, 6]), sb("mv", [P, 2 * K4, 2]), sb("rs", [P, 2 * K4])
        stats2, mv2, rs2 = sb("stats2", [P, K4, 6]), sb("mv2", [P, K4, 2]), sb("rs2", [P, K4])
        ss, rn = sb("ss", [P, K4]), sb("rn", [P, K4])
        ps_turn = c.ps(pre + "turn", [P, 2, 512], ctx=ctx)
        ps_h = c.ps(pre + "h", [P, K4, D], ctx=ctx)
        ps_acc = c.ps(pre + "acc", [P, 2, 512], ctx=ctx)
        ps_score = c.ps(pre + "ps_score", [P, 512], ctx=ctx)
        ps_max = c.ps(pre + "ps_max", [P, 512], ctx=ctx)
        raw = ps_score[:, 0:2 * K4 * 2 * H2].rearrange("p (o k h) -> p o k h", o=2, k=K4)
        back = ps_score[:, 128:128 + K4 * H].rearrange("p (k h) -> p k h", k=K4)
        head_of = ps_score[:, 256:256 + H]
        s = signals(c, pre)
        got_s, got_d, keyed, sent = ([s(f"{n}{u}") for u in range(2)] for n in ("got_s", "got_d", "keyed", "sent"))
        if two:
            split = lambda t: t.rearrange("p k (h d) -> p k h d", h=H)
            spread = lambda t: t.rearrange("p k (h o) -> p k h o", o=1).to_broadcast([t.shape[0], t.shape[1], H, D // H])
        else:
            split = lambda t: t.rearrange("p k (d h) -> p k d h", h=H)
            spread = lambda t: t.rearrange("p k (o h) -> p k o h", o=1).to_broadcast([t.shape[0], t.shape[1], D // H, H])
        one = lambda t: t.rearrange("p (o d) -> p o d", o=1)
        block = ctx.enter_context(nc.Block())

        @block.gpsimd
        def _(pool):
            def scatter(g, u):
                pool.wait_ge(s("y_done"), g + 1)
                pool.sem_inc(s("issuing"), 1)
                for k in range(K4):
                    pool.indirect_dma_start(target[:, :], bass.IndirectOffsetOnAxis(ap=at[:, u, 2, k:k + 1], axis=0),
                                            y[:, u, k, :], None, bounds_check=N - 1, oob_is_err=False).then_inc(sent[u], 16)

            def step(g, u, i):
                if not early(g, 2):
                    pool.wait_ge(sent[u], i * 16 * K4)
                    pool.wait_ge(s("msg"), g - 1)
                    pool.wait_ge(s("summed"), g - 1)
                for n, col in enumerate((side["other"], side["own"], side["last_at"])):
                    pool.tensor_copy(at[:, u, n, :], col[:, bass.ds(g * K4, K4)]).then_inc(s("at"), 1)
                pool.wait_ge(s("at"), g * 3 + 3)
                pool.sem_inc(s("issuing"), 1)
                for n, got in enumerate((got_s, got_d)):
                    for k in range(K4):
                        pool.indirect_dma_start(x[:, u, n * K4 + k, :], None, source[:, :],
                                                bass.IndirectOffsetOnAxis(ap=at[:, u, n, k:k + 1], axis=0)).then_inc(got[u], 16)
                if not early(g, 1):
                    scatter(g - 1, 1 - u)
            steps(pool, GROUPS, step)
            scatter(GROUPS - 1, 1)
            for u in range(2):
                pool.wait_ge(sent[u], GROUPS // 2 * 16 * K4)

        @block.sync
        def _(sp):
            def step(g, u, i):
                if not early(g, 2):
                    sp.wait_ge(s("masked"), g - 1)
                    sp.wait_ge(s("seg_max"), g - 1)
                sp.dma_start(keys[:, u, :], side["keys"][bass.ds(g * ROWS, ROWS + 1)].rearrange("(o n) -> o n", o=1)
                             .to_broadcast([P, ROWS + 1])).then_inc(keyed[u], 16)
                sp.dma_start(cuts[0:H, u, :], side["cuts"][bass.ds(g * ROWS, ROWS + 1)].rearrange("(o n) -> o n", o=1)
                             .to_broadcast([H, ROWS + 1])).then_inc(keyed[u], 16)
            steps(sp, GROUPS, step)

        @block.tensor
        def _(pe):
            def step(g, u, i):
                for n in range(2):
                    if two:
                        pe.wait_ge(s("x2"), g + 1)
                    else:
                        pe.wait_ge((got_s, got_d)[n][u], (i + 1) * 16 * K4)
                    pe.wait_ge(s("xT_sb"), 2 * g + n)
                    for f in range(2):
                        for k in range(K4):
                            last = pe.transpose(ps_turn[:, f, k * P:(k + 1) * P], x[:, u, n * K4 + k, f * P:(f + 1) * P],
                                                c.ident[:, :])
                    last.then_inc(s("xT"), 1)
                    pe.wait_ge(s("xT_sb"), 2 * g + n + 1)
                    if two:
                        pe.wait_ge(s("h_sb"), 2 * g + n)
                        for k in range(K4):
                            for f in range(2):
                                last = pe.matmul(ps_h[:, k, :], xT[:, n, f, k * P:(k + 1) * P], c.wg[:, f, 0:D],
                                                 start=(f == 0), stop=(f == 1))
                        last.then_inc(s("h"), 1)
                pe.wait_ge(s("fade_in"), g)
                for n in range(2):
                    vec = (lambda f: c.wg[:, f, D:D + 2 * H2]) if two else (lambda f: c.wuv[:, f, n * H3:(n + 1) * H3])
                    for k in range(K4):
                        for f in range(2):
                            last = pe.matmul(raw[:, n, k, :], xT[:, n, f, k * P:(k + 1) * P], vec(f), start=(f == 0), stop=(f == 1))
                last.then_inc(s("raw"), 1)
                pe.wait_ge(s("esc"), g + 1)
                for k in range(K4):
                    last = pe.matmul(ps_max[0:H, k * P:(k + 1) * P], esc[:, k, :], c.ident[:, :], start=True, stop=True)
                last.then_inc(s("escT"), 1)
                pe.wait_ge(s("seg_max"), g + 1)
                for k in range(K4):
                    last = pe.matmul(back[:, k, :], seg_max[0:H, k * P:(k + 1) * P], c.ident[0:H, 0:H], start=True, stop=True)
                last.then_inc(s("back"), 1)
                pe.wait_ge(s("top"), g + 1)
                pe.matmul(head_of, c.first[:, :], top[:, u, 0, :], start=True, stop=True).then_inc(s("head_of"), 1)
                pe.wait_ge(s("msg"), g + 1)
                pe.wait_ge(s("masked"), g + 1)
                pe.wait_ge(s("carry"), g + 1)
                for k in range(K4):
                    if k >= 2:
                        pe.wait_ge(s("total"), g * K4 + k - 1)
                    pe.matmul(ps_acc[:, k % 2, 0:W], same[:, k, :], msg[:, k, :], start=True, stop=False)
                    if k:
                        pe.wait_ge(s("total"), g * K4 + k)
                    rest = carry[96:P, :] if k == 0 else total[96:P, k - 1, :]
                    pe.matmul(ps_acc[:, k % 2, 0:W], cont[96:P, k, :], rest, start=False, stop=True).then_inc(s("acc"), 1)
            steps(pe, GROUPS, step)

        @block.scalar
        def _(act):
            def step(g, u, i):
                if two:
                    row_scale(act, c, mv, rs, s, "a", g)
                for n in range(2):
                    act.wait_ge(s("xT"), 2 * g + n + 1)
                    act.activation(xT[:, n, :, :], ps_turn[:, :, :], ACT.Copy).then_inc(s("xT_sb"), 1)
                    if two:
                        act.wait_ge(s("h"), 2 * g + n + 1)
                        act.wait_ge(s("h_used"), g)
                        act.activation(hh[:, n, :, :], ps_h[:, :, :], ACT.Copy).then_inc(s("h_sb"), 1)
                act.wait_ge(s("raw"), g + 1)
                act.activation(score[:, :, :, :], raw, ACT.Copy).then_inc(s("score"), 1)
                act.wait_ge(s("below"), g + 1)
                act.activation(prob[:, 0:kinds, :, :], prob[:, 0:kinds, :, :], ACT.Exp).then_inc(s("prob"), 1)
                act.wait_ge(s("fade_in"), g + 1)
                act.activation(fade[96:P, :], fade[96:P, :], ACT.Exp).then_inc(s("fade"), 1)
                if two:
                    act.wait_ge(s("biased"), g + 1)
                    act.activation(r[:, :, :], r[:, :, :], ACT.Relu).then_inc(s("relu"), 1)
                    act.wait_ge(s("relu"), g + 1)
                    for k in range(K4):
                        last = act.activation(square[:, k, :], r[:, k, :], ACT.Square, accum_out=ss[:, k:k + 1])
                    last.then_inc(s("squared"), 1)
                    act.wait_ge(s("guarded"), g + 1)
                    act.activation(rn[:, :], ss[:, :], ACT.Ln, scale=NORM_SCALE).then_inc(s("rn_log"), 1)
                    act.wait_ge(s("rn_log"), g + 1)
                    act.activation(rn[:, :], rn[:, :], ACT.Exp, scale=-0.5, bias=c.consts[:, 2:3]).then_inc(s("rn"), 1)
                row_scale(act, c, mv2, rs2, s, "b", g)
            steps(act, GROUPS, step)

        @block.vector
        def _(dve):
            count = {}

            def chain(name, ins, g, per):
                ins.then_inc(s(name), 1)
                count[name] = count.get(name, 0) % per + 1
                dve.wait_ge(s(name), g * per + count[name])

            dve.memset(total[:, K4 - 1, :], 0.0).then_inc(s("clear"), 1)
            dve.memset(top[:, 1, :, :], 0.0).then_inc(s("clear"), 1)
            dve.memset(run_max[0:H, 1, :], LOW).then_inc(s("clear"), 1)
            dve.wait_ge(s("clear"), 3)

            def step(g, u, i):
                dve.wait_ge(keyed[u], 32 * (i + 1))
                dve.wait_ge(s("acc"), g * K4)
                for k in range(K4):
                    row = keys[:, u, 1 + k * P:1 + (k + 1) * P]
                    dve.tensor_scalar(same[:, k, :], row, side["key"][:, bass.ds(g * K4 + k + 1, 1)], None, ALU.is_equal)
                    last = dve.tensor_scalar(cont[96:P, k, :], row[96:P, :], side["key"][96:P, bass.ds(g * K4 + k, 1)],
                                             c.end[96:P, 0:1], ALU.is_equal, ALU.mult)
                last.then_inc(s("masked"), 1)
                if two:
                    dve.wait_ge(got_s[u], (i + 1) * 16 * K4)
                    dve.wait_ge(got_d[u], (i + 1) * 16 * K4)
                    row_stats(dve, x[:, u], stats, mv, 2 * K4, s, "a", g)
                    row_apply(dve, x[:, u], x[:, u], mv, rs, 2 * K4, s, "a", g, "x2")
                dve.wait_ge(s("score"), g + 1)
                if two:
                    for n in range(2):
                        last = dve.tensor_tensor(e[:, n, :, :], score[:, n, :, 0:H], score[:, 1, :, H:2 * H], ALU.add)
                    m = 2
                else:
                    last = dve.tensor_tensor(e[:, 0, :, :], score[:, 0, :, :], score[:, 1, :, :], ALU.add)
                    chain("e", last, g, 3)
                    last = dve.tensor_tensor(e[:, 0, :, :], e[:, 0, :, :], one(c.bu[:, :]).to_broadcast([P, K4, H]), ALU.add)
                    m = 1
                per_e = 2 if two else 3
                chain("e", last, g, per_e)
                last = dve.scalar_tensor_tensor(out=e[:, 0:m, :, :], in0=e[:, 0:m, :, :], scalar=0.2, in1=e[:, 0:m, :, :],
                                                op0=ALU.mult, op1=ALU.max)
                chain("e", last, g, per_e)
                dve.tensor_tensor(esc[:, :, :], e[:, 0, :, :], e[:, m - 1, :, :], ALU.max).then_inc(s("esc"), 1)
                dve.wait_ge(s("escT"), g + 1)
                dve.tensor_tensor_scan(run_max[0:H, u, :], cuts[0:H, u, 0:ROWS], ps_max[0:H, :],
                                       run_max[0:H, 1 - u, ROWS - 1:ROWS], ALU.add, ALU.max).then_inc(s("run_max"), 1)
                dve.wait_ge(s("run_max"), g + 1)
                dve.wait_ge(s("back"), g)
                dve.tensor_tensor_scan(seg_max[0:H, :][:, ::-1], cuts[0:H, u, 1:ROWS + 1][:, ::-1], run_max[0:H, u, :][:, ::-1],
                                       LOW, ALU.add, ALU.max).then_inc(s("seg_max"), 1)
                dve.wait_ge(s("back"), g + 1)
                dve.tensor_copy(top[:, u, :, :], back).then_inc(s("top"), 1)
                dve.wait_ge(s("top"), g + 1)
                for n in range(m):
                    last = dve.tensor_tensor(prob[:, n, :, :], e[:, n, :, :], top[:, u, :, :], ALU.subtract)
                last.then_inc(s("below"), 1)
                dve.wait_ge(s("head_of"), g + 1)
                last = dve.tensor_tensor(fade[96:P, :], top[96:P, 1 - u, K4 - 1, :], head_of[96:P, :], ALU.subtract)
                chain("fade_sub", last, g, 1)
                dve.tensor_scalar(fade[96:P, :], fade[96:P, :], 0.0, None, ALU.min).then_inc(s("fade_in"), 1)
                dve.wait_ge(s("prob"), g + 1)
                feat = hh[:, 0, :, :] if two else x[:, u, 0:K4, :]
                dve.tensor_copy(msg[:, :, D:W], prob[:, 0, :, :])
                dve.tensor_tensor(split(msg[:, :, 0:D]), split(feat), spread(prob[:, 0, :, :]), ALU.mult).then_inc(s("msg"), 1)
                dve.wait_ge(s("fade"), g + 1)
                dve.tensor_tensor(split(one(carry[96:P, 0:D])), split(total[96:P, K4 - 1:K4, 0:D]), spread(one(fade[96:P, :])), ALU.mult)
                dve.tensor_tensor(carry[96:P, D:W], total[96:P, K4 - 1, D:W], fade[96:P, :], ALU.mult).then_inc(s("carry"), 1)
                for k in range(K4):
                    dve.wait_ge(s("acc"), g * K4 + k + 1)
                    if k == K4 - 1:
                        dve.wait_ge(s("carry"), g + 1)
                    dve.tensor_copy(total[:, k, :], ps_acc[:, k % 2, 0:W]).then_inc(s("total"), 1)
                dve.wait_ge(s("total"), (g + 1) * K4)
                if two:
                    last = dve.tensor_tensor(split(r[:, :, :]), split(hh[:, 1, :, :]), spread(prob[:, 1, :, :]), ALU.mult)
                    last = dve.tensor_tensor(den[:, :, :], total[:, :, D:W], prob[:, 1, :, :], ALU.add)
                    last.then_inc(s("h_used"), 1)
                    dve.wait_ge(s("h_used"), g + 1)
                    dve.tensor_tensor(r[:, :, :], r[:, :, :], total[:, :, 0:D], ALU.add)
                    chain("r", dve.reciprocal(den[:, :, :], den[:, :, :]), g, 3)
                    chain("r", dve.tensor_tensor(split(r[:, :, :]), split(r[:, :, :]), spread(den[:, :, :]), ALU.mult), g, 3)
                    chain("r", dve.tensor_tensor(r[:, :, :], r[:, :, :], one(c.bias[:, :]).to_broadcast([P, K4, D]), ALU.add), g, 3)
                    dve.sem_inc(s("biased"), 1)
                    dve.wait_ge(s("squared"), g + 1)
                    dve.tensor_scalar(ss[:, :], ss[:, :], NORM_EPS2, None, ALU.max).then_inc(s("guarded"), 1)
                    dve.wait_ge(s("rn"), g + 1)
                    if not early(g, 2):
                        dve.wait_ge(sent[u], i * 16 * K4)
                    for k in range(K4):
                        last = dve.scalar_tensor_tensor(out=y[:, u, k, :], in0=r[:, k, :], scalar=rn[:, k:k + 1],
                                                        in1=x[:, u, K4 + k, :], op0=ALU.mult, op1=ALU.add)
                    last.then_inc(s("summed"), 1)
                else:
                    chain("r", dve.reciprocal(den[:, :, :], total[:, :, D:W]), g, 2)
                    chain("r", dve.tensor_tensor(split(r[:, :, :]), split(total[:, :, 0:D]), spread(den[:, :, :]), ALU.mult), g, 2)
                    if not early(g, 2):
                        dve.wait_ge(sent[u], i * 16 * K4)
                    dve.wait_ge(got_d[u], (i + 1) * 16 * K4)
                    dve.tensor_tensor(y[:, u, :, :], r[:, :, :], x[:, u, K4:2 * K4, :], ALU.add).then_inc(s("summed"), 1)
                dve.wait_ge(s("summed"), g + 1)
                row_stats(dve, y[:, u], stats2, mv2, K4, s, "b", g)
                row_apply(dve, y[:, u], y[:, u], mv2, rs2, K4, s, "b", g, "y_done")
            steps(dve, GROUPS, step)


_NAMES = {"x": "x", "src": "src", "dst": "dst", "ea": "edge_attr_64", "ew": "edge_weight", "fw1": "L0_gnn_fw1",
          "fb1": "L0_gnn_fb1", "fw2": "L0_gnn_fw2", "fb2": "L0_gnn_fb2", "w1": "L0_gnn_w1", "w2": "L0_gnn_w2",
          "b2": "L0_gnn_b2", "w3": "L0_gnn_w3", "b3": "L0_gnn_b3", "W": "L2_gnn_W", "att_src": "L2_gnn_att_src",
          "att_dst": "L2_gnn_att_dst", "bias": "L2_gnn_bias", "W_u": "L3_gnn_W_u", "b_u": "L3_gnn_b_u",
          "W_v": "L3_gnn_W_v"}


def build(nc, a, out, stop=None):
    with ExitStack() as ctx:
        c = Core(nc, ctx)
        c.out = out
        dram = lambda n, shape, dt=F32: nc.dram_tensor(n, shape, dt, kind="Internal").ap()
        c.h1_dram, c.h2_dram = dram("h1_rows", (EP + 1, D)), dram("h2_rows", (EP + 1, D))
        c.place_dram = dram("node_places", (N, 1), I32)
        c.a_dram, c.x3_dram = dram("a_rows", (N, D)), dram("x3_rows", (N, D))
        c.wg = c.sb("wg", [P, 2, D + 2 * H2])
        c.fw2T, c.w1T, c.w2T, c.w3T = (c.sb(n, [P, 2, D]) for n in ("fw2T", "w1T", "w2T", "w3T"))
        c.fw1T, c.wuv = c.sb("fw1T", [BASIS, D]), c.sb("wuv", [P, 2, 16])
        c.fb1, c.b2 = c.sb("fb1", [P, 2]), c.sb("b2", [P, 2])
        c.fb2, c.b3, c.bias, c.c0 = (c.sb(n, [P, D]) for n in ("fb2", "b3", "bias", "c0"))
        c.bu = c.sb("bu", [P, H3])
        c.ident, c.identb, c.first = c.sb("ident", [P, P]), c.sb("identb", [P, P], BF16), c.sb("first", [P, P])
        c.ltri, c.ones = c.sb("ltri", [P, P], BF16), c.sb("ones", [P, P], BF16)
        c.window, c.digits = c.sb("window", [P, 2 * P], BF16), c.sb("digits", [P, 256], BF16)
        c.digits_i, c.end = c.sb("digits_i", [P, 256], I32), c.sb("end", [P, 1])
        c.consts, c.zero_row = c.sb("consts", [P, 8]), c.sb("zero_row", [P, D])
        c.absent = c.sb("absent", [P, N // 125], I32)
        c.pay_d, c.pay_s = c.sb("pay_d", [P, T, 4], I32), c.sb("pay_s", [P, T, 4], I32)
        sides = {}
        for s, pay in (("d", c.pay_d), ("s", c.pay_s)):
            sides[s] = {"pay": pay, "key": c.sb(s + "_key", [P, T + 1]), "last_at": c.sb(s + "_last", [P, T], I32),
                        "keys": dram(s + "_keys", (EP + 2,)), "w": c.sb(s + "_w", [P, T]), "w8": c.sb(s + "_w8", [P, T]),
                        "cuts": dram(s + "_cuts", (EP + 1,)),
                        "own": c.sb(s + "_own", [P, T], I32), "other": c.sb(s + "_other", [P, T], I32),
                        "rows": dram(s + "_sorted", (EP, 4), I32), "rows0": dram(s + "_half_sorted", (EP, 4), I32)}
            sides[s]["columns"] = [(sides[s]["own"], 0, N - 1), (sides[s]["other"], 1, N - 1)]
        c.edge_of = c.sb("edge_of", [P, T], I32)
        sides["d"]["columns"].append((c.edge_of, 3, E - 1))
        c.d, c.s = sides["d"], sides["s"]
        c.cutoff, c.s_place = c.sb("cutoff", [P, T]), c.sb("s_place", [P, T], I32)
        setup_phase(c, a)
        if stop == "setup": return c
        payload_phase(c, a)
        for s in ("d", "s"):
            sort_pass(c, s + "0_", sides[s]["pay"], 0, sides[s]["rows0"])
            sort_pass(c, s + "1_", sides[s]["pay"], 8, sides[s]["rows"])
            index_phase(c, s + "_ix_", sides[s])
        if stop == "sort": return c
        node_pass_one(c, a)
        cosine_phase(c)
        if stop == "p1": return c
        filter_layer(c, a)
        if stop == "l0": return c
        place_phase(c)
        propagation_round(c, 1)
        if stop == "l11": return c
        propagation_round(c, 2)
        propagation_round(c, 3)
        if stop == "l1": return c
        node_pass_two(c)
        if stop == "p2": return c
        attention_layer(c, 2)
        attention_layer(c, 3)


_INS = ["x", "src", "dst", "edge_attr_64", "edge_weight", "L0_gnn_fw1", "L0_gnn_fb1", "L0_gnn_fw2", "L0_gnn_fb2",
        "L0_gnn_w1", "L0_gnn_w2", "L0_gnn_b2", "L0_gnn_w3", "L0_gnn_b3", "L2_gnn_W", "L2_gnn_att_src",
        "L2_gnn_att_dst", "L2_gnn_bias", "L3_gnn_W_u", "L3_gnn_b_u", "L3_gnn_W_v"]


def kernel(**inputs):
    import numpy as np
    import concourse.bacc as bacc
    from concourse.bass_utils import run_bass_kernel_spmd

    nc = bacc.Bacc("TRN2", target_bir_lowering=False, num_devices=1)
    arrays, given = {}, {}
    for name in _INS:
        array = np.ascontiguousarray(inputs[name])
        arrays[name + "_in"] = array
        given[name] = nc.dram_tensor(name + "_in", array.shape, mybir.dt.from_np(array.dtype), kind="ExternalInput").ap()
    out = nc.dram_tensor("out", (N, D), F32, kind="ExternalOutput").ap()
    build(nc, {short: given[name] for short, name in _NAMES.items()}, out)
    result = run_bass_kernel_spmd(nc, [arrays], core_ids=[0])
    return result.results[0]["out"]
```

```python
from contextlib import ExitStack, contextmanager
import math

import concourse.bass as bass
from concourse import mybir

F32 = mybir.dt.float32
BF16 = mybir.dt.bfloat16
I32 = mybir.dt.int32
ALU = mybir.AluOpType
ACT = mybir.ActivationFunctionType

P = 128
N, D = 50000, 256
E = 25000
BASIS = 64
K4 = 4
ROWS = K4 * P
GROUPS = 50
T = GROUPS * K4
EP = T * P
EDGE_PARTS = E // T
HALVES = ((0, 26), (26, 24))
NG = -(-N // ROWS)
PAD_KEY = 65535
FAR = 100000.0
LOW = -1.0e30
OTHER, OWN, EDGE, LAST = range(4)
LN_EPS = 1e-5
NORM_EPS2 = 1e-24
NORM_SCALE = 2.0 ** 20
H2, H3 = 4, 8


class Step:

    def __init__(self, r, unroll, off):
        self.g, self.r, self.unroll, self.off = r * unroll + off, r, unroll, off

    def slot(self, n):
        return self.off % n

    def turn(self, n):
        return self.r * (self.unroll // n) + self.off // n

    def early(self, n):
        return isinstance(self.g, int) and self.g < n

    def last(self, n):
        return isinstance(self.g, int) and self.g == n - 1


def skewed(eng, n, stages, unroll=4, start=0):
    lag = max(x for x, _ in stages)
    a = -(-(start + lag + unroll) // unroll) * unroll
    b = a + max(0, (start + n - 1 - a) // unroll) * unroll

    def iteration(r, off, peeled):
        for x, fn in stages:
            if not peeled or start <= off - x < start + n:
                fn(Step(r, unroll, off - x))

    for j in range(start, a):
        iteration(0, j, True)
    with eng.Fori(a // unroll, b // unroll) as r:
        for off in range(unroll):
            iteration(r, off, False)
    for j in range(b, start + n + lag):
        iteration(0, j, True)


def node_base(g):
    return N - ROWS if isinstance(g, int) and g == NG - 1 else g * ROWS


def node_rows(dram, g):
    return dram[bass.ds(node_base(g), ROWS), :].rearrange("(p k) d -> p k d", k=K4)


def edge_rows(dram, g, width=D):
    return dram[bass.ds(g * ROWS, ROWS), :].rearrange("(k p) d -> p k d", p=P)


class Core:

    def __init__(self, nc, ctx):
        self.nc, self.ctx = nc, ctx

    def sb(self, name, shape, dt=F32, ctx=None):
        t = (ctx or self.ctx).enter_context(self.nc.sbuf_tensor(name, shape, dt))
        return t

    def ps(self, name, shape, dt=F32, ctx=None):
        return (ctx or self.ctx).enter_context(self.nc.psum_tensor(name, shape, dt))

    def sem(self, name):
        self.phase_sems.append(self.nc.alloc_semaphore(name))
        return self.phase_sems[-1]

    @contextmanager
    def phase(self):
        self.phase_sems = []
        with ExitStack() as ctx:
            yield ctx
        self.nc.clear_and_free_semaphores(self.phase_sems)
        self.nc.all_engine_barrier()


def setup_phase(c, a):
    nc = c.nc
    with c.phase() as ctx:
        nat = {n: c.sb("nat_" + n, [P, 2, D], ctx=ctx) for n in ("fw2", "w1", "w2", "w3")}
        nat["fw1"] = c.sb("nat_fw1", [P, 2, BASIS], ctx=ctx)
        heads = c.sb("heads", [16, D], ctx=ctx)
        att = c.sb("att", [P, 2, 2], ctx=ctx)
        blocks = c.sb("blocks", [P, 2, 2 * H2], ctx=ctx)
        wgT = c.sb("wgT", [P, 2, D], ctx=ctx)
        b2s = c.sb("b2s", [P, 4, 2], ctx=ctx)
        tp = [c.ps(f"tp{i}", [P, 512], ctx=ctx) for i in range(4)]
        loaded, masks, blocked = c.sem("w_loaded"), c.sem("w_masks"), c.sem("w_blocks")
        turned, copied = c.sem("w_turned"), c.sem("w_copied")
        soft, soft2, base = c.sem("w_soft"), c.sem("w_soft2"), c.sem("w_base")
        init, zeroed = c.sem("w_init"), c.sem("w_zeroed")
        block = ctx.enter_context(nc.Block())
        loads = [(nat[n][:, :, :], a[n].rearrange("(c p) i -> p c i", p=P)) for n in nat]
        loads += [(c.wg[:, :, 0:D], a["W"].rearrange("(c p) i -> p c i", p=P)),
                  (heads[0:8, :], a["W_u"]), (heads[8:16, :], a["W_v"]),
                  (c.fb1[:, :], a["fb1"].rearrange("(c p) -> p c", p=P)),
                  (c.b2[:, :], a["b2"].rearrange("(c p) -> p c", p=P)),
                  (att[:, :, 0], a["att_src"].rearrange("(c h) d -> (h d) c", h=2)),
                  (att[:, :, 1], a["att_dst"].rearrange("(c h) d -> (h d) c", h=2)),
                  (c.fb2[:, :], a["fb2"].rearrange("(o d) -> o d", o=1).to_broadcast([P, D])),
                  (c.b3[:, :], a["b3"].rearrange("(o d) -> o d", o=1).to_broadcast([P, D])),
                  (c.bias[:, :], a["bias"].rearrange("(o d) -> o d", o=1).to_broadcast([P, D])),
                  (c.bias_row[0:1, 0:D], a["bias"].rearrange("(o d) -> o d", o=1)),
                  (c.bias_row[0:1, D:2 * D], a["bias"].rearrange("(o d) -> o d", o=1)),
                  (c.bu[:, :], a["b_u"].rearrange("(o d) -> o d", o=1).to_broadcast([P, H3]))]
        turns = []
        for n, to in (("fw2", c.fw2T), ("w1", c.w1T), ("w2", c.w2T), ("w3", c.w3T)):
            for i in range(2):
                turns.append(([nat[n][:, o, i * P:(i + 1) * P] for o in range(2)], P, to[:, i, :], P))
        for i in range(2):
            turns.append(([c.wg[:, o, i * P:(i + 1) * P] for o in range(2)], P, wgT[:, i, :], P))
        turns.append(([nat["fw1"][:, o, :] for o in range(2)], P, c.fw1T[:, :], BASIS))
        for i in range(2):
            turns.append(([heads[:, i * P:(i + 1) * P]], 16, c.wuv[:, i, :], P))

        @block.sync
        def _(sp):
            for to, frm in loads:
                sp.dma_start(to, frm, allow_slow_non_contiguous=True).then_inc(loaded, 16)
            sp.wait_ge(zeroed, 3)
            sp.dma_start(c.h1_dram[EP:EP + 1, :], c.zero_row[0:1, :]).then_inc(init, 16)
            sp.dma_start(c.h2_dram[EP:EP + 1, :], c.zero_row[0:1, :]).then_inc(init, 16)
            sp.dma_start(c.place_dram.rearrange("(p j) o -> p (j o)", p=125), c.absent[0:125, :]).then_inc(init, 16)
            sp.wait_ge(init, 48)

        @block.gpsimd
        def _(pool):
            pool.memset(c.ident[:, :], 0.0).then_inc(masks, 1)
            pool.memset(c.ltri[:, :], 1.0).then_inc(masks, 1)
            pool.memset(c.window[:, :], 0.0).then_inc(masks, 1)
            pool.memset(c.ones[:, :], 1.0).then_inc(masks, 1)
            pool.memset(c.first[:, :], 0.0).then_inc(masks, 1)
            pool.memset(c.end[:, :], 0.0).then_inc(masks, 1)
            pool.memset(c.zero_row[:, :], 0.0).then_inc(zeroed, 1)
            pool.memset(c.absent[:, :], EP).then_inc(zeroed, 1)
            pool.iota(c.digits_i[:, :], pattern=[[1, 256]], base=0, channel_multiplier=0).then_inc(zeroed, 1)
            pool.wait_ge(masks, 6)
            pool.affine_select(out=c.ident[:, :], in_=c.ident[:, :], compare_op=ALU.not_equal, fill=1.0,
                               base=0, pattern=[[-1, P]], channel_multiplier=1).then_inc(masks, 1)
            pool.affine_select(out=c.ltri[:, :], in_=c.ltri[:, :], compare_op=ALU.is_gt, fill=0.0,
                               base=0, pattern=[[1, P]], channel_multiplier=-1).then_inc(masks, 1)
            pool.memset(c.window[:, P:P + 1], 1.0).then_inc(masks, 1)
            pool.memset(c.first[0:1, :], 1.0).then_inc(masks, 1)
            pool.affine_select(out=c.end[:, :], in_=c.end[:, :], compare_op=ALU.not_equal, fill=1.0,
                               base=-(P - 1), pattern=[[0, 1]], channel_multiplier=1).then_inc(masks, 1)
            pool.wait_ge(masks, 11)
            pool.tensor_copy(c.identb[:, :], c.ident[:, :]).then_inc(masks, 1)

        @block.vector
        def _(dve):
            dve.memset(blocks[:, :, :], 0.0).then_inc(blocked, 1)
            dve.memset(c.consts[:, 0:1], LN_EPS).then_inc(blocked, 1)
            dve.memset(c.consts[:, 1:2], math.log(1.25)).then_inc(blocked, 1)
            dve.memset(c.consts[:, 2:3], 0.5 * math.log(NORM_SCALE)).then_inc(blocked, 1)
            dve.memset(c.consts[:, 3:4], math.pi / 2).then_inc(blocked, 1)
            dve.memset(c.consts[:, 4:5], 0.5)
            dve.memset(c.consts[:, 6:7], -NORM_EPS2 * NORM_SCALE)
            dve.memset(c.consts[:, 7:8], NORM_EPS2 * NORM_SCALE)
            dve.memset(c.consts[:, 8:9], LN_EPS ** 2)
            dve.memset(c.one_row[:, :], 1.0)
            dve.memset(c.consts[:, 5:6], 0.5 * math.log(NORM_SCALE) + math.log(0.25)).then_inc(blocked, 1)
            dve.wait_ge(zeroed, 3)
            dve.tensor_copy(c.digits[:, :], c.digits_i[:, :]).then_inc(blocked, 1)
            dve.wait_ge(loaded, 16 * len(loads))
            dve.wait_ge(blocked, 7)
            for which in range(2):
                for h in range(H2):
                    r = slice(64 * (h % 2), 64 * (h % 2) + 64)
                    dve.tensor_copy(blocks[r, h // 2, which * H2 + h:which * H2 + h + 1],
                                    att[r, h // 2, which:which + 1]).then_inc(blocked, 1)
            for n, (parts, wide, to, rows) in enumerate(turns):
                dve.wait_ge(turned, n + 1)
                dve.tensor_copy(to, tp[n % 4][0:rows, 0:wide * len(parts)]).then_inc(copied, 1)
            n = len(turns)
            for i in range(2):
                dve.wait_ge(turned, n + i + 1)
                dve.tensor_copy(c.wg[:, i, D:D + 2 * H2], tp[(n + i) % 4][:, 0:2 * H2]).then_inc(copied, 1)
            dve.tensor_scalar(b2s[:, 0, :], c.b2[:, :], 0.0, None, ALU.max).then_inc(soft2, 1)
            dve.wait_ge(soft2, 1)
            dve.wait_ge(soft, 3)
            dve.tensor_tensor(b2s[:, 0, :], b2s[:, 0, :], b2s[:, 3, :], ALU.add).then_inc(soft2, 1)
            dve.wait_ge(base, 1)
            dve.tensor_tensor(c.c0[:, :], tp[(n + 2) % 4][:, 0:D], c.b3[:, :], ALU.add).then_inc(base, 1)

        @block.scalar
        def _(act):
            act.wait_ge(loaded, 16 * len(loads))
            act.wait_ge(blocked, 6)
            act.activation(b2s[:, 1, :], c.b2[:, :], ACT.Abs).then_inc(soft, 1)
            act.wait_ge(soft, 1)
            act.activation(b2s[:, 2, :], b2s[:, 1, :], ACT.Exp, scale=-1.0).then_inc(soft, 1)
            act.wait_ge(soft, 2)
            act.activation(b2s[:, 3, :], b2s[:, 2, :], ACT.Ln, bias=c.consts[:, 4:5], scale=0.5).then_inc(soft, 1)

        @block.tensor
        def _(pe):
            pe.wait_ge(masks, 12)
            pe.wait_ge(loaded, 16 * len(loads))
            for n, (parts, wide, to, rows) in enumerate(turns):
                if n >= 4:
                    pe.wait_ge(copied, n - 3)
                for o, part in enumerate(parts):
                    last = pe.transpose(tp[n % 4][0:rows, o * wide:(o + 1) * wide], part, c.ident[0:wide, 0:wide])
                last.then_inc(turned, 1)
            n = len(turns)
            pe.wait_ge(copied, n)
            pe.wait_ge(blocked, 7 + 2 * H2)
            for i in range(2):
                for o in range(2):
                    last = pe.matmul(tp[(n + i) % 4][:, 0:2 * H2], wgT[:, o, i * P:(i + 1) * P], blocks[:, o, :],
                                     start=(o == 0), stop=(o == 1))
                last.then_inc(turned, 1)
            pe.wait_ge(soft2, 2)
            for o in range(2):
                last = pe.matmul(tp[(n + 2) % 4][:, 0:D], b2s[:, 0, o:o + 1].to_broadcast([P, P]), c.w3T[:, o, :],
                                 start=(o == 0), stop=(o == 1))
            last.then_inc(base, 1)


def payload_phase(c, a):
    nc = c.nc
    with c.phase() as ctx:
        dst = c.sb("pl_dst", [P, T], I32, ctx=ctx)
        src = c.sb("pl_src", [P, T], I32, ctx=ctx)
        w = c.sb("pl_w", [P, T], ctx=ctx)
        num = c.sb("pl_num", [P, T], I32, ctx=ctx)
        pad = c.sb("pl_pad", [P, 1], ctx=ctx)
        ready, loaded, made, numbered = c.sem("pl_ready"), c.sem("pl_loaded"), c.sem("pl_made"), c.sem("pl_numbered")
        block = ctx.enter_context(nc.Block())

        @block.sync
        def _(sp):
            sp.wait_ge(ready, 3)
            sp.dma_start(dst[0:EDGE_PARTS, :], a["dst"].rearrange("(p t) -> p t", t=T)).then_inc(loaded, 16)
            sp.dma_start(src[0:EDGE_PARTS, :], a["src"].rearrange("(p t) -> p t", t=T)).then_inc(loaded, 16)
            sp.dma_start(w[0:EDGE_PARTS, :], a["ew"].rearrange("(p t) -> p t", t=T)).then_inc(loaded, 16)

        @block.gpsimd
        def _(pool):
            pool.iota(num[:, :], pattern=[[1, T]], base=0, channel_multiplier=T).then_inc(numbered, 1)
            pool.memset(pad[:, :], float(PAD_KEY)).then_inc(numbered, 1)
            pool.wait_ge(numbered, 2)
            pool.affine_select(out=pad[:, :], in_=pad[:, :], compare_op=ALU.is_ge, fill=0.0,
                               base=-EDGE_PARTS, pattern=[[0, 1]], channel_multiplier=1).then_inc(numbered, 1)

        @block.vector
        def _(dve):
            dve.memset(dst[:, :], 0).then_inc(ready, 1)
            dve.memset(src[:, :], 0).then_inc(ready, 1)
            dve.memset(w[:, :], 0.0).then_inc(ready, 1)
            dve.wait_ge(numbered, 3)
            dve.tensor_scalar(num[:, :], num[:, :], float(E - 1), None, ALU.min).then_inc(made, 1)
            dve.wait_ge(loaded, 48)
            dve.wait_ge(made, 1)
            for table, key, other in ((c.pay_d, dst, src), (c.pay_s, src, dst)):
                dve.tensor_scalar(table[:, :, 0], key[:, :], pad[:, 0:1], None, ALU.max)
                dve.tensor_copy(table[:, :, 1], other[:, :])
                dve.tensor_copy(table[:, :, :].bitcast(F32)[:, :, 2], w[:, :])
                dve.tensor_copy(table[:, :, 3], num[:, :]).then_inc(made, 1)


def sort_pass(c, name, pay, shift, out_dram):
    nc = c.nc
    with c.phase() as ctx:
        digit_i = c.sb(name + "digit_i", [P, T], I32, ctx=ctx)
        digit = c.sb(name + "digit", [P, T], ctx=ctx)
        hot = c.sb(name + "hot", [P, 2 * K4, 256], BF16, ctx=ctx)
        junk = c.sb(name + "junk", [P, 2 * K4, 256], BF16, ctx=ctx)
        counts = c.sb(name + "counts", [P, 2, 256], BF16, ctx=ctx)
        zeros = c.sb(name + "zeros", [P, 256], ctx=ctx)
        total = c.sb(name + "total", [P, 256], ctx=ctx)
        base = c.sb(name + "base", [P, 256], ctx=ctx)
        ahead = c.sb(name + "ahead", [P, 2, 256], ctx=ctx)
        ahead_hi = c.sb(name + "ahead_hi", [P, 2, 256], BF16, ctx=ctx)
        ahead_lo = c.sb(name + "ahead_lo", [P, 2, 256], BF16, ctx=ctx)
        place = c.sb(name + "place", [P, 2, K4], ctx=ctx)
        at = c.sb(name + "at", [P, 2, K4], I32, ctx=ctx)
        rows = c.sb(name + "rows", [P, 2, K4, 4], I32, ctx=ctx)
        tab = c.ps(name + "tab", [P, 2, 512], ctx=ctx)
        rank = c.ps(name + "rank", [P, 2 * K4, 256], ctx=ctx)
        digits_ready, hot_made, hot_counted = c.sem(name + "digits"), c.sem(name + "hot_made"), c.sem(name + "hot_counted")
        tables = c.sem(name + "tables")
        sums, heads, ranked, read = c.sem(name + "sums"), c.sem(name + "heads"), c.sem(name + "ranked"), c.sem(name + "read")
        placed, copied, back = c.sem(name + "placed"), c.sem(name + "copied"), c.sem(name + "back")
        issuing = c.sem(name + "issuing")
        hot2, sent = c.sem(name + "hot2"), [c.sem(f"{name}sent{u}") for u in range(2)]
        block = ctx.enter_context(nc.Block())

        def make_hot(dve, t, made):
            for k in range(K4):
                last = dve.tensor_scalar(hot[:, t.slot(2) * K4 + k, :], c.digits[:, :], digit[:, bass.ds(t.g * K4 + k, 1)],
                                         None, ALU.is_equal)
            last.then_inc(made, 1)

        @block.vector
        def _(dve):
            dve.memset(zeros[:, :], 0.0).then_inc(digits_ready, 1)
            dve.tensor_scalar(digit_i[:, :], pay[:, :, 0], shift, 255, ALU.logical_shift_right, ALU.bitwise_and)\
               .then_inc(digits_ready, 1)
            dve.wait_ge(digits_ready, 2)
            dve.tensor_copy(digit[:, :], digit_i[:, :]).then_inc(digits_ready, 1)
            dve.wait_ge(digits_ready, 3)

            def count(t):
                if not t.early(2):
                    dve.wait_ge(hot_counted, t.g - 1)
                make_hot(dve, t, hot_made)
            for start, n in HALVES:
                skewed(dve, n, [(0, count)], 2, start)
            dve.wait_ge(tables, 1)
            dve.tensor_copy(counts[:, :, :], tab[:, :, 0:256]).then_inc(tables, 1)
            dve.wait_ge(sums, 1)
            dve.tensor_copy(total[:, :], rank[:, 0, :]).then_inc(heads, 1)
            dve.wait_ge(heads, 1)
            dve.tensor_tensor_scan(base[:, :], total[:, :], zeros[:, :], 0.0, ALU.add, ALU.add).then_inc(heads, 1)
            dve.wait_ge(heads, 2)
            dve.tensor_tensor(base[:, :], base[:, :], total[:, :], ALU.subtract).then_inc(heads, 1)
            dve.wait_ge(heads, 3)
            dve.wait_ge(sums, 2)
            for h in range(2):
                dve.tensor_tensor(ahead[:, h, :], rank[:, 2 + 2 * h, :], base[:, :], ALU.add).then_inc(heads, 1)
            dve.wait_ge(heads, 5)
            dve.tensor_copy(ahead_hi[:, :, :], ahead[:, :, :]).then_inc(heads, 1)
            dve.wait_ge(heads, 6)
            dve.tensor_tensor(ahead_lo[:, :, :], ahead[:, :, :], ahead_hi[:, :, :], ALU.subtract).then_inc(heads, 1)

            def mark(t):
                if not t.early(2):
                    dve.wait_ge(read, t.g - 1)
                make_hot(dve, t, hot2)

            def positions(t):
                u = t.slot(2)
                dve.wait_ge(ranked, t.g + 1)
                for k in range(K4):
                    last = dve.scalar_tensor_tensor(
                        out=junk[:, u * K4 + k, :], in0=hot[:, u * K4 + k, :], scalar=1.0, in1=rank[:, u * K4 + k, :],
                        op0=ALU.mult, op1=ALU.mult, accum_out=place[:, u, k:k + 1])
                last.then_inc(read, 1)
                dve.wait_ge(read, t.g + 1)
                if not t.early(2):
                    dve.wait_ge(sent[u], t.turn(2) * 16 * K4)
                dve.tensor_copy(at[:, u, :], place[:, u, :]).then_inc(placed, 1)
            dve.wait_ge(hot_counted, GROUPS)
            skewed(dve, GROUPS, [(0, mark), (1, positions)], 2)

        @block.tensor
        def _(pe):
            for h, (start, n) in enumerate(HALVES):
                pe.matmul(tab[:, h, 0:256], c.window[:, 0:P], c.window[:, 0:256], start=True, stop=False)

                def count(t):
                    pe.wait_ge(hot_made, t.g + 1)
                    for k in range(K4):
                        last = pe.matmul(tab[:, h, 0:256], c.window[:, bass.ds((t.g - start) * (-K4) + P - k, P)],
                                         hot[:, t.slot(2) * K4 + k, :], start=False, stop=False)
                    last.then_inc(hot_counted, 1)
                skewed(pe, n, [(0, count)], 2, start)
                last = pe.matmul(tab[:, h, 0:256], c.window[:, 0:P], c.window[:, 0:256], start=False, stop=True)
            last.then_inc(tables, 1)
            pe.wait_ge(tables, 2)
            for h in range(2):
                last = pe.matmul(rank[:, 0, :], c.ones[:, :], counts[:, h, :], start=(h == 0), stop=(h == 1))
            last.then_inc(sums, 1)
            pe.matmul(rank[:, 2, :], c.ltri[:, :], counts[:, 0, :], start=True, stop=True)
            pe.matmul(rank[:, 4, :], c.ltri[:, :], counts[:, 1, :], start=True, stop=False)
            pe.matmul(rank[:, 4, :], c.ones[:, :], counts[:, 0, :], start=False, stop=True).then_inc(sums, 1)
            pe.wait_ge(heads, 7)
            for h, (start, n) in enumerate(HALVES):
                def rank_step(t):
                    pe.wait_ge(hot2, t.g + 1)
                    if not t.early(2):
                        pe.wait_ge(read, t.g - 1)
                    for k in range(K4):
                        out = rank[:, t.slot(2) * K4 + k, :]
                        pick = c.identb[:, bass.ds((t.g - start) * K4 + k, 1)].to_broadcast([P, P])
                        pe.matmul(out, c.ltri[:, :], hot[:, t.slot(2) * K4 + k, :], start=True, stop=False)
                        pe.matmul(out, pick, ahead_hi[:, h, :], start=False, stop=False)
                        last = pe.matmul(out, pick, ahead_lo[:, h, :], start=False, stop=True)
                    last.then_inc(ranked, 1)
                skewed(pe, n, [(0, rank_step)], 2, start)

        @block.gpsimd
        def _(pool):
            def send(t):
                u = t.slot(2)
                if not t.early(2):
                    pool.wait_ge(sent[u], t.turn(2) * 16 * K4)
                    pool.sem_inc(issuing, 1)
                pool.tensor_copy(rows[:, u, :, :], pay[:, bass.ds(t.g * K4, K4), :]).then_inc(copied, 1)
                pool.wait_ge(copied, t.g + 1)
                pool.wait_ge(placed, t.g + 1)
                pool.sem_inc(issuing, 1)
                for k in range(K4):
                    pool.indirect_dma_start(out_dram[:, :], bass.IndirectOffsetOnAxis(ap=at[:, u, k:k + 1], axis=0),
                                            rows[:, u, k, :], None).then_inc(sent[u], 16)
            skewed(pool, GROUPS, [(0, send)], 2)

        @block.sync
        def _(sp):
            for u in range(2):
                sp.wait_ge(sent[u], GROUPS // 2 * 16 * K4)
            sp.dma_start(pay[:, :, :], out_dram.rearrange("(t p) c -> p t c", p=P)).then_inc(back, 16)
            sp.wait_ge(back, 16)


def index_phase(c, name, side):
    nc = c.nc
    pay, key, keys_dram = side["pay"], side["key"], side["keys"]
    with c.phase() as ctx:
        keyT = c.sb(name + "keyT", [P, 2, P], ctx=ctx)
        nextT = c.sb(name + "nextT", [P, 2, P], ctx=ctx)
        sentinels = c.sb(name + "sentinels", [1, 2], ctx=ctx)
        turn = c.ps(name + "turn", [P, 2, 512], ctx=ctx)
        turn2 = c.ps(name + "turn2", [P, 2, 512], ctx=ctx)
        keyed, turned, keyedT, stored = c.sem(name + "keyed"), c.sem(name + "turned"), c.sem(name + "keyedT"), c.sem(name + "stored")
        cuts = c.sb(name + "cuts", [P, 2, P], ctx=ctx)
        loaded, marked, back = c.sem(name + "loaded"), c.sem(name + "marked"), c.sem(name + "ix_back")
        block = ctx.enter_context(nc.Block())
        half = T // 2

        @block.vector
        def _(dve):
            dve.memset(sentinels[0:1, 0:1], -1.0).then_inc(keyed, 1)
            dve.memset(sentinels[0:1, 1:2], -2.0).then_inc(keyed, 1)
            dve.memset(key[:, 0:1], -1.0).then_inc(keyed, 1)
            dve.tensor_copy(key[:, 1:T + 1], pay[:, :, 0]).then_inc(keyed, 1)
            for kind, (col, top) in enumerate(side["columns"]):
                dve.tensor_scalar(side["index"][:, :, kind, :], pay[:, :, col].rearrange("p (g k) -> p g k", k=K4),
                                  float(top), None, ALU.min)
            dve.wait_ge(keyed, 4)
            dve.tensor_scalar(side["key_end"][:, :], key[:, 0:T], 3.0, c.end[:, 0:1], ALU.add, ALU.mult).then_inc(keyed, 1)
            dve.wait_ge(keyed, 5)
            dve.tensor_scalar(side["key_end"][:, :], side["key_end"][:, :], 3.0, None, ALU.subtract)
            dve.tensor_copy(side["w"][:, :], pay[:, :, :].bitcast(F32)[:, :, 2])
            dve.tensor_scalar(side["w8"][:, :], pay[:, :, :].bitcast(F32)[:, :, 2], 0.8, None, ALU.mult)
            dve.wait_ge(turned, 1)
            dve.tensor_copy(keyT[0:half, :, :], turn[0:half, :, 0:P]).then_inc(keyedT, 1)
            dve.wait_ge(loaded, 16)
            dve.tensor_tensor(nextT[0:half, :, :], nextT[0:half, :, :], keyT[0:half, :, :], ALU.is_equal).then_inc(marked, 1)
            dve.wait_ge(marked, 1)
            dve.tensor_scalar(cuts[0:half, :, :], nextT[0:half, :, :], -LOW, LOW, ALU.mult, ALU.add).then_inc(marked, 1)
            dve.wait_ge(marked, 2)
            dve.scalar_tensor_tensor(out=nextT[0:half, :, :], in0=nextT[0:half, :, :], scalar=FAR, in1=keyT[0:half, :, :],
                                     op0=ALU.mult, op1=ALU.add).then_inc(marked, 1)
            dve.wait_ge(back, 1)
            for h in range(2):
                dve.tensor_copy(side["index"][:, h * GROUPS // 2:(h + 1) * GROUPS // 2, LAST, :],
                                turn2[:, h, 0:half].rearrange("p (g k) -> p g k", k=K4))

        @block.tensor
        def _(pe):
            pe.wait_ge(keyed, 4)
            for h in range(2):
                last = pe.transpose(turn[0:half, h, 0:P], key[:, 1 + h * half:1 + (h + 1) * half], c.ident[:, :])
            last.then_inc(turned, 1)
            pe.wait_ge(marked, 3)
            for h in range(2):
                last = pe.transpose(turn2[:, h, 0:half], nextT[0:half, h, :], c.ident[0:half, 0:half])
            last.then_inc(back, 1)

        @block.sync
        def _(sp):
            sp.wait_ge(keyedT, 1)
            sp.dma_start(keys_dram[1:EP + 1].rearrange("(h t p) -> t h p", h=2, p=P), keyT[0:half, :, :]).then_inc(stored, 16)
            sp.dma_start(keys_dram[0:1].rearrange("(o n) -> o n", o=1), sentinels[0:1, 0:1]).then_inc(stored, 16)
            sp.dma_start(keys_dram[EP + 1:EP + 2].rearrange("(o n) -> o n", o=1), sentinels[0:1, 1:2]).then_inc(stored, 16)
            sp.wait_ge(stored, 48)
            sp.dma_start(nextT[0:half, :, :], keys_dram[2:EP + 2].rearrange("(h t p) -> t h p", h=2, p=P)).then_inc(loaded, 16)
            sp.wait_ge(marked, 2)
            sp.dma_start(side["cuts"][1:EP + 1].rearrange("(h t p) -> t h p", h=2, p=P), cuts[0:half, :, :]).then_inc(stored, 16)
            sp.dma_start(side["cuts"][0:1].rearrange("(o n) -> o n", o=1), sentinels[0:1, 0:1]).then_inc(stored, 16)
            sp.wait_ge(stored, 80)


def signals(c, prefix):
    made = {}

    def get(name):
        if name not in made:
            made[name] = c.sem(prefix + name)
        return made[name]
    return get


def over_tiles(row):
    return row.rearrange("p (o d) -> p o d", o=1).to_broadcast([row.shape[0], K4, row.shape[1]])


def along(col):
    return col.rearrange("p (k o) -> p k o", o=1).to_broadcast([col.shape[0], K4, P])


def row_stats(dve, x, stats, mv, s, what, g):
    for k in range(K4):
        last = dve.bn_stats(stats[:, k, :], x[:, k, :])
    last.then_inc(s(what + "_stats"), 1)
    dve.wait_ge(s(what + "_stats"), g + 1)
    dve.sem_inc(s(what + "_held"), 1)
    for k in range(K4):
        last = dve.bn_aggr(mv[:, k, :], stats[:, k, :])
    last.then_inc(s(what + "_var"), 1)


def row_scale(act, c, mv, rs, s, what, g, bias=0.0):
    act.wait_ge(s(what + "_var"), g + 1)
    act.activation(rs, mv[:, :, 1], ACT.Ln, bias=c.consts[:, 0:1]).then_inc(s(what + "_log"), 1)
    act.wait_ge(s(what + "_log"), g + 1)
    act.activation(rs, rs, ACT.Exp, bias=bias, scale=-0.5).then_inc(s(what + "_scale"), 1)


def row_apply(dve, out, x, mv, rs, s, what, g, done):
    dve.wait_ge(s(what + "_scale"), g + 1)
    for k in range(K4):
        last = dve.tensor_scalar(out[:, k, :], x[:, k, :], mv[:, k, 0:1], rs[:, k:k + 1], ALU.subtract, ALU.mult)
    last.then_inc(s(done), 1)


def inverse_norm(act, c, ss, rn, s, g, bias):
    act.activation(rn, ss, ACT.Relu, scale=NORM_SCALE, bias=c.consts[:, 6:7]).then_inc(s("rn_guard"), 1)
    act.wait_ge(s("rn_guard"), g + 1)
    act.activation(rn, rn, ACT.Ln, bias=c.consts[:, 7:8]).then_inc(s("rn_log"), 1)
    act.wait_ge(s("rn_log"), g + 1)
    act.activation(rn, rn, ACT.Exp, scale=-0.5, bias=bias).then_inc(s("rn"), 1)


def node_pass_one(c, a):
    nc = c.nc
    with c.phase() as ctx:
        x = c.sb("n1_x", [P, 4, K4, D], ctx=ctx)
        y = c.sb("n1_y", [P, 4, K4, D], ctx=ctx)
        stats, mv, rs = (c.sb("n1_" + n, [P, 2, K4] + m, ctx=ctx) for n, m in (("stats", [6]), ("mv", [2]), ("rs", [])))
        s = signals(c, "n1_")
        loaded, stored = ([s(f"{n}{u}") for u in range(4)] for n in ("loaded", "stored"))
        block = ctx.enter_context(nc.Block())

        @block.sync
        def _(sp):
            def load(t):
                if not t.early(4):
                    sp.wait_ge(s("y_done"), t.g - 3)
                sp.dma_start(x[:, t.slot(4), :, :], node_rows(a["x"], t.g)).then_inc(loaded[t.slot(4)], 16)

            def store(t):
                sp.wait_ge(s("y_done"), t.g + 1)
                if t.last(NG):
                    sp.wait_ge(stored[(NG - 2) % 4], 16 * ((NG - 2) // 4 + 1))
                sp.dma_start(node_rows(c.a_dram, t.g), y[:, t.slot(4), :, :]).then_inc(stored[t.slot(4)], 16)
            skewed(sp, NG, [(0, load), (3, store)])
            for u in range(4):
                sp.wait_ge(stored[u], 16 * len(range(u, NG, 4)))

        @block.gpsimd
        def _(pool):
            def shift(t):
                pool.wait_ge(loaded[t.slot(4)], 16 * (t.turn(4) + 1))
                pool.tensor_tensor(x[:, t.slot(4), :, :], x[:, t.slot(4), :, :], over_tiles(c.c0[:, :]), ALU.add)\
                    .then_inc(s("shifted"), 1)
            skewed(pool, NG, [(0, shift)])

        @block.vector
        def _(dve):
            def measure(t):
                dve.wait_ge(s("shifted"), t.g + 1)
                row_stats(dve, x[:, t.slot(4)], stats[:, t.slot(2)], mv[:, t.slot(2)], s, "x", t.g)

            def apply(t):
                if not t.early(4):
                    dve.wait_ge(stored[t.slot(4)], 16 * t.turn(4))
                row_apply(dve, y[:, t.slot(4)], x[:, t.slot(4)], mv[:, t.slot(2)], rs[:, t.slot(2)], s, "x", t.g, "y_done")
            skewed(dve, NG, [(0, measure), (1, apply)])

        @block.scalar
        def _(act):
            skewed(act, NG, [(0, lambda t: row_scale(act, c, mv[:, t.slot(2)], rs[:, t.slot(2), :], s, "x", t.g,
                                                     c.consts[:, 1:2]))])


def cosine_phase(c):
    nc = c.nc
    with c.phase() as ctx:
        half = c.sb("co_half", [P, T], ctx=ctx)
        s = signals(c, "co_")
        block = ctx.enter_context(nc.Block())
        rounder = 1.5 * 2.0 ** 23
        w = c.d["w"]

        @block.vector
        def _(dve):
            dve.tensor_scalar(half[:, :], w[:, :], 0.5, rounder, ALU.mult, ALU.add).then_inc(s("step"), 1)
            dve.wait_ge(s("step"), 1)
            dve.tensor_scalar(half[:, :], half[:, :], rounder, -2.0, ALU.subtract, ALU.mult).then_inc(s("step"), 1)
            dve.wait_ge(s("step"), 2)
            dve.tensor_tensor(half[:, :], half[:, :], w[:, :], ALU.add).then_inc(s("reduced"), 1)
            dve.wait_ge(s("sine"), 1)
            dve.tensor_scalar(c.cutoff[:, :], half[:, :], 1.0, 0.25, ALU.add, ALU.mult)

        @block.scalar
        def _(act):
            act.wait_ge(s("reduced"), 1)
            act.activation(half[:, :], half[:, :], ACT.Abs).then_inc(s("abs"), 1)
            act.wait_ge(s("abs"), 1)
            act.activation(half[:, :], half[:, :], ACT.Sin, bias=c.consts[:, 3:4], scale=-math.pi).then_inc(s("sine"), 1)


def load_keys(sp, dram, to, t, lo, n, slots, used, keyed, parts=P):
    if not t.early(slots):
        sp.wait_ge(used, t.g - (slots - 1))
    sp.dma_start(to, dram[bass.ds(t.g * ROWS + lo, n)].rearrange("(o n) -> o n", o=1).to_broadcast([parts, n]))\
      .then_inc(keyed[t.slot(slots)], 16)


def filter_layer(c, a):
    nc = c.nc
    side = c.d
    with c.phase() as ctx:
        sb = lambda n, shape, dt=F32: c.sb("l0_" + n, shape, dt, ctx=ctx)
        xs, xd = sb("xs", [P, 2, K4, D]), sb("xd", [P, 4, K4, D])
        ea, keys = sb("ea", [P, 2, K4, BASIS]), sb("keys", [P, 2, ROWS + 1])
        at = sb("at", [P, 4, 4, K4], I32)
        eaT, xsT = sb("eaT", [BASIS, ROWS]), sb("xsT", [P, 2, ROWS])
        pre, log, soft = (sb(n, [P, 2, 2, ROWS]) for n in ("pre", "log", "soft"))
        filt, msg = sb("filt", [P, K4, D]), sb("msg", [P, K4, D])
        same, cont = sb("same", [P, 2, K4, P]), sb("cont", [P, 2, K4, P])
        agg, y = sb("agg", [P, 2, ROWS]), sb("y", [P, 4, K4, D])
        stats, mv, rs = sb("stats", [P, K4, 6]), sb("mv", [P, K4, 2]), sb("rs", [P, K4])
        ps_x, ps_z, ps_o, ps_a = (c.ps("l0_p" + n, [P, 2, 512], ctx=ctx) for n in "xzoa")
        tiles_of = lambda p: p[:, :, :].rearrange("p b (j d) -> p (b j) d", d=D)
        s = signals(c, "l0_")
        got_s, got_e, keyed = ([s(f"{n}{u}") for u in range(2)] for n in ("got_s", "got_e", "keyed"))
        got_d, sent = ([s(f"{n}{u}") for u in range(4)] for n in ("got_d", "sent"))
        block = ctx.enter_context(nc.Block())

        @block.gpsimd
        def _(pool):
            def gather(t):
                u, v = t.slot(2), t.slot(4)
                if not t.early(2):
                    pool.wait_ge(s("xsT"), t.g - 1)
                    pool.wait_ge(s("eaT"), t.g - 1)
                if not t.early(4):
                    pool.wait_ge(sent[v], t.turn(4) * 16 * K4)
                    pool.wait_ge(s("summed"), t.g - 3)
                    pool.sem_inc(s("issuing"), 1)
                pool.tensor_copy(at[:, v, :, :], side["index"][:, bass.ds(t.g, 1), :, :].rearrange("p o n k -> p (o n) k"))\
                    .then_inc(s("at"), 1)
                pool.wait_ge(s("at"), t.g + 1)
                pool.sem_inc(s("issuing"), 1)
                for to, frm, kind, got in ((ea[:, u], a["ea"], EDGE, got_e[u]), (xs[:, u], a["x"], OTHER, got_s[u]),
                                           (xd[:, v], a["x"], OWN, got_d[v])):
                    for k in range(K4):
                        pool.indirect_dma_start(to[:, k, :], None, frm[:, :],
                                                bass.IndirectOffsetOnAxis(ap=at[:, v, kind, k:k + 1], axis=0)).then_inc(got, 16)

            def scatter(t):
                v = t.slot(4)
                pool.wait_ge(s("y_done"), t.g + 1)
                pool.sem_inc(s("issuing"), 1)
                for k in range(K4):
                    pool.indirect_dma_start(c.a_dram[:, :], bass.IndirectOffsetOnAxis(ap=at[:, v, LAST, k:k + 1], axis=0),
                                            y[:, v, k, :], None, bounds_check=N - 1, oob_is_err=False).then_inc(sent[v], 16)
            skewed(pool, GROUPS, [(0, gather), (3, scatter)])
            for v in range(4):
                pool.wait_ge(sent[v], len(range(v, GROUPS, 4)) * 16 * K4)

        @block.sync
        def _(sp):
            skewed(sp, GROUPS, [(0, lambda t: load_keys(sp, side["keys"], keys[:, t.slot(2), :], t, 0, ROWS + 1, 2,
                                                        s("masked"), keyed))])

        @block.tensor
        def _(pe):
            def turn(t):
                u = t.slot(2)
                pe.wait_ge(got_e[u], (t.turn(2) + 1) * 16 * K4)
                pe.wait_ge(s("filt"), t.g)
                pe.sem_inc(s("held"), 1)
                for k in range(K4):
                    last = pe.transpose(ps_z[0:BASIS, 0, k * P:(k + 1) * P], ea[:, u, k, :], c.ident[:, :])
                last.then_inc(s("eaT"), 1)
                pe.wait_ge(got_s[u], (t.turn(2) + 1) * 16 * K4)
                pe.wait_ge(s("msg"), t.g)
                for f in range(2):
                    for k in range(K4):
                        last = pe.transpose(ps_x[:, f, k * P:(k + 1) * P], xs[:, u, k, f * P:(f + 1) * P], c.ident[:, :])
                last.then_inc(s("xsT"), 1)
                pe.wait_ge(s("eaT_sb"), t.g + 1)
                for f in range(2):
                    last = pe.matmul(ps_z[:, f, :], c.fw1T[:, f * P:(f + 1) * P], eaT[:, :], start=True, stop=True)
                last.then_inc(s("hidden"), 1)

            def first_out(t):
                pe.wait_ge(s("agg"), (t.g + 1) * K4)
                pe.wait_ge(s("pre1"), t.g)
                for o in range(2):
                    for f in range(2):
                        last = pe.matmul(ps_o[:, o, :], c.w2T[:, f, o * P:(o + 1) * P], agg[:, f, :],
                                         start=(f == 0), stop=(f == 1))
                last.then_inc(s("o1"), 1)

            def messages(t):
                pe.wait_ge(s("xsT_sb"), t.g + 1)
                for k in range(K4):
                    for f in range(2):
                        last = pe.matmul(tiles_of(ps_x)[:, k, :], xsT[:, f, k * P:(k + 1) * P], c.w1T[:, f, :],
                                         start=(f == 0), stop=(f == 1))
                last.then_inc(s("h"), 1)
                pe.wait_ge(s("soft0"), t.g + 1)
                for k in range(K4):
                    for f in range(2):
                        last = pe.matmul(tiles_of(ps_z)[:, k, :], soft[:, 0, f, k * P:(k + 1) * P], c.fw2T[:, f, :],
                                         start=(f == 0), stop=(f == 1))
                last.then_inc(s("filter"), 1)

            def second_out(t):
                pe.wait_ge(s("soft1"), t.g + 1)
                for k in range(K4):
                    for o in range(2):
                        last = pe.matmul(tiles_of(ps_a)[:, k, :], soft[:, 1, o, k * P:(k + 1) * P], c.w3T[:, o, :],
                                         start=(o == 0), stop=(o == 1))
                last.then_inc(s("o2"), 1)

            def runs(t):
                pe.wait_ge(s("msg"), t.g + 1)
                pe.wait_ge(s("masked"), t.g + 1)
                pe.wait_ge(s("summed"), t.g)
                for f in range(2):
                    for k in range(K4):
                        last = pe.matmul(ps_a[:, f, k * P:(k + 1) * P], msg[:, k, f * P:(f + 1) * P], same[:, t.slot(2), k, :],
                                         start=True, stop=True)
                last.then_inc(s("runs"), 1)
            skewed(pe, GROUPS, [(0, turn), (1, first_out), (0, messages), (1, second_out), (0, runs)])

        @block.scalar
        def _(act):
            def copies(t):
                act.wait_ge(s("eaT"), t.g + 1)
                act.activation(eaT[:, :], ps_z[0:BASIS, 0, :], ACT.Copy).then_inc(s("eaT_sb"), 1)
                act.wait_ge(s("xsT"), t.g + 1)
                act.wait_ge(s("h"), t.g)
                act.activation(xsT[:, :, :], ps_x[:, :, :], ACT.Copy).then_inc(s("xsT_sb"), 1)

            def softplus(t, n, ps, ready, bias):
                act.wait_ge(s(ready), t.g + 1)
                act.wait_ge(s(f"soft{n}"), t.g)
                for f in range(2):
                    last = act.activation(pre[:, n, f, :], ps[:, f, :], ACT.Identity, bias=bias[:, f:f + 1])
                last.then_inc(s(f"pre{n}"), 1)
                act.wait_ge(s(f"pre{n}"), t.g + 1)
                act.activation(log[:, n, :, :], pre[:, n, :, :], ACT.Abs).then_inc(s(f"abs{n}"), 1)
                act.wait_ge(s(f"abs{n}"), t.g + 1)
                act.activation(log[:, n, :, :], log[:, n, :, :], ACT.Exp, scale=-1.0).then_inc(s(f"exp{n}"), 1)
                act.wait_ge(s(f"exp{n}"), t.g + 1)
                act.activation(log[:, n, :, :], log[:, n, :, :], ACT.Ln, bias=c.consts[:, 4:5], scale=0.5).then_inc(s(f"log{n}"), 1)
            skewed(act, GROUPS, [(0, copies), (0, lambda t: softplus(t, 0, ps_z, "hidden", c.fb1)),
                                 (1, lambda t: softplus(t, 1, ps_o, "o1", c.b2)),
                                 (1, lambda t: row_scale(act, c, mv, rs[:, :], s, "x", t.g, c.consts[:, 1:2]))])

        @block.vector
        def _(dve):
            dve.memset(agg[:, :, :], 0.0).then_inc(s("agg_clear"), 1)

            def softplus(t, n, used):
                dve.wait_ge(s(f"log{n}"), t.g + 1)
                dve.wait_ge(s(used), t.g)
                dve.scalar_tensor_tensor(out=soft[:, n, :, :], in0=pre[:, n, :, :], scalar=0.0, in1=log[:, n, :, :],
                                         op0=ALU.max, op1=ALU.add).then_inc(s(f"soft{n}"), 1)

            def carry_on(t):
                dve.wait_ge(s("runs"), t.g + 1)
                dve.wait_ge(s("o1"), t.g)
                for k in range(K4):
                    if t.early(1) and k == 0:
                        dve.wait_ge(s("agg_clear"), 1)
                    else:
                        dve.wait_ge(s("agg"), t.g * K4 + k)
                    before = (k * P - 1) % ROWS
                    for f in range(2):
                        last = dve.scalar_tensor_tensor(
                            out=agg[:, f, k * P:(k + 1) * P], in0=cont[:, t.slot(2), k, :], scalar=agg[:, f, before:before + 1],
                            in1=ps_a[:, f, k * P:(k + 1) * P], op0=ALU.mult, op1=ALU.add)
                    last.then_inc(s("agg"), 1)

            def masks(t):
                u = t.slot(2)
                dve.wait_ge(keyed[u], 16 * (t.turn(2) + 1))
                if not t.early(2):
                    dve.wait_ge(s("runs"), t.g - 1)
                rows = keys[:, u, 1:ROWS + 1].rearrange("p (k j) -> p k j", k=K4)
                dve.tensor_tensor(same[:, u, :, :], rows, along(side["key"][:, bass.ds(t.g * K4 + 1, K4)]), ALU.is_equal)
                dve.tensor_tensor(cont[:, u, :, :], rows, along(keys[:, u, 0:ROWS:P]), ALU.is_equal).then_inc(s("masked"), 1)

            def messages(t):
                dve.wait_ge(s("filter"), t.g + 1)
                dve.tensor_tensor(filt[:, :, :], tiles_of(ps_z), over_tiles(c.fb2[:, :]), ALU.add).then_inc(s("filt"), 1)
                dve.wait_ge(s("filt"), t.g + 1)
                dve.wait_ge(s("h"), t.g + 1)
                dve.wait_ge(s("runs"), t.g)
                for k in range(K4):
                    last = dve.scalar_tensor_tensor(out=msg[:, k, :], in0=filt[:, k, :], scalar=c.cutoff[:, bass.ds(t.g * K4 + k, 1)],
                                                    in1=tiles_of(ps_x)[:, k, :], op0=ALU.mult, op1=ALU.mult)
                last.then_inc(s("msg"), 1)

            def add_bias(t):
                v = t.slot(4)
                dve.wait_ge(got_d[v], (t.turn(4) + 1) * 16 * K4)
                dve.tensor_tensor(xd[:, v, :, :], xd[:, v, :, :], over_tiles(c.b3[:, :]), ALU.add).then_inc(s("xd"), 1)

            def finish(t):
                v = t.slot(4)
                dve.wait_ge(s("xd"), t.g + 1)
                dve.wait_ge(s("o2"), t.g + 1)
                if not t.early(4):
                    dve.wait_ge(sent[v], t.turn(4) * 16 * K4)
                dve.tensor_tensor(y[:, v, :, :], tiles_of(ps_a), xd[:, v, :, :], ALU.add).then_inc(s("summed"), 1)
                dve.wait_ge(s("summed"), t.g + 1)
                row_stats(dve, y[:, v], stats, mv, s, "x", t.g)
                row_apply(dve, y[:, v], y[:, v], mv, rs, s, "x", t.g, "y_done")
            skewed(dve, GROUPS, [(1, carry_on), (0, masks), (0, add_bias), (0, lambda t: softplus(t, 0, "filter")),
                                 (1, lambda t: softplus(t, 1, "o2")), (0, messages), (1, finish)])


def place_phase(c):
    nc = c.nc
    side = c.s
    with c.phase() as ctx:
        pos = c.sb("pp_pos", [P, GROUPS, K4], I32, ctx=ctx)
        at, row = c.sb("pp_at", [P, 4, K4], I32, ctx=ctx), c.sb("pp_row", [P, 4, K4], I32, ctx=ctx)
        s = signals(c, "pp_")
        moved = [s(f"moved{u}") for u in range(4)]
        got = [s(f"got{u}") for u in range(4)]
        block = ctx.enter_context(nc.Block())

        @block.gpsimd
        def _(pool):
            pool.iota(pos[:, :, :], pattern=[[ROWS, GROUPS], [P, K4]], base=0, channel_multiplier=1).then_inc(s("pos"), 1)
            pool.wait_ge(s("pos"), 1)

            def send(t):
                u = t.slot(4)
                if not t.early(4):
                    pool.wait_ge(moved[u], t.turn(4) * 16 * K4)
                    pool.sem_inc(s("issuing"), 1)
                pool.tensor_copy(at[:, u, :], side["index"][:, bass.ds(t.g, 1), LAST, :].rearrange("p o k -> p (o k)"))\
                    .then_inc(s("at"), 1)
                pool.tensor_copy(row[:, u, :], pos[:, bass.ds(t.g, 1), :].rearrange("p o k -> p (o k)")).then_inc(s("at"), 1)
                pool.wait_ge(s("at"), t.g * 2 + 2)
                pool.sem_inc(s("issuing"), 1)
                for k in range(K4):
                    pool.indirect_dma_start(c.place_dram[:, :], bass.IndirectOffsetOnAxis(ap=at[:, u, k:k + 1], axis=0),
                                            row[:, u, k:k + 1], None, bounds_check=N - 1, oob_is_err=False).then_inc(moved[u], 16)
            skewed(pool, GROUPS, [(0, send)])
            for u in range(4):
                pool.wait_ge(moved[u], len(range(u, GROUPS, 4)) * 16 * K4)

            def look(t):
                u = t.slot(4)
                if not t.early(4):
                    pool.wait_ge(s("kept"), t.g - 3)
                    pool.sem_inc(s("issuing"), 1)
                pool.tensor_copy(at[:, u, :], side["index"][:, bass.ds(t.g, 1), OTHER, :].rearrange("p o k -> p (o k)"))\
                    .then_inc(s("at2"), 1)
                pool.wait_ge(s("at2"), t.g + 1)
                pool.sem_inc(s("issuing"), 1)
                for k in range(K4):
                    pool.indirect_dma_start(row[:, u, k:k + 1], None, c.place_dram[:, :],
                                            bass.IndirectOffsetOnAxis(ap=at[:, u, k:k + 1], axis=0)).then_inc(got[u], 16)

            def keep(t):
                u = t.slot(4)
                pool.wait_ge(got[u], (t.turn(4) + 1) * 16 * K4)
                pool.sem_inc(s("issuing"), 1)
                pool.tensor_copy(c.s_place[:, bass.ds(t.g, 1), :].rearrange("p o k -> p (o k)"), row[:, u, :]).then_inc(s("kept"), 1)
            skewed(pool, GROUPS, [(2, keep), (0, look)])


def propagation_round(c, n):
    nc = c.nc
    side = c.s
    table = (c.a_dram, c.h1_dram, c.h2_dram)[n - 1]
    weight = side["w8"] if n == 1 else side["w"]
    with c.phase() as ctx:
        pre = f"l1{n}_"
        sb = lambda m, shape, dt=F32: c.sb(pre + m, shape, dt, ctx=ctx)
        x, keys, at = sb("x", [P, 4, K4, D]), sb("keys", [P, 2, ROWS]), sb("at", [P, 4, 2, K4], I32)
        same, cont = sb("same", [P, 4, K4, P]), sb("cont", [P, 4, K4, P])
        total, h, square = sb("total", [P, 4, K4, D]), sb("h", [P, 4, K4, D]), sb("square", [P, K4, D])
        ss, rn = sb("ss", [P, 2, K4]), sb("rn", [P, 2, K4])
        old = sb("old", [P, 2, 2, K4, D]) if n == 3 else None
        acc = c.ps(pre + "acc", [P, 2 * K4, 512], ctx=ctx)
        s = signals(c, pre)
        got, sent = ([s(f"{m}{u}") for u in range(4)] for m in ("got", "sent"))
        keyed, older = ([s(f"{m}{u}") for u in range(2)] for m in ("keyed", "older"))
        per_send = 16 * K4 if n == 3 else 16
        block = ctx.enter_context(nc.Block())

        @block.gpsimd
        def _(pool):
            def gather(t):
                u = t.slot(4)
                if not t.early(4):
                    pool.wait_ge(s("opened"), t.g - 3)
                    if n == 3:
                        pool.wait_ge(sent[u], t.turn(4) * per_send)
                    pool.sem_inc(s("issuing"), 1)
                place = side["index"][:, bass.ds(t.g, 1), OTHER, :] if n == 1 else c.s_place[:, bass.ds(t.g, 1), :]
                pool.tensor_copy(at[:, u, 0, :], place.rearrange("p o k -> p (o k)")).then_inc(s("at"), 1)
                if n == 3:
                    pool.tensor_copy(at[:, u, 1, :], side["index"][:, bass.ds(t.g, 1), LAST, :].rearrange("p o k -> p (o k)"))\
                        .then_inc(s("at"), 1)
                pool.wait_ge(s("at"), (t.g + 1) * (2 if n == 3 else 1))
                pool.sem_inc(s("issuing"), 1)
                for k in range(K4):
                    pool.indirect_dma_start(x[:, u, k, :], None, table[:, :],
                                            bass.IndirectOffsetOnAxis(ap=at[:, u, 0, k:k + 1], axis=0)).then_inc(got[u], 16)

            def scatter(t):
                u = t.slot(4)
                pool.wait_ge(s("h_done"), t.g + 1)
                pool.sem_inc(s("issuing"), 1)
                for k in range(K4):
                    pool.indirect_dma_start(c.a_dram[:, :], bass.IndirectOffsetOnAxis(ap=at[:, u, 1, k:k + 1], axis=0),
                                            h[:, u, k, :], None, bounds_check=N - 1, oob_is_err=False,
                                            compute_op=ALU.add).then_inc(sent[u], 16)
            skewed(pool, GROUPS, [(0, gather)] + ([(3, scatter)] if n == 3 else []))
            if n == 3:
                for u in range(4):
                    pool.wait_ge(sent[u], len(range(u, GROUPS, 4)) * per_send)

        @block.sync
        def _(sp):
            def load_old(t):
                if not t.early(2):
                    sp.wait_ge(s("h_done"), t.g - 1)
                sp.dma_start(old[:, t.slot(2), 0, :, :], edge_rows(c.h1_dram, t.g)).then_inc(older[t.slot(2)], 16)
                sp.dma_start(old[:, t.slot(2), 1, :, :], edge_rows(c.h2_dram, t.g)).then_inc(older[t.slot(2)], 16)

            def store(t):
                sp.wait_ge(s("h_own"), t.g + 1)
                sp.dma_start(edge_rows((c.h1_dram, c.h2_dram)[n - 1], t.g), h[:, t.slot(4), :, :]).then_inc(sent[t.slot(4)], 16)
            skewed(sp, GROUPS, [(0, lambda t: load_keys(sp, side["keys"], keys[:, t.slot(2), :], t, 1, ROWS, 2, s("masked"), keyed)),
                                (2, load_old) if n == 3 else (4, store)])
            if n < 3:
                for u in range(4):
                    sp.wait_ge(sent[u], len(range(u, GROUPS, 4)) * per_send)

        @block.tensor
        def _(pe):
            def inside(t, k):
                if k == 0:
                    pe.wait_ge(got[t.slot(4)], (t.turn(4) + 1) * 16 * K4)
                    pe.wait_ge(s("masked"), t.g + 1)
                    if not t.early(2):
                        pe.wait_ge(s("total"), (t.g - 1) * K4)
                last = pe.matmul(acc[:, t.slot(2) * K4 + k, 0:D], same[:, t.slot(4), k, :], x[:, t.slot(4), k, :],
                                 start=True, stop=False)
                if k == K4 - 1:
                    last.then_inc(s("opened"), 1)

            def across(t, k):
                if t.early(1) and k == 0:
                    pe.wait_ge(s("total_clear"), 1)
                else:
                    pe.wait_ge(s("total"), t.g * K4 + k)
                before = total[96:P, t.slot(4), k - 1, :] if k else total[96:P, (t.slot(4) - 1) % 4, K4 - 1, :]
                pe.matmul(acc[:, t.slot(2) * K4 + k, 0:D], cont[96:P, t.slot(4), k, :], before,
                          start=False, stop=True).then_inc(s("acc"), 1)
            skewed(pe, GROUPS, [(lag, lambda t, k=k, fn=fn: fn(t, k)) for k in range(K4) for lag, fn in ((1, across), (0, inside))])

        @block.scalar
        def _(act):
            def norms(t):
                act.wait_ge(s("squared"), t.g + 1)
                inverse_norm(act, c, ss[:, t.slot(2), :], rn[:, t.slot(2), :], s, t.g, c.consts[:, 5:6] if n == 3 else c.consts[:, 2:3])

            def totals(t):
                for k in range(K4):
                    act.wait_ge(s("acc"), t.g * K4 + k + 1)
                    if k == 0 and not t.early(4):
                        act.wait_ge(s("h_own"), t.g - 3)
                    act.activation(total[:, t.slot(4), k, :], acc[:, t.slot(2) * K4 + k, 0:D], ACT.Copy).then_inc(s("total"), 1)
            skewed(act, GROUPS, [(2, norms), (1, totals)])

        @block.vector
        def _(dve):
            dve.memset(total[:, 3, K4 - 1, :], 0.0).then_inc(s("total_clear"), 1)

            def masks(t):
                u, v = t.slot(2), t.slot(4)
                dve.wait_ge(keyed[u], 16 * (t.turn(2) + 1))
                if not t.early(4):
                    dve.wait_ge(s("acc"), (t.g - 3) * K4)
                for k in range(K4):
                    dve.tensor_scalar(same[:, v, k, :], keys[:, u, k * P:(k + 1) * P], side["key"][:, bass.ds(t.g * K4 + k + 1, 1)],
                                      weight[:, bass.ds(t.g * K4 + k, 1)], ALU.is_equal, ALU.mult)
                dve.tensor_tensor(cont[96:P, v, :, :], keys[96:P, u, :].rearrange("p (k j) -> p k j", k=K4),
                                  along(side["key_end"][96:P, bass.ds(t.g * K4, K4)]), ALU.is_equal).then_inc(s("masked"), 1)

            def squares(t):
                dve.wait_ge(s("total"), (t.g + 1) * K4)
                if not t.early(2):
                    dve.wait_ge(s("rn_guard"), t.g - 1)
                if not t.early(1):
                    dve.wait_ge(s("squared"), t.g)
                for k in range(K4):
                    last = dve.scalar_tensor_tensor(out=square[:, k, :], in0=total[:, t.slot(4), k, :], scalar=1.0,
                                                    in1=total[:, t.slot(4), k, :], op0=ALU.mult, op1=ALU.mult,
                                                    accum_out=ss[:, t.slot(2), k:k + 1])
                last.then_inc(s("squared"), 1)

            def scale(t):
                u, v = t.slot(2), t.slot(4)
                dve.wait_ge(s("rn"), t.g + 1)
                if not t.early(4):
                    dve.wait_ge(sent[v], t.turn(4) * per_send)
                for k in range(K4):
                    last = dve.tensor_scalar(h[:, v, k, :], total[:, v, k, :], rn[:, u, k:k + 1], None, ALU.mult)
                last.then_inc(s("h_own"), 1)
                if n < 3:
                    return
                dve.wait_ge(older[u], (t.turn(2) + 1) * 32)
                dve.wait_ge(s("h_own"), t.g + 1)
                dve.scalar_tensor_tensor(out=h[:, v, :, :], in0=old[:, u, 0, :, :], scalar=0.25, in1=h[:, v, :, :],
                                         op0=ALU.mult, op1=ALU.add).then_inc(s("h_first"), 1)
                dve.wait_ge(s("h_first"), t.g + 1)
                dve.scalar_tensor_tensor(out=h[:, v, :, :], in0=old[:, u, 1, :, :], scalar=0.25, in1=h[:, v, :, :],
                                         op0=ALU.mult, op1=ALU.add).then_inc(s("h_done"), 1)
            skewed(dve, GROUPS, [(0, masks), (1, squares), (2, scale)])


def node_pass_two(c):
    nc = c.nc
    with c.phase() as ctx:
        sb = lambda n, shape, dt=F32: c.sb("n2_" + n, shape, dt, ctx=ctx)
        x, x3, y = sb("x", [P, 4, K4, D]), sb("x3", [P, 4, K4, D]), sb("y", [P, 2, K4, D])
        xT, h, square = sb("xT", [P, 2, 2, ROWS]), sb("h", [P, 2, K4, D]), sb("square", [P, K4, D])
        stats, mv, rs = sb("stats", [P, 2, K4, 6]), sb("mv", [P, 2, 2, K4, 2]), sb("rs", [P, 2, K4])
        log, fac = sb("log", [P, 2, 2, K4]), sb("fac", [P, 2, 3, K4])
        ss, rn = sb("ss", [P, 2, K4]), sb("rn", [P, 2, K4])
        turn = c.ps("n2_turn", [P, 4, 512], ctx=ctx)
        prod = c.ps("n2_prod", [P, 4, 512], ctx=ctx)
        s = signals(c, "n2_")
        loaded, sent2, sent3 = ([s(f"{n}{u}") for u in range(4)] for n in ("loaded", "sent2_", "sent3_"))
        senty = [s("senty0"), s("senty1")]
        tiles = lambda t: prod[:, 2 * t.slot(2):2 * t.slot(2) + 2, :].rearrange("p b (j d) -> p (b j) d", d=D)
        block = ctx.enter_context(nc.Block())

        @block.sync
        def _(sp):
            def load(t):
                if not t.early(4):
                    sp.wait_ge(sent2[t.slot(4)], 16 * t.turn(4))
                    sp.wait_ge(s("z"), t.g - 3)
                sp.dma_start(x[:, t.slot(4), :, :], node_rows(c.a_dram, t.g)).then_inc(loaded[t.slot(4)], 16)

            def store(t, dram, buf, slots, done, sent):
                if t.last(NG):
                    sp.wait_ge(sent[(NG - 2) % slots], 16 * ((NG - 2) // slots + 1))
                sp.wait_ge(s(done), t.g + 1)
                sp.dma_start(node_rows(dram, t.g), buf[:, t.slot(slots), :, :]).then_inc(sent[t.slot(slots)], 16)
            skewed(sp, NG, [(0, load), (1, lambda t: store(t, c.x2_dram, x, 4, "x2", sent2)),
                            (3, lambda t: store(t, c.x3_dram, x3, 4, "x3_done", sent3)),
                            (3, lambda t: store(t, c.out, y, 2, "y_done", senty))])
            for u in range(4):
                sp.wait_ge(sent2[u], 16 * len(range(u, NG, 4)))
                sp.wait_ge(sent3[u], 16 * len(range(u, NG, 4)))
            for u in range(2):
                sp.wait_ge(senty[u], 16 * len(range(u, NG, 2)))

        @block.vector
        def _(dve):
            def sum_up(t):
                v = t.slot(4)
                dve.wait_ge(s("rn"), t.g + 1)
                if not t.early(4):
                    dve.wait_ge(sent3[v], 16 * t.turn(4))
                    dve.wait_ge(s("y_done"), t.g - 3)
                for k in range(K4):
                    last = dve.scalar_tensor_tensor(out=x3[:, v, k, :], in0=h[:, t.slot(2), k, :], scalar=rn[:, t.slot(2), k:k + 1],
                                                    in1=x[:, v, k, :], op0=ALU.mult, op1=ALU.add)
                last.then_inc(s("z"), 1)
                dve.wait_ge(s("z"), t.g + 1)
                row_stats(dve, x3[:, v], stats[:, 1], mv[:, 1, t.slot(2)], s, "b", t.g)

            def measure(t):
                dve.wait_ge(loaded[t.slot(4)], 16 * (t.turn(4) + 1))
                row_stats(dve, x[:, t.slot(4)], stats[:, 0], mv[:, 0, t.slot(2)], s, "a", t.g)

            def out(t):
                row_apply(dve, x3[:, t.slot(4)], x3[:, t.slot(4)], mv[:, 1, t.slot(2)], fac[:, t.slot(2), 0], s, "b", t.g, "x3_done")

            def apply(t):
                row_apply(dve, x[:, t.slot(4)], x[:, t.slot(4)], mv[:, 0, t.slot(2)], rs[:, t.slot(2)], s, "a", t.g, "x2")
            skewed(dve, NG, [(2, sum_up), (0, measure), (2, out), (0, apply)])

        @block.gpsimd
        def _(pool):
            def twice(t):
                pool.wait_ge(s("x3_done"), t.g + 1)
                if not t.early(2):
                    pool.wait_ge(senty[t.slot(2)], 16 * t.turn(2))
                pool.sem_inc(s("held"), 1)
                for k in range(K4):
                    last = pool.tensor_scalar(y[:, t.slot(2), k, :], x3[:, t.slot(4), k, :], fac[:, t.slot(2), 1, k:k + 1],
                                              fac[:, t.slot(2), 2, k:k + 1], ALU.mult, ALU.mult)
                last.then_inc(s("y_done"), 1)
            skewed(pool, NG, [(0, twice)])

        @block.scalar
        def _(act):
            def scales(t):
                u = t.slot(2)
                act.wait_ge(s("b_var"), t.g + 1)
                if not t.early(2):
                    act.wait_ge(s("y_done"), t.g - 1)
                act.activation(log[:, u, 0, :], mv[:, 1, u, :, 1], ACT.Ln, bias=c.consts[:, 0:1])
                act.activation(log[:, u, 1, :], mv[:, 1, u, :, 1], ACT.Ln, bias=c.consts[:, 8:9], scale=1.0 + LN_EPS)\
                   .then_inc(s("b_log"), 1)
                act.wait_ge(s("b_log"), t.g + 1)
                act.activation(fac[:, u, 1, :], log[:, u, 0, :], ACT.Exp, scale=0.5)
                act.activation(fac[:, u, 2, :], log[:, u, 1, :], ACT.Exp, scale=-0.5)
                act.activation(fac[:, u, 0, :], log[:, u, 0, :], ACT.Exp, scale=-0.5).then_inc(s("b_scale"), 1)

            def norm(t):
                u = t.slot(2)
                act.wait_ge(s("prod"), t.g + 1)
                if not t.early(2):
                    act.wait_ge(s("z"), t.g - 1)
                act.activation(h[:, u, :, :], tiles(t), ACT.Relu).then_inc(s("relu"), 1)
                act.wait_ge(s("relu"), t.g + 1)
                if not t.early(1):
                    act.wait_ge(s("squared"), t.g)
                for k in range(K4):
                    last = act.activation(square[:, k, :], h[:, u, k, :], ACT.Square, accum_out=ss[:, u, k:k + 1])
                last.then_inc(s("squared"), 1)
                act.wait_ge(s("squared"), t.g + 1)
                inverse_norm(act, c, ss[:, u, :], rn[:, u, :], s, t.g, c.consts[:, 2:3])

            def copy(t):
                u = t.slot(2)
                act.wait_ge(s("xT"), t.g + 1)
                if not t.early(2):
                    act.wait_ge(s("prod"), t.g - 1)
                act.activation(xT[:, u, :, :], turn[:, 2 * u:2 * u + 2, :], ACT.Copy).then_inc(s("xT_sb"), 1)
            skewed(act, NG, [(2, scales), (0, lambda t: row_scale(act, c, mv[:, 0, t.slot(2)], rs[:, t.slot(2), :], s, "a", t.g)),
                             (1, norm), (0, copy)])

        @block.tensor
        def _(pe):
            def step(t):
                u = t.slot(2)
                pe.wait_ge(s("x2"), t.g + 1)
                if not t.early(2):
                    pe.wait_ge(s("xT_sb"), t.g - 1)
                for f in range(2):
                    for k in range(K4):
                        last = pe.transpose(turn[:, 2 * u + f, k * P:(k + 1) * P], x[:, t.slot(4), k, f * P:(f + 1) * P], c.ident[:, :])
                last.then_inc(s("xT"), 1)
                if not t.early(2):
                    pe.wait_ge(s("relu"), t.g - 1)
                for b in range(2):
                    pe.matmul(prod[:, 2 * u + b, :], c.one_row[0:1, :], c.bias_row[0:1, :], start=True, stop=False)
                pe.wait_ge(s("xT_sb"), t.g + 1)
                for k in range(K4):
                    for f in range(2):
                        last = pe.matmul(tiles(t)[:, k, :], xT[:, u, f, k * P:(k + 1) * P], c.wg[:, f, 0:D],
                                         start=False, stop=(f == 1 and k % 2 == 1))
                last.then_inc(s("prod"), 1)
            skewed(pe, NG, [(0, step)])


def attention_layer(c, layer):
    nc = c.nc
    side = c.d
    two = layer == 2
    H = H2 if two else H3
    W = D + H
    kinds = 2 if two else 1
    source = c.x2_dram if two else c.x3_dram
    target = c.x3_dram if two else c.out
    with c.phase() as ctx:
        pre = f"l{layer}_"
        sb = lambda n, shape, dt=F32: c.sb(pre + n, shape, dt, ctx=ctx)
        xs, xd = sb("xs", [P, 2, K4, D]), sb("xd", [P, 4, K4, D])
        at = sb("at", [P, 4, 4, K4], I32)
        keys, cuts = sb("keys", [P, 2, ROWS]), sb("cuts", [H3, 2, ROWS + 1])
        same, cont = sb("same", [P, 4, K4, P]), sb("cont", [P, 4, K4, P])
        xT = sb("xT", [P, 2, 2, ROWS])
        hs, hd = (sb("hs", [P, 2, K4, D]), sb("hd", [P, 4, K4, D])) if two else (None, None)
        score, e = sb("score", [P, 2, 2, K4, 2 * H2]), sb("e", [P, 2, 2, K4, H])
        esc, top = sb("esc", [P, K4, H]), sb("top", [P, 2, K4, H])
        run_max, seg_max = sb("run_max", [H3, 2, ROWS]), sb("seg_max", [H3, ROWS])
        prob, fade = sb("prob", [P, 4, 2, K4, H]), sb("fade", [P, 2, H])
        msg, total, carry = sb("msg", [P, 2, K4, W]), sb("total", [P, 2, K4, W]), sb("carry", [P, W])
        den, r, y = sb("den", [P, K4, H]), sb("r", [P, K4, D]), sb("y", [P, 4, K4, D])
        square = sb("square", [P, K4, D]) if two else None
        stats, mv, rs = sb("stats", [P, K4, 6]), sb("mv", [P, K4, 2]), sb("rs", [P, K4])
        ss, rn = sb("ss", [P, K4]), sb("rn", [P, K4])
        ps_turn = c.ps(pre + "ps_turn", [P, 2, 512], ctx=ctx)
        ps_h = c.ps(pre + "ps_h", [P, K4, D], ctx=ctx) if two else None
        ps_acc = c.ps(pre + "ps_acc", [P, 2, 512], ctx=ctx)
        ps_score = c.ps(pre + "ps_score", [P, 512], ctx=ctx)
        ps_max = c.ps(pre + "ps_max", [P, 512], ctx=ctx)
        raw = ps_score[:, 0:2 * K4 * 2 * H2].rearrange("p (o k h) -> p o k h", o=2, k=K4)
        back = ps_score[:, 128:128 + K4 * H].rearrange("p (k h) -> p k h", k=K4)
        head_of = ps_score[:, 256:256 + H]
        s = signals(c, pre)
        got_s, keyed = ([s(f"{n}{u}") for u in range(2)] for n in ("got_s", "keyed"))
        got_d, sent = ([s(f"{n}{u}") for u in range(4)] for n in ("got_d", "sent"))
        if two:
            split = lambda v: v.rearrange("p k (h d) -> p k h d", h=H)
            spread = lambda v: v.rearrange("p k (h o) -> p k h o", o=1).to_broadcast([v.shape[0], v.shape[1], H, D // H])
        else:
            split = lambda v: v.rearrange("p k (d h) -> p k d h", h=H)
            spread = lambda v: v.rearrange("p k (o h) -> p k o h", o=1).to_broadcast([v.shape[0], v.shape[1], D // H, H])
        one = lambda v: v.rearrange("p (o d) -> p o d", o=1)
        block = ctx.enter_context(nc.Block())

        @block.gpsimd
        def _(pool):
            def gather(t):
                u, v = t.slot(2), t.slot(4)
                if not t.early(2):
                    if two:
                        pool.wait_ge(s("xT"), 2 * (t.g - 1))
                    else:
                        pool.wait_ge(s("msg"), t.g - 1)
                if not t.early(4):
                    pool.wait_ge(sent[v], t.turn(4) * 16 * K4)
                    pool.wait_ge(s("summed"), t.g - 3)
                    pool.sem_inc(s("issuing"), 1)
                pool.tensor_copy(at[:, v, :, :], side["index"][:, bass.ds(t.g, 1), :, :].rearrange("p o n k -> p (o n) k"))\
                    .then_inc(s("at"), 1)
                pool.wait_ge(s("at"), t.g + 1)
                pool.sem_inc(s("issuing"), 1)
                for to, kind, got in ((xs[:, u], OTHER, got_s[u]), (xd[:, v], OWN, got_d[v])):
                    for k in range(K4):
                        pool.indirect_dma_start(to[:, k, :], None, source[:, :],
                                                bass.IndirectOffsetOnAxis(ap=at[:, v, kind, k:k + 1], axis=0)).then_inc(got, 16)

            def scatter(t):
                v = t.slot(4)
                pool.wait_ge(s("y_done"), t.g + 1)
                pool.sem_inc(s("issuing"), 1)
                for k in range(K4):
                    pool.indirect_dma_start(target[:, :], bass.IndirectOffsetOnAxis(ap=at[:, v, LAST, k:k + 1], axis=0),
                                            y[:, v, k, :], None, bounds_check=N - 1, oob_is_err=False).then_inc(sent[v], 16)
            skewed(pool, GROUPS, [(0, gather), (3, scatter)])
            for v in range(4):
                pool.wait_ge(sent[v], len(range(v, GROUPS, 4)) * 16 * K4)

        @block.sync
        def _(sp):
            def load(t):
                if not t.early(2):
                    sp.wait_ge(s("masked"), t.g - 1)
                load_keys(sp, side["keys"], keys[:, t.slot(2), :], t, 1, ROWS, 2, s("seg_max"), keyed)
                sp.dma_start(cuts[0:H, t.slot(2), :], side["cuts"][bass.ds(t.g * ROWS, ROWS + 1)].rearrange("(o n) -> o n", o=1)
                             .to_broadcast([H, ROWS + 1])).then_inc(keyed[t.slot(2)], 16)
            skewed(sp, GROUPS, [(0, load)])

        @block.tensor
        def _(pe):
            def scores_across(t):
                pe.wait_ge(s("esc"), t.g + 1)
                pe.wait_ge(s("run_max"), t.g)
                for k in range(K4):
                    last = pe.matmul(ps_max[0:H, k * P:(k + 1) * P], esc[:, k, :], c.ident[:, :], start=True, stop=True)
                last.then_inc(s("escT"), 1)

            def accumulate(t, k):
                u, v = t.slot(2), t.slot(4)
                if k == 0:
                    pe.wait_ge(s("msg"), t.g + 1)
                    pe.wait_ge(s("masked"), t.g + 1)
                    pe.wait_ge(s("carry"), t.g + 1)
                    pe.wait_ge(s("total"), t.g * K4)
                pe.matmul(ps_acc[:, k % 2, 0:W], same[:, v, k, :], msg[:, u, k, :], start=True, stop=False)
                if k:
                    pe.wait_ge(s("total"), t.g * K4 + k)
                rest = carry[96:P, :] if k == 0 else total[96:P, u, k - 1, :]
                pe.matmul(ps_acc[:, k % 2, 0:W], cont[96:P, v, k, :], rest, start=False, stop=True).then_inc(s("acc"), 1)

            def turn(t, n):
                x, got, i = ((xs[:, t.slot(2)], got_s[t.slot(2)], t.turn(2)), (xd[:, t.slot(4)], got_d[t.slot(4)], t.turn(4)))[n]
                pe.wait_ge(got, (i + 1) * 16 * K4)
                pe.wait_ge(s("xT_sb"), 2 * t.g + n)
                for f in range(2):
                    for k in range(K4):
                        last = pe.transpose(ps_turn[:, f, k * P:(k + 1) * P], x[:, k, f * P:(f + 1) * P], c.ident[:, :])
                last.then_inc(s("xT"), 1)

            def project(t, n):
                pe.wait_ge(s("xT_sb"), 2 * t.g + n + 1)
                if two:
                    pe.wait_ge(s("h_sb"), 2 * t.g + n)
                    for k in range(K4):
                        for f in range(2):
                            last = pe.matmul(ps_h[:, k, :], xT[:, n, f, k * P:(k + 1) * P], c.wg[:, f, 0:D],
                                             start=(f == 0), stop=(f == 1))
                    last.then_inc(s("h"), 1)

            def raw_scores(t):
                pe.wait_ge(s("fade_sub"), t.g)
                for n in range(2):
                    for k in range(K4):
                        for f in range(2):
                            vec = c.wg[:, f, D:D + 2 * H2] if two else c.wuv[:, f, n * H3:(n + 1) * H3]
                            last = pe.matmul(raw[:, n, k, :], xT[:, n, f, k * P:(k + 1) * P], vec, start=(f == 0), stop=(f == 1))
                last.then_inc(s("raw"), 1)

            def maxima_back(t):
                pe.wait_ge(s("seg_max"), t.g + 1)
                for k in range(K4):
                    last = pe.matmul(back[:, k, :], seg_max[0:H, k * P:(k + 1) * P], c.ident[0:H, 0:H], start=True, stop=True)
                last.then_inc(s("back"), 1)

            def first_maximum(t):
                pe.wait_ge(s("top"), t.g + 1)
                pe.matmul(head_of, c.first[:, :], top[:, t.slot(2), 0, :], start=True, stop=True).then_inc(s("head_of"), 1)

            at_ = lambda fn, *args: (lambda t: fn(t, *args))
            skewed(pe, GROUPS, [(1, scores_across), (2, at_(accumulate, 0)), (0, at_(turn, 0)), (2, at_(accumulate, 1)),
                                (0, at_(project, 0)), (1, maxima_back), (2, at_(accumulate, 2)), (0, at_(turn, 1)),
                                (2, at_(accumulate, 3)), (1, first_maximum), (0, at_(project, 1)), (0, raw_scores)])

        @block.scalar
        def _(act):
            def totals(t, k):
                act.wait_ge(s("acc"), t.g * K4 + k + 1)
                if k == 0 and not t.early(2):
                    act.wait_ge(s("total_used"), t.g - 1)
                if k == K4 - 1:
                    act.wait_ge(s("carry"), t.g + 1)
                act.activation(total[:, t.slot(2), k, :], ps_acc[:, k % 2, 0:W], ACT.Copy).then_inc(s("total"), 1)

            def copy(t, n):
                act.wait_ge(s("xT"), 2 * t.g + n + 1)
                act.wait_ge(s("raw"), t.g)
                act.activation(xT[:, n, :, :], ps_turn[:, :, :], ACT.Copy).then_inc(s("xT_sb"), 1)

            def features(t, n):
                if two:
                    act.wait_ge(s("h"), 2 * t.g + n + 1)
                    if n == 0 and not t.early(2):
                        act.wait_ge(s("msg"), t.g - 1)
                    if n == 1 and not t.early(4):
                        act.wait_ge(s("own_used"), t.g - 3)
                    act.activation((hs[:, t.slot(2)], hd[:, t.slot(4)])[n], ps_h[:, :, :], ACT.Copy).then_inc(s("h_sb"), 1)

            def exp_prob(t):
                act.wait_ge(s("below"), t.g + 1)
                act.activation(prob[:, t.slot(4), 0:kinds, :, :], prob[:, t.slot(4), 0:kinds, :, :], ACT.Exp).then_inc(s("prob"), 1)

            def exp_fade(t):
                act.wait_ge(s("fade_in"), t.g + 1)
                act.activation(fade[96:P, t.slot(2), :], fade[96:P, t.slot(2), :], ACT.Exp).then_inc(s("fade"), 1)

            def scores(t):
                act.wait_ge(s("raw"), t.g + 1)
                act.activation(score[:, t.slot(2), :, :, :], raw, ACT.Copy).then_inc(s("score"), 1)

            def norm(t):
                act.wait_ge(s("biased"), t.g + 1)
                act.activation(r[:, :, :], r[:, :, :], ACT.Relu).then_inc(s("relu"), 1)
                act.wait_ge(s("relu"), t.g + 1)
                if not t.early(1):
                    act.wait_ge(s("squared"), t.g)
                for k in range(K4):
                    last = act.activation(square[:, k, :], r[:, k, :], ACT.Square, accum_out=ss[:, k:k + 1])
                last.then_inc(s("squared"), 1)
                act.wait_ge(s("squared"), t.g + 1)
                inverse_norm(act, c, ss[:, :], rn[:, :], s, t.g, c.consts[:, 2:3])

            at_ = lambda fn, *args: (lambda t: fn(t, *args))
            stages = [(2, at_(totals, 0)), (0, at_(copy, 0)), (2, at_(totals, 1)), (0, at_(features, 0)), (2, at_(totals, 2)),
                      (0, at_(copy, 1)), (1, exp_prob), (2, at_(totals, 3)), (1, exp_fade), (0, at_(features, 1)), (0, scores)]
            if two:
                stages.append((3, norm))
            skewed(act, GROUPS, stages + [(3, lambda t: row_scale(act, c, mv, rs[:, :], s, "b", t.g))])

        @block.vector
        def _(dve):
            def chained(name, ins, g):
                ins.then_inc(s(name), 1)
                dve.wait_ge(s(name), g + 1)

            dve.memset(total[:, 1, K4 - 1, :], 0.0).then_inc(s("clear"), 1)
            dve.memset(top[:, 1, :, :], 0.0).then_inc(s("clear"), 1)
            dve.memset(run_max[0:H, 1, :], LOW).then_inc(s("clear"), 1)
            dve.wait_ge(s("clear"), 3)

            def carry_in(t):
                u = t.slot(2)
                dve.wait_ge(s("fade"), t.g + 1)
                dve.wait_ge(s("total"), t.g * K4)
                if not t.early(1):
                    dve.wait_ge(s("acc"), (t.g - 1) * K4 + 1)
                before, f = total[96:P, 1 - u, K4 - 1:K4, :], fade[96:P, u, :]
                dve.tensor_tensor(split(one(carry[96:P, 0:D])), split(before[:, :, 0:D]), spread(one(f)), ALU.mult)
                dve.tensor_tensor(carry[96:P, D:W], total[96:P, 1 - u, K4 - 1, D:W], f, ALU.mult).then_inc(s("carry"), 1)

            def edge_scores(t):
                u = t.slot(2)
                dve.wait_ge(s("score"), t.g + 1)
                if two:
                    for n in range(2):
                        last = dve.tensor_tensor(e[:, u, n, :, :], score[:, u, n, :, 0:H], score[:, u, 1, :, H:2 * H], ALU.add)
                else:
                    chained("e_sum", dve.tensor_tensor(e[:, u, 0, :, :], score[:, u, 0, :, :], score[:, u, 1, :, :], ALU.add), t.g)
                    last = dve.tensor_tensor(e[:, u, 0, :, :], e[:, u, 0, :, :], over_tiles(c.bu[:, :]), ALU.add)
                chained("e_raw", last, t.g)
                last = dve.scalar_tensor_tensor(out=e[:, u, 0:kinds, :, :], in0=e[:, u, 0:kinds, :, :], scalar=0.2,
                                                in1=e[:, u, 0:kinds, :, :], op0=ALU.mult, op1=ALU.max)
                chained("e_leaky", last, t.g)
                dve.wait_ge(s("escT"), t.g)
                dve.tensor_tensor(esc[:, :, :], e[:, u, 0, :, :], e[:, u, kinds - 1, :, :], ALU.max).then_inc(s("esc"), 1)

            def masks(t):
                u, v = t.slot(2), t.slot(4)
                dve.wait_ge(keyed[u], 32 * (t.turn(2) + 1))
                if not t.early(4):
                    dve.wait_ge(s("acc"), (t.g - 3) * K4)
                rows = keys[:, u, :].rearrange("p (k j) -> p k j", k=K4)
                dve.tensor_tensor(same[:, v, :, :], rows, along(side["key"][:, bass.ds(t.g * K4 + 1, K4)]), ALU.is_equal)
                dve.tensor_tensor(cont[96:P, v, :, :], rows[96:P, :, :], along(side["key_end"][96:P, bass.ds(t.g * K4, K4)]),
                                  ALU.is_equal).then_inc(s("masked"), 1)

            def scans(t):
                u = t.slot(2)
                dve.wait_ge(s("escT"), t.g + 1)
                dve.wait_ge(keyed[u], 32 * (t.turn(2) + 1))
                chained("run_max", dve.tensor_tensor_scan(run_max[0:H, u, :], cuts[0:H, u, 0:ROWS], ps_max[0:H, :],
                                                          run_max[0:H, 1 - u, ROWS - 1:ROWS], ALU.add, ALU.max), t.g)
                dve.wait_ge(s("back"), t.g)
                dve.tensor_tensor_scan(seg_max[0:H, :][:, ::-1], cuts[0:H, u, 1:ROWS + 1][:, ::-1], run_max[0:H, u, :][:, ::-1],
                                       LOW, ALU.add, ALU.max).then_inc(s("seg_max"), 1)

            def subtract_max(t):
                u, v = t.slot(2), t.slot(4)
                dve.wait_ge(s("back"), t.g + 1)
                chained("top", dve.tensor_copy(top[:, u, :, :], back), t.g)
                if not t.early(4):
                    dve.wait_ge(s("own_used"), t.g - 3)
                for n in range(kinds):
                    last = dve.tensor_tensor(prob[:, v, n, :, :], e[:, u, n, :, :], top[:, u, :, :], ALU.subtract)
                last.then_inc(s("below"), 1)

            def fade_out(t):
                u = t.slot(2)
                dve.wait_ge(s("head_of"), t.g + 1)
                chained("fade_sub", dve.tensor_tensor(fade[96:P, u, :], top[96:P, 1 - u, K4 - 1, :], head_of[96:P, :], ALU.subtract), t.g)
                dve.tensor_scalar(fade[96:P, u, :], fade[96:P, u, :], 0.0, None, ALU.min).then_inc(s("fade_in"), 1)

            def messages(t):
                u = t.slot(2)
                dve.wait_ge(s("prob"), t.g + 1)
                if not t.early(2):
                    dve.wait_ge(s("acc"), (t.g - 1) * K4)
                p = prob[:, t.slot(4), 0, :, :]
                dve.tensor_copy(msg[:, u, :, D:W], p)
                last = dve.tensor_tensor(split(msg[:, u, :, 0:D]), split((hs if two else xs)[:, u, :, :]), spread(p), ALU.mult)
                last.then_inc(s("msg"), 1)

            def own_loop(t):
                if two:
                    dve.wait_ge(s("total"), (t.g + 1) * K4)
                    dve.wait_ge(s("summed"), t.g)
                    p = prob[:, t.slot(4), 1, :, :]
                    dve.tensor_tensor(den[:, :, :], total[:, t.slot(2), :, D:W], p, ALU.add)
                    chained("own_used", dve.tensor_tensor(split(r[:, :, :]), split(hd[:, t.slot(4), :, :]), spread(p), ALU.mult), t.g)
                    dve.tensor_tensor(r[:, :, :], r[:, :, :], total[:, t.slot(2), :, 0:D], ALU.add).then_inc(s("total_used"), 1)
                    chained("den", dve.reciprocal(den[:, :, :], den[:, :, :]), t.g)

            def divide(t):
                v = t.slot(4)
                if two:
                    chained("divided", dve.tensor_tensor(split(r[:, :, :]), split(r[:, :, :]), spread(den[:, :, :]), ALU.mult), t.g)
                    dve.tensor_tensor(r[:, :, :], r[:, :, :], over_tiles(c.bias[:, :]), ALU.add).then_inc(s("biased"), 1)
                else:
                    dve.wait_ge(s("total"), (t.g + 1) * K4)
                    chained("den", dve.reciprocal(den[:, :, :], total[:, t.slot(2), :, D:W]), t.g)
                    last = dve.tensor_tensor(split(r[:, :, :]), split(total[:, t.slot(2), :, 0:D]), spread(den[:, :, :]), ALU.mult)
                    chained("total_used", last, t.g)
                    dve.sem_inc(s("own_used"), 1)

            def finish(t):
                v = t.slot(4)
                if not t.early(4):
                    dve.wait_ge(sent[v], t.turn(4) * 16 * K4)
                dve.wait_ge(got_d[v], (t.turn(4) + 1) * 16 * K4)
                if two:
                    dve.wait_ge(s("rn"), t.g + 1)
                    for k in range(K4):
                        last = dve.scalar_tensor_tensor(out=y[:, v, k, :], in0=r[:, k, :], scalar=rn[:, k:k + 1],
                                                        in1=xd[:, v, k, :], op0=ALU.mult, op1=ALU.add)
                else:
                    last = dve.tensor_tensor(y[:, v, :, :], r[:, :, :], xd[:, v, :, :], ALU.add)
                chained("summed", last, t.g)
                row_stats(dve, y[:, v], stats, mv, s, "b", t.g)
                row_apply(dve, y[:, v], y[:, v], mv, rs, s, "b", t.g, "y_done")
            skewed(dve, GROUPS, [(2, carry_in), (1, edge_scores), (0, masks), (1, scans), (3, own_loop), (1, subtract_max),
                                 (3, divide), (1, fade_out), (1, messages), (3, finish)])


_NAMES = {"x": "x", "src": "src", "dst": "dst", "ea": "edge_attr_64", "ew": "edge_weight", "fw1": "L0_gnn_fw1",
          "fb1": "L0_gnn_fb1", "fw2": "L0_gnn_fw2", "fb2": "L0_gnn_fb2", "w1": "L0_gnn_w1", "w2": "L0_gnn_w2",
          "b2": "L0_gnn_b2", "w3": "L0_gnn_w3", "b3": "L0_gnn_b3", "W": "L2_gnn_W", "att_src": "L2_gnn_att_src",
          "att_dst": "L2_gnn_att_dst", "bias": "L2_gnn_bias", "W_u": "L3_gnn_W_u", "b_u": "L3_gnn_b_u",
          "W_v": "L3_gnn_W_v"}


def build(nc, a, out, stop=None):
    with ExitStack() as ctx:
        c = Core(nc, ctx)
        c.out = out
        dram = lambda n, shape, dt=F32: nc.dram_tensor(n, shape, dt, kind="Internal").ap()
        c.h1_dram, c.h2_dram = dram("h1_rows", (EP + 1, D)), dram("h2_rows", (EP + 1, D))
        c.place_dram = dram("node_places", (N, 1), I32)
        c.a_dram, c.x3_dram = dram("a_rows", (N, D)), dram("x3_rows", (N, D))
        c.wg = c.sb("wg", [P, 2, D + 2 * H2])
        c.fw2T, c.w1T, c.w2T, c.w3T = (c.sb(n, [P, 2, D]) for n in ("fw2T", "w1T", "w2T", "w3T"))
        c.fw1T, c.wuv = c.sb("fw1T", [BASIS, D]), c.sb("wuv", [P, 2, 16])
        c.fb1, c.b2 = c.sb("fb1", [P, 2]), c.sb("b2", [P, 2])
        c.fb2, c.b3, c.bias, c.c0 = (c.sb(n, [P, D]) for n in ("fb2", "b3", "bias", "c0"))
        c.bu = c.sb("bu", [P, H3])
        c.ident, c.identb, c.first = c.sb("ident", [P, P]), c.sb("identb", [P, P], BF16), c.sb("first", [P, P])
        c.ltri, c.ones = c.sb("ltri", [P, P], BF16), c.sb("ones", [P, P], BF16)
        c.window, c.digits = c.sb("window", [P, 2 * P], BF16), c.sb("digits", [P, 256], BF16)
        c.digits_i, c.end = c.sb("digits_i", [P, 256], I32), c.sb("end", [P, 1])
        c.consts, c.zero_row = c.sb("consts", [P, 16]), c.sb("zero_row", [P, D])
        c.one_row, c.bias_row = c.sb("one_row", [1, P]), c.sb("bias_row", [1, 2 * D])
        c.x2_dram = dram("x2_rows", (N, D))
        c.absent = c.sb("absent", [P, N // 125], I32)
        c.pay_d, c.pay_s = c.sb("pay_d", [P, T, 4], I32), c.sb("pay_s", [P, T, 4], I32)
        sides = {}
        for s, pay in (("d", c.pay_d), ("s", c.pay_s)):
            sides[s] = {"pay": pay, "key": c.sb(s + "_key", [P, T + 1]), "key_end": c.sb(s + "_key_end", [P, T]),
                        "index": c.sb(s + "_index", [P, GROUPS, 4, K4], I32),
                        "keys": dram(s + "_keys", (EP + 2,)), "w": c.sb(s + "_w", [P, T]), "w8": c.sb(s + "_w8", [P, T]),
                        "cuts": dram(s + "_cuts", (EP + 1,)),
                        "rows": dram(s + "_sorted", (EP, 4), I32), "rows0": dram(s + "_half_sorted", (EP, 4), I32)}
            sides[s]["columns"] = [(1, N - 1), (0, N - 1), (3, E - 1)]
        c.d, c.s = sides["d"], sides["s"]
        c.cutoff, c.s_place = c.sb("cutoff", [P, T]), c.sb("s_place", [P, GROUPS, K4], I32)
        setup_phase(c, a)
        if stop == "setup": return c
        payload_phase(c, a)
        for s in ("d", "s"):
            sort_pass(c, s + "0_", sides[s]["pay"], 0, sides[s]["rows0"])
            sort_pass(c, s + "1_", sides[s]["pay"], 8, sides[s]["rows"])
            index_phase(c, s + "_ix_", sides[s])
        if stop == "sort": return c
        node_pass_one(c, a)
        cosine_phase(c)
        if stop == "p1": return c
        filter_layer(c, a)
        if stop == "l0": return c
        place_phase(c)
        propagation_round(c, 1)
        if stop == "l11": return c
        propagation_round(c, 2)
        propagation_round(c, 3)
        if stop == "l1": return c
        node_pass_two(c)
        if stop == "p2": return c
        attention_layer(c, 2)
        attention_layer(c, 3)


_INS = ["x", "src", "dst", "edge_attr_64", "edge_weight", "L0_gnn_fw1", "L0_gnn_fb1", "L0_gnn_fw2", "L0_gnn_fb2",
        "L0_gnn_w1", "L0_gnn_w2", "L0_gnn_b2", "L0_gnn_w3", "L0_gnn_b3", "L2_gnn_W", "L2_gnn_att_src",
        "L2_gnn_att_dst", "L2_gnn_bias", "L3_gnn_W_u", "L3_gnn_b_u", "L3_gnn_W_v"]


def kernel(**inputs):
    import numpy as np
    import concourse.bacc as bacc
    from concourse.bass_utils import run_bass_kernel_spmd

    nc = bacc.Bacc("TRN2", target_bir_lowering=False, num_devices=1)
    arrays, given = {}, {}
    for name in _INS:
        array = np.ascontiguousarray(inputs[name])
        arrays[name + "_in"] = array
        given[name] = nc.dram_tensor(name + "_in", array.shape, mybir.dt.from_np(array.dtype), kind="ExternalInput").ap()
    out = nc.dram_tensor("out", (N, D), F32, kind="ExternalOutput").ap()
    build(nc, {short: given[name] for short, name in _NAMES.items()}, out)
    result = run_bass_kernel_spmd(nc, [arrays], core_ids=[0])
    return result.results[0]["out"]
```

```python
from contextlib import ExitStack, contextmanager
import math

import concourse.bass as bass
from concourse import mybir

F32 = mybir.dt.float32
BF16 = mybir.dt.bfloat16
I32 = mybir.dt.int32
ALU = mybir.AluOpType
ACT = mybir.ActivationFunctionType

P = 128
N, D = 50000, 256
E = 25000
BASIS = 64
K4 = 4
ROWS = K4 * P
GROUPS = 50
T = GROUPS * K4
EP = T * P
EDGE_PARTS = E // T
HALVES = ((0, 26), (26, 24))
NG = -(-N // ROWS)
PAD_KEY = 65535
FAR = 100000.0
LOW = -1.0e30
OTHER, OWN, EDGE, LAST = range(4)
LN_EPS = 1e-5
NORM_EPS2 = 1e-24
NORM_SCALE = 2.0 ** 20
LOG_EXP_SET = 6
H2, H3 = 4, 8


class Step:

    def __init__(self, r, unroll, off):
        self.g, self.r, self.unroll, self.off = r * unroll + off, r, unroll, off

    def slot(self, n):
        return self.off % n

    def turn(self, n):
        return self.r * (self.unroll // n) + self.off // n

    def early(self, n):
        return isinstance(self.g, int) and self.g < n

    def last(self, n):
        return isinstance(self.g, int) and self.g == n - 1


def skewed(eng, n, stages, unroll=4, start=0):
    lag = max(x for x, _ in stages)
    a = -(-(start + lag + unroll) // unroll) * unroll
    b = a + max(0, (start + n - 1 - a) // unroll) * unroll

    def iteration(r, off, peeled):
        for x, fn in stages:
            if not peeled or start <= off - x < start + n:
                fn(Step(r, unroll, off - x))

    for j in range(start, a):
        iteration(0, j, True)
    with eng.Fori(a // unroll, b // unroll) as r:
        for off in range(unroll):
            iteration(r, off, False)
    for j in range(b, start + n + lag):
        iteration(0, j, True)


def node_base(g):
    return N - ROWS if isinstance(g, int) and g == NG - 1 else g * ROWS


def node_rows(dram, g):
    return dram[bass.ds(node_base(g), ROWS), :].rearrange("(p k) d -> p k d", k=K4)


def edge_rows(dram, g, width=D):
    return dram[bass.ds(g * ROWS, ROWS), :].rearrange("(k p) d -> p k d", p=P)


class Core:

    def __init__(self, nc, ctx):
        self.nc, self.ctx = nc, ctx

    def sb(self, name, shape, dt=F32, ctx=None):
        t = (ctx or self.ctx).enter_context(self.nc.sbuf_tensor(name, shape, dt))
        return t

    def ps(self, name, shape, dt=F32, ctx=None):
        return (ctx or self.ctx).enter_context(self.nc.psum_tensor(name, shape, dt))

    def sem(self, name):
        self.phase_sems.append(self.nc.alloc_semaphore(name))
        return self.phase_sems[-1]

    @contextmanager
    def phase(self):
        self.phase_sems = []
        with ExitStack() as ctx:
            yield ctx
        self.nc.clear_and_free_semaphores(self.phase_sems)
        self.nc.all_engine_barrier()


def setup_phase(c, a):
    nc = c.nc
    with c.phase() as ctx:
        nat = {n: c.sb("nat_" + n, [P, 2, D], ctx=ctx) for n in ("fw2", "w1", "w2", "w3")}
        nat["fw1"] = c.sb("nat_fw1", [P, 2, BASIS], ctx=ctx)
        heads = c.sb("heads", [16, D], ctx=ctx)
        att = c.sb("att", [P, 2, 2], ctx=ctx)
        blocks = c.sb("blocks", [P, 2, 2 * H2], ctx=ctx)
        wgT = c.sb("wgT", [P, 2, D], ctx=ctx)
        b2s = c.sb("b2s", [P, 4, 2], ctx=ctx)
        bias_row, parts_row = c.sb("bias_row", [1, 3, D], ctx=ctx), c.sb("parts_row", [1, 3, 2, D], BF16, ctx=ctx)
        tp = [c.ps(f"tp{i}", [P, 512], ctx=ctx) for i in range(4)]
        loaded, masks, blocked = c.sem("w_loaded"), c.sem("w_masks"), c.sem("w_blocks")
        turned, copied = c.sem("w_turned"), c.sem("w_copied")
        soft, soft2, base = c.sem("w_soft"), c.sem("w_soft2"), c.sem("w_base")
        init, zeroed, parted = c.sem("w_init"), c.sem("w_zeroed"), c.sem("w_parted")
        block = ctx.enter_context(nc.Block())
        loads = [(nat[n][:, :, :], a[n].rearrange("(c p) i -> p c i", p=P)) for n in nat]
        loads += [(c.wg[:, :, 0:D], a["W"].rearrange("(c p) i -> p c i", p=P)),
                  (heads[0:8, :], a["W_u"]), (heads[8:16, :], a["W_v"]),
                  (c.fb1[:, :], a["fb1"].rearrange("(c p) -> p c", p=P)),
                  (c.b2[:, :], a["b2"].rearrange("(c p) -> p c", p=P)),
                  (att[:, :, 0], a["att_src"].rearrange("(c h) d -> (h d) c", h=2)),
                  (att[:, :, 1], a["att_dst"].rearrange("(c h) d -> (h d) c", h=2)),
                  (c.fb2[:, :], a["fb2"].rearrange("(o d) -> o d", o=1).to_broadcast([P, D])),
                  (c.b3[:, :], a["b3"].rearrange("(o d) -> o d", o=1).to_broadcast([P, D])),
                  (c.bias[:, :], a["bias"].rearrange("(o d) -> o d", o=1).to_broadcast([P, D])),
                  (bias_row[0:1, 0, :], a["bias"].rearrange("(o d) -> o d", o=1)),
                  (c.bu[:, :], a["b_u"].rearrange("(o d) -> o d", o=1).to_broadcast([P, H3]))]
        turns = []
        for n, to in (("fw2", c.fw2T), ("w1", c.w1T), ("w2", c.w2T), ("w3", c.w3T)):
            for i in range(2):
                turns.append(([nat[n][:, o, i * P:(i + 1) * P] for o in range(2)], P, to[:, i, :], P))
        for i in range(2):
            turns.append(([c.wg[:, o, i * P:(i + 1) * P] for o in range(2)], P, wgT[:, i, :], P))
        turns.append(([nat["fw1"][:, o, :] for o in range(2)], P, c.fw1T[:, :], BASIS))
        for i in range(2):
            turns.append(([heads[:, i * P:(i + 1) * P]], 16, c.wuv[:, i, :], P))

        @block.sync
        def _(sp):
            for to, frm in loads:
                sp.dma_start(to, frm, allow_slow_non_contiguous=True).then_inc(loaded, 16)
            sp.wait_ge(zeroed, 3)
            sp.dma_start(c.h1_dram[EP:EP + 1, :], c.zero_row[0:1, :]).then_inc(init, 16)
            sp.dma_start(c.h2_dram[EP:EP + 1, :], c.zero_row[0:1, :]).then_inc(init, 16)
            sp.dma_start(c.place_dram.rearrange("(p j) o -> p (j o)", p=125), c.absent[0:125, :]).then_inc(init, 16)
            sp.wait_ge(parted, 8)
            sp.dma_start(c.bias_parts[:, :], parts_row[0:1, :, :, :].rearrange("o n b d -> o n (b d)")).then_inc(init, 16)
            sp.wait_ge(init, 64)

        @block.gpsimd
        def _(pool):
            pool.memset(c.ident[:, :], 0.0).then_inc(masks, 1)
            pool.memset(c.ltri[:, :], 1.0).then_inc(masks, 1)
            pool.memset(c.window[:, :], 0.0).then_inc(masks, 1)
            pool.memset(c.ones[:, :], 1.0).then_inc(masks, 1)
            pool.memset(c.first[:, :], 0.0).then_inc(masks, 1)
            pool.memset(c.end[:, :], 0.0).then_inc(masks, 1)
            pool.memset(c.zero_row[:, :], 0.0).then_inc(zeroed, 1)
            pool.memset(c.absent[:, :], EP).then_inc(zeroed, 1)
            pool.iota(c.digits_i[:, :], pattern=[[1, 256]], base=0, channel_multiplier=0).then_inc(zeroed, 1)
            pool.wait_ge(masks, 6)
            pool.affine_select(out=c.ident[:, :], in_=c.ident[:, :], compare_op=ALU.not_equal, fill=1.0,
                               base=0, pattern=[[-1, P]], channel_multiplier=1).then_inc(masks, 1)
            pool.affine_select(out=c.ltri[:, :], in_=c.ltri[:, :], compare_op=ALU.is_gt, fill=0.0,
                               base=0, pattern=[[1, P]], channel_multiplier=-1).then_inc(masks, 1)
            pool.memset(c.window[:, P:P + 1], 1.0).then_inc(masks, 1)
            pool.memset(c.first[0:1, :], 1.0).then_inc(masks, 1)
            pool.affine_select(out=c.end[:, :], in_=c.end[:, :], compare_op=ALU.not_equal, fill=1.0,
                               base=-(P - 1), pattern=[[0, 1]], channel_multiplier=1).then_inc(masks, 1)
            pool.wait_ge(masks, 11)
            pool.tensor_copy(c.identb[:, :], c.ident[:, :]).then_inc(masks, 1)

        @block.vector
        def _(dve):
            dve.memset(blocks[:, :, :], 0.0).then_inc(blocked, 1)
            dve.memset(c.consts[:, 0:1], LN_EPS).then_inc(blocked, 1)
            dve.memset(c.consts[:, 1:2], math.log(1.25)).then_inc(blocked, 1)
            dve.memset(c.consts[:, 2:3], 0.5 * math.log(NORM_SCALE)).then_inc(blocked, 1)
            dve.memset(c.consts[:, 3:4], math.pi / 2).then_inc(blocked, 1)
            dve.memset(c.consts[:, 4:5], 0.5)
            dve.memset(c.consts[:, 6:7], -NORM_EPS2 * NORM_SCALE)
            dve.memset(c.consts[:, 7:8], NORM_EPS2 * NORM_SCALE)
            dve.memset(c.consts[:, 8:9], LN_EPS ** 2)
            dve.memset(c.consts[:, 5:6], 0.5 * math.log(NORM_SCALE) + math.log(0.25)).then_inc(blocked, 1)
            dve.wait_ge(zeroed, 3)
            dve.tensor_copy(c.digits[:, :], c.digits_i[:, :]).then_inc(blocked, 1)
            dve.wait_ge(loaded, 16 * len(loads))
            dve.wait_ge(blocked, 7)
            for which in range(2):
                for h in range(H2):
                    r = slice(64 * (h % 2), 64 * (h % 2) + 64)
                    dve.tensor_copy(blocks[r, h // 2, which * H2 + h:which * H2 + h + 1],
                                    att[r, h // 2, which:which + 1]).then_inc(blocked, 1)
            for i in range(3):
                for b in range(2):
                    dve.tensor_copy(parts_row[0:1, i, b, :], bias_row[0:1, i, :]).then_inc(parted, 1)
                if i < 2:
                    dve.wait_ge(parted, 3 * i + 2)
                    dve.tensor_tensor(bias_row[0:1, i + 1, :], bias_row[0:1, i, :], parts_row[0:1, i, 0, :], ALU.subtract)\
                       .then_inc(parted, 1)
                    dve.wait_ge(parted, 3 * i + 3)
            for n, (parts, wide, to, rows) in enumerate(turns):
                dve.wait_ge(turned, n + 1)
                dve.tensor_copy(to, tp[n % 4][0:rows, 0:wide * len(parts)]).then_inc(copied, 1)
            n = len(turns)
            for i in range(2):
                dve.wait_ge(turned, n + i + 1)
                dve.tensor_copy(c.wg[:, i, D:D + 2 * H2], tp[(n + i) % 4][:, 0:2 * H2]).then_inc(copied, 1)
            dve.tensor_scalar(b2s[:, 0, :], c.b2[:, :], 0.0, None, ALU.max).then_inc(soft2, 1)
            dve.wait_ge(soft2, 1)
            dve.wait_ge(soft, 3)
            dve.tensor_tensor(b2s[:, 0, :], b2s[:, 0, :], b2s[:, 3, :], ALU.add).then_inc(soft2, 1)
            dve.wait_ge(base, 1)
            dve.tensor_tensor(c.c0[:, :], tp[(n + 2) % 4][:, 0:D], c.b3[:, :], ALU.add).then_inc(base, 1)

        @block.scalar
        def _(act):
            log_exp_tables(nc, act)
            act.wait_ge(loaded, 16 * len(loads))
            act.wait_ge(blocked, 6)
            act.activation(b2s[:, 1, :], c.b2[:, :], ACT.Abs).then_inc(soft, 1)
            act.wait_ge(soft, 1)
            act.activation(b2s[:, 2, :], b2s[:, 1, :], ACT.Exp, scale=-1.0).then_inc(soft, 1)
            act.wait_ge(soft, 2)
            act.activation(b2s[:, 3, :], b2s[:, 2, :], ACT.Ln, bias=c.consts[:, 4:5], scale=0.5).then_inc(soft, 1)

        @block.tensor
        def _(pe):
            pe.wait_ge(masks, 12)
            pe.wait_ge(loaded, 16 * len(loads))
            for n, (parts, wide, to, rows) in enumerate(turns):
                if n >= 4:
                    pe.wait_ge(copied, n - 3)
                for o, part in enumerate(parts):
                    last = pe.transpose(tp[n % 4][0:rows, o * wide:(o + 1) * wide], part, c.ident[0:wide, 0:wide])
                last.then_inc(turned, 1)
            n = len(turns)
            pe.wait_ge(copied, n)
            pe.wait_ge(blocked, 7 + 2 * H2)
            for i in range(2):
                for o in range(2):
                    last = pe.matmul(tp[(n + i) % 4][:, 0:2 * H2], wgT[:, o, i * P:(i + 1) * P], blocks[:, o, :],
                                     start=(o == 0), stop=(o == 1))
                last.then_inc(turned, 1)
            pe.wait_ge(soft2, 2)
            for o in range(2):
                last = pe.matmul(tp[(n + 2) % 4][:, 0:D], b2s[:, 0, o:o + 1].to_broadcast([P, P]), c.w3T[:, o, :],
                                 start=(o == 0), stop=(o == 1))
            last.then_inc(base, 1)


def payload_phase(c, a):
    nc = c.nc
    with c.phase() as ctx:
        dst = c.sb("pl_dst", [P, T], I32, ctx=ctx)
        src = c.sb("pl_src", [P, T], I32, ctx=ctx)
        w = c.sb("pl_w", [P, T], ctx=ctx)
        num = c.sb("pl_num", [P, T], I32, ctx=ctx)
        pad = c.sb("pl_pad", [P, 1], ctx=ctx)
        ready, loaded, made, numbered = c.sem("pl_ready"), c.sem("pl_loaded"), c.sem("pl_made"), c.sem("pl_numbered")
        block = ctx.enter_context(nc.Block())

        @block.sync
        def _(sp):
            sp.wait_ge(ready, 3)
            sp.dma_start(dst[0:EDGE_PARTS, :], a["dst"].rearrange("(p t) -> p t", t=T)).then_inc(loaded, 16)
            sp.dma_start(src[0:EDGE_PARTS, :], a["src"].rearrange("(p t) -> p t", t=T)).then_inc(loaded, 16)
            sp.dma_start(w[0:EDGE_PARTS, :], a["ew"].rearrange("(p t) -> p t", t=T)).then_inc(loaded, 16)

        @block.gpsimd
        def _(pool):
            pool.iota(num[:, :], pattern=[[1, T]], base=0, channel_multiplier=T).then_inc(numbered, 1)
            pool.memset(pad[:, :], float(PAD_KEY)).then_inc(numbered, 1)
            pool.wait_ge(numbered, 2)
            pool.affine_select(out=pad[:, :], in_=pad[:, :], compare_op=ALU.is_ge, fill=0.0,
                               base=-EDGE_PARTS, pattern=[[0, 1]], channel_multiplier=1).then_inc(numbered, 1)

        @block.vector
        def _(dve):
            dve.memset(dst[:, :], 0).then_inc(ready, 1)
            dve.memset(src[:, :], 0).then_inc(ready, 1)
            dve.memset(w[:, :], 0.0).then_inc(ready, 1)
            dve.wait_ge(numbered, 3)
            dve.tensor_scalar(num[:, :], num[:, :], float(E - 1), None, ALU.min).then_inc(made, 1)
            dve.wait_ge(loaded, 48)
            dve.wait_ge(made, 1)
            for table, key, other in ((c.pay_d, dst, src), (c.pay_s, src, dst)):
                dve.tensor_scalar(table[:, :, 0], key[:, :], pad[:, 0:1], None, ALU.max)
                dve.tensor_copy(table[:, :, 1], other[:, :])
                dve.tensor_copy(table[:, :, :].bitcast(F32)[:, :, 2], w[:, :])
                dve.tensor_copy(table[:, :, 3], num[:, :]).then_inc(made, 1)


def sort_pass(c, name, pay, shift, out_dram):
    nc = c.nc
    with c.phase() as ctx:
        digit_i = c.sb(name + "digit_i", [P, T], I32, ctx=ctx)
        digit = c.sb(name + "digit", [P, T], ctx=ctx)
        hot = c.sb(name + "hot", [P, 2 * K4, 256], BF16, ctx=ctx)
        junk = c.sb(name + "junk", [P, 2 * K4, 256], BF16, ctx=ctx)
        counts = c.sb(name + "counts", [P, 2, 256], BF16, ctx=ctx)
        zeros = c.sb(name + "zeros", [P, 256], ctx=ctx)
        total = c.sb(name + "total", [P, 256], ctx=ctx)
        base = c.sb(name + "base", [P, 256], ctx=ctx)
        ahead = c.sb(name + "ahead", [P, 2, 256], ctx=ctx)
        ahead_hi = c.sb(name + "ahead_hi", [P, 2, 256], BF16, ctx=ctx)
        ahead_lo = c.sb(name + "ahead_lo", [P, 2, 256], BF16, ctx=ctx)
        place = c.sb(name + "place", [P, 2, K4], ctx=ctx)
        at = c.sb(name + "at", [P, 2, K4], I32, ctx=ctx)
        rows = c.sb(name + "rows", [P, 2, K4, 4], I32, ctx=ctx)
        tab = c.ps(name + "tab", [P, 2, 512], ctx=ctx)
        rank = c.ps(name + "rank", [P, 2 * K4, 256], ctx=ctx)
        digits_ready, hot_made, hot_counted = c.sem(name + "digits"), c.sem(name + "hot_made"), c.sem(name + "hot_counted")
        tables = c.sem(name + "tables")
        sums, heads, ranked, read = c.sem(name + "sums"), c.sem(name + "heads"), c.sem(name + "ranked"), c.sem(name + "read")
        placed, copied, back = c.sem(name + "placed"), c.sem(name + "copied"), c.sem(name + "back")
        issuing = c.sem(name + "issuing")
        hot2, sent = c.sem(name + "hot2"), [c.sem(f"{name}sent{u}") for u in range(2)]
        block = ctx.enter_context(nc.Block())

        def make_hot(dve, t, made):
            for k in range(K4):
                last = dve.tensor_scalar(hot[:, t.slot(2) * K4 + k, :], c.digits[:, :], digit[:, bass.ds(t.g * K4 + k, 1)],
                                         None, ALU.is_equal)
            last.then_inc(made, 1)

        @block.vector
        def _(dve):
            dve.memset(zeros[:, :], 0.0).then_inc(digits_ready, 1)
            dve.tensor_scalar(digit_i[:, :], pay[:, :, 0], shift, 255, ALU.logical_shift_right, ALU.bitwise_and)\
               .then_inc(digits_ready, 1)
            dve.wait_ge(digits_ready, 2)
            dve.tensor_copy(digit[:, :], digit_i[:, :]).then_inc(digits_ready, 1)
            dve.wait_ge(digits_ready, 3)

            def count(t):
                if not t.early(2):
                    dve.wait_ge(hot_counted, t.g - 1)
                make_hot(dve, t, hot_made)
            for start, n in HALVES:
                skewed(dve, n, [(0, count)], 2, start)
            dve.wait_ge(tables, 1)
            dve.tensor_copy(counts[:, :, :], tab[:, :, 0:256]).then_inc(tables, 1)
            dve.wait_ge(sums, 1)
            dve.tensor_copy(total[:, :], rank[:, 0, :]).then_inc(heads, 1)
            dve.wait_ge(heads, 1)
            dve.tensor_tensor_scan(base[:, :], total[:, :], zeros[:, :], 0.0, ALU.add, ALU.add).then_inc(heads, 1)
            dve.wait_ge(heads, 2)
            dve.tensor_tensor(base[:, :], base[:, :], total[:, :], ALU.subtract).then_inc(heads, 1)
            dve.wait_ge(heads, 3)
            dve.wait_ge(sums, 2)
            for h in range(2):
                dve.tensor_tensor(ahead[:, h, :], rank[:, 2 + 2 * h, :], base[:, :], ALU.add).then_inc(heads, 1)
            dve.wait_ge(heads, 5)
            dve.tensor_copy(ahead_hi[:, :, :], ahead[:, :, :]).then_inc(heads, 1)
            dve.wait_ge(heads, 6)
            dve.tensor_tensor(ahead_lo[:, :, :], ahead[:, :, :], ahead_hi[:, :, :], ALU.subtract).then_inc(heads, 1)

            def mark(t):
                if not t.early(2):
                    dve.wait_ge(read, t.g - 1)
                make_hot(dve, t, hot2)

            def positions(t):
                u = t.slot(2)
                dve.wait_ge(ranked, t.g + 1)
                for k in range(K4):
                    last = dve.scalar_tensor_tensor(
                        out=junk[:, u * K4 + k, :], in0=hot[:, u * K4 + k, :], scalar=1.0, in1=rank[:, u * K4 + k, :],
                        op0=ALU.mult, op1=ALU.mult, accum_out=place[:, u, k:k + 1])
                last.then_inc(read, 1)
                dve.wait_ge(read, t.g + 1)
                if not t.early(2):
                    dve.wait_ge(sent[u], t.turn(2) * 16 * K4)
                dve.tensor_copy(at[:, u, :], place[:, u, :]).then_inc(placed, 1)
            dve.wait_ge(hot_counted, GROUPS)
            skewed(dve, GROUPS, [(0, mark), (1, positions)], 2)

        @block.tensor
        def _(pe):
            for h, (start, n) in enumerate(HALVES):
                pe.matmul(tab[:, h, 0:256], c.window[:, 0:P], c.window[:, 0:256], start=True, stop=False)

                def count(t):
                    pe.wait_ge(hot_made, t.g + 1)
                    for k in range(K4):
                        last = pe.matmul(tab[:, h, 0:256], c.window[:, bass.ds((t.g - start) * (-K4) + P - k, P)],
                                         hot[:, t.slot(2) * K4 + k, :], start=False, stop=False)
                    last.then_inc(hot_counted, 1)
                skewed(pe, n, [(0, count)], 2, start)
                last = pe.matmul(tab[:, h, 0:256], c.window[:, 0:P], c.window[:, 0:256], start=False, stop=True)
            last.then_inc(tables, 1)
            pe.wait_ge(tables, 2)
            for h in range(2):
                last = pe.matmul(rank[:, 0, :], c.ones[:, :], counts[:, h, :], start=(h == 0), stop=(h == 1))
            last.then_inc(sums, 1)
            pe.matmul(rank[:, 2, :], c.ltri[:, :], counts[:, 0, :], start=True, stop=True)
            pe.matmul(rank[:, 4, :], c.ltri[:, :], counts[:, 1, :], start=True, stop=False)
            pe.matmul(rank[:, 4, :], c.ones[:, :], counts[:, 0, :], start=False, stop=True).then_inc(sums, 1)
            pe.wait_ge(heads, 7)
            for h, (start, n) in enumerate(HALVES):
                def rank_step(t):
                    pe.wait_ge(hot2, t.g + 1)
                    if not t.early(2):
                        pe.wait_ge(read, t.g - 1)
                    for k in range(K4):
                        out = rank[:, t.slot(2) * K4 + k, :]
                        pick = c.identb[:, bass.ds((t.g - start) * K4 + k, 1)].to_broadcast([P, P])
                        pe.matmul(out, c.ltri[:, :], hot[:, t.slot(2) * K4 + k, :], start=True, stop=False)
                        pe.matmul(out, pick, ahead_hi[:, h, :], start=False, stop=False)
                        last = pe.matmul(out, pick, ahead_lo[:, h, :], start=False, stop=True)
                    last.then_inc(ranked, 1)
                skewed(pe, n, [(0, rank_step)], 2, start)

        @block.gpsimd
        def _(pool):
            def send(t):
                u = t.slot(2)
                if not t.early(2):
                    pool.wait_ge(sent[u], t.turn(2) * 16 * K4)
                    pool.sem_inc(issuing, 1)
                pool.tensor_copy(rows[:, u, :, :], pay[:, bass.ds(t.g * K4, K4), :]).then_inc(copied, 1)
                pool.wait_ge(copied, t.g + 1)
                pool.wait_ge(placed, t.g + 1)
                pool.sem_inc(issuing, 1)
                for k in range(K4):
                    pool.indirect_dma_start(out_dram[:, :], bass.IndirectOffsetOnAxis(ap=at[:, u, k:k + 1], axis=0),
                                            rows[:, u, k, :], None).then_inc(sent[u], 16)
            skewed(pool, GROUPS, [(0, send)], 2)

        @block.sync
        def _(sp):
            for u in range(2):
                sp.wait_ge(sent[u], GROUPS // 2 * 16 * K4)
            sp.dma_start(pay[:, :, :], out_dram.rearrange("(t p) c -> p t c", p=P)).then_inc(back, 16)
            sp.wait_ge(back, 16)


def index_phase(c, name, side):
    nc = c.nc
    pay, key, keys_dram = side["pay"], side["key"], side["keys"]
    with c.phase() as ctx:
        keyT = c.sb(name + "keyT", [P, 2, P], ctx=ctx)
        nextT = c.sb(name + "nextT", [P, 2, P], ctx=ctx)
        sentinels = c.sb(name + "sentinels", [1, 2], ctx=ctx)
        turn = c.ps(name + "turn", [P, 2, 512], ctx=ctx)
        turn2 = c.ps(name + "turn2", [P, 2, 512], ctx=ctx)
        keyed, turned, keyedT, stored = c.sem(name + "keyed"), c.sem(name + "turned"), c.sem(name + "keyedT"), c.sem(name + "stored")
        cuts = c.sb(name + "cuts", [P, 2, P], ctx=ctx)
        loaded, marked, back = c.sem(name + "loaded"), c.sem(name + "marked"), c.sem(name + "ix_back")
        block = ctx.enter_context(nc.Block())
        half = T // 2

        @block.vector
        def _(dve):
            dve.memset(sentinels[0:1, 0:1], -1.0).then_inc(keyed, 1)
            dve.memset(sentinels[0:1, 1:2], -2.0).then_inc(keyed, 1)
            dve.memset(key[:, 0:1], -1.0).then_inc(keyed, 1)
            dve.tensor_copy(key[:, 1:T + 1], pay[:, :, 0]).then_inc(keyed, 1)
            for kind, (col, top) in enumerate(side["columns"]):
                dve.tensor_scalar(side["index"][:, :, kind, :], pay[:, :, col].rearrange("p (g k) -> p g k", k=K4),
                                  float(top), None, ALU.min)
            dve.wait_ge(keyed, 4)
            dve.tensor_scalar(side["key_end"][:, :], key[:, 0:T], 3.0, c.end[:, 0:1], ALU.add, ALU.mult).then_inc(keyed, 1)
            dve.wait_ge(keyed, 5)
            dve.tensor_scalar(side["key_end"][:, :], side["key_end"][:, :], 3.0, None, ALU.subtract)
            dve.tensor_copy(side["w"][:, :], pay[:, :, :].bitcast(F32)[:, :, 2])
            dve.tensor_scalar(side["w8"][:, :], pay[:, :, :].bitcast(F32)[:, :, 2], 0.8, None, ALU.mult)
            dve.wait_ge(turned, 1)
            dve.tensor_copy(keyT[0:half, :, :], turn[0:half, :, 0:P]).then_inc(keyedT, 1)
            dve.wait_ge(loaded, 16)
            dve.tensor_tensor(nextT[0:half, :, :], nextT[0:half, :, :], keyT[0:half, :, :], ALU.is_equal).then_inc(marked, 1)
            dve.wait_ge(marked, 1)
            dve.tensor_scalar(cuts[0:half, :, :], nextT[0:half, :, :], -LOW, LOW, ALU.mult, ALU.add).then_inc(marked, 1)
            dve.wait_ge(marked, 2)
            dve.scalar_tensor_tensor(out=nextT[0:half, :, :], in0=nextT[0:half, :, :], scalar=FAR, in1=keyT[0:half, :, :],
                                     op0=ALU.mult, op1=ALU.add).then_inc(marked, 1)
            dve.wait_ge(back, 1)
            for h in range(2):
                dve.tensor_copy(side["index"][:, h * GROUPS // 2:(h + 1) * GROUPS // 2, LAST, :],
                                turn2[:, h, 0:half].rearrange("p (g k) -> p g k", k=K4))

        @block.tensor
        def _(pe):
            pe.wait_ge(keyed, 4)
            for h in range(2):
                last = pe.transpose(turn[0:half, h, 0:P], key[:, 1 + h * half:1 + (h + 1) * half], c.ident[:, :])
            last.then_inc(turned, 1)
            pe.wait_ge(marked, 3)
            for h in range(2):
                last = pe.transpose(turn2[:, h, 0:half], nextT[0:half, h, :], c.ident[0:half, 0:half])
            last.then_inc(back, 1)

        @block.sync
        def _(sp):
            sp.wait_ge(keyedT, 1)
            sp.dma_start(keys_dram[1:EP + 1].rearrange("(h t p) -> t h p", h=2, p=P), keyT[0:half, :, :]).then_inc(stored, 16)
            sp.dma_start(keys_dram[0:1].rearrange("(o n) -> o n", o=1), sentinels[0:1, 0:1]).then_inc(stored, 16)
            sp.dma_start(keys_dram[EP + 1:EP + 2].rearrange("(o n) -> o n", o=1), sentinels[0:1, 1:2]).then_inc(stored, 16)
            sp.wait_ge(stored, 48)
            sp.dma_start(nextT[0:half, :, :], keys_dram[2:EP + 2].rearrange("(h t p) -> t h p", h=2, p=P)).then_inc(loaded, 16)
            sp.wait_ge(marked, 2)
            sp.dma_start(side["cuts"][1:EP + 1].rearrange("(h t p) -> t h p", h=2, p=P), cuts[0:half, :, :]).then_inc(stored, 16)
            sp.dma_start(side["cuts"][0:1].rearrange("(o n) -> o n", o=1), sentinels[0:1, 0:1]).then_inc(stored, 16)
            sp.wait_ge(stored, 80)


def signals(c, prefix):
    made = {}

    def get(name):
        if name not in made:
            made[name] = c.sem(prefix + name)
        return made[name]
    return get


def over_tiles(row):
    return row.rearrange("p (o d) -> p o d", o=1).to_broadcast([row.shape[0], K4, row.shape[1]])


def along(col):
    return col.rearrange("p (k o) -> p k o", o=1).to_broadcast([col.shape[0], K4, P])


def log_exp_tables(nc, act):
    act.add_instruction(mybir.InstLoadActFuncSet(name=nc.get_next_instruction_name(), act_func_set_id=LOG_EXP_SET,
                                                 ins=[], outs=[]))


def row_stats(dve, x, stats, mv, s, what, g):
    for k in range(K4):
        last = dve.bn_stats(stats[:, k, :], x[:, k, :])
    last.then_inc(s(what + "_stats"), 1)
    dve.wait_ge(s(what + "_stats"), g + 1)
    dve.sem_inc(s(what + "_held"), 1)
    for k in range(K4):
        last = dve.bn_aggr(mv[:, k, :], stats[:, k, :])
    last.then_inc(s(what + "_var"), 1)


def row_scale(act, c, mv, rs, s, what, g, bias=0.0):
    act.wait_ge(s(what + "_var"), g + 1)
    act.activation(rs, mv[:, :, 1], ACT.Ln, bias=c.consts[:, 0:1]).then_inc(s(what + "_log"), 1)
    act.wait_ge(s(what + "_log"), g + 1)
    act.activation(rs, rs, ACT.Exp, bias=bias, scale=-0.5).then_inc(s(what + "_scale"), 1)


def newton_part(dve, n, root, value, scalar, half, work, done, g):
    if n:
        dve.wait_ge(done, 3 * g + n)
    if n == 0:
        ins = dve.scalar_tensor_tensor(out=work, in0=value, scalar=scalar, in1=root, op0=ALU.add, op1=ALU.mult)
    elif n == 1:
        ins = dve.scalar_tensor_tensor(out=work, in0=work, scalar=half, in1=root, op0=ALU.mult, op1=ALU.mult)
    else:
        ins = dve.scalar_tensor_tensor(out=root, in0=work, scalar=1.5, in1=root, op0=ALU.add, op1=ALU.mult)
    ins.then_inc(done, 1)


def newton(dve, root, done, g):
    for n in range(3):
        newton_part(dve, n, *root, done, g)
    dve.wait_ge(done, 3 * g + 3)


def variance_root(rs, mv, work):
    return rs, mv[:, :, 1], LN_EPS, -0.5, work


def norm_root(rn, guarded, work):
    return rn, guarded, NORM_EPS2 * NORM_SCALE, -0.5 / NORM_SCALE, work


def row_apply(dve, out, x, mv, rs, s, what, g, done, work=None):
    dve.wait_ge(s(what + "_scale"), g + 1)
    if work is not None:
        newton(dve, variance_root(rs, mv, work), s(what + "_newton"), g)
    for k in range(K4):
        last = dve.tensor_scalar(out[:, k, :], x[:, k, :], mv[:, k, 0:1], rs[:, k:k + 1], ALU.subtract, ALU.mult)
    last.then_inc(s(done), 1)


def row_shift(dve, off, mv, rs, s, what, g):
    dve.wait_ge(s(what + "_scale"), g + 1)
    dve.scalar_tensor_tensor(out=off, in0=mv[:, :, 0], scalar=-1.0, in1=rs, op0=ALU.mult, op1=ALU.mult)\
       .then_inc(s(what + "_shift"), 1)


def row_apply_act(act, out, x, off, rs, s, what, g, done):
    act.wait_ge(s(what + "_shift"), g + 1)
    for k in range(K4):
        last = act.activation(out[:, k, :], x[:, k, :], ACT.Identity, bias=off[:, k:k + 1], scale=rs[:, k:k + 1])
    last.then_inc(s(done), 1)


def inverse_norm(act, c, ss, guarded, rn, s, g, bias):
    act.activation(guarded, ss, ACT.Relu, scale=NORM_SCALE, bias=c.consts[:, 6:7]).then_inc(s("rn_guard"), 1)
    act.wait_ge(s("rn_guard"), g + 1)
    act.activation(rn, guarded, ACT.Ln, bias=c.consts[:, 7:8]).then_inc(s("rn_log"), 1)
    act.wait_ge(s("rn_log"), g + 1)
    act.activation(rn, rn, ACT.Exp, scale=-0.5, bias=bias).then_inc(s("rn"), 1)


def node_pass_one(c, a):
    nc = c.nc
    with c.phase() as ctx:
        x = c.sb("n1_x", [P, 4, K4, D], ctx=ctx)
        y = c.sb("n1_y", [P, 4, K4, D], ctx=ctx)
        stats, mv, rs = (c.sb("n1_" + n, [P, 2, K4] + m, ctx=ctx) for n, m in (("stats", [6]), ("mv", [2]), ("rs", [])))
        off = c.sb("n1_off", [P, 2, K4], ctx=ctx)
        s = signals(c, "n1_")
        loaded, stored, moved = ([s(f"{n}{u}") for u in range(4)] for n in ("loaded", "stored", "moved"))
        pos = c.sb("n1_pos", [P, GROUPS, K4], I32, ctx=ctx)
        at, row = c.sb("n1_at", [P, 4, K4], I32, ctx=ctx), c.sb("n1_row", [P, 4, K4], I32, ctx=ctx)
        block = ctx.enter_context(nc.Block())

        @block.sync
        def _(sp):
            def load(t):
                if not t.early(4):
                    sp.wait_ge(s("y_done"), t.g - 3)
                sp.dma_start(x[:, t.slot(4), :, :], node_rows(a["x"], t.g)).then_inc(loaded[t.slot(4)], 16)

            def store(t):
                sp.wait_ge(s("y_done"), t.g + 1)
                if t.last(NG):
                    sp.wait_ge(stored[(NG - 2) % 4], 16 * ((NG - 2) // 4 + 1))
                sp.dma_start(node_rows(c.a_dram, t.g), y[:, t.slot(4), :, :]).then_inc(stored[t.slot(4)], 16)
            skewed(sp, NG, [(0, load), (3, store)])
            for u in range(4):
                sp.wait_ge(stored[u], 16 * len(range(u, NG, 4)))

        @block.gpsimd
        def _(pool):
            pool.iota(pos[:, :, :], pattern=[[ROWS, GROUPS], [P, K4]], base=0, channel_multiplier=1).then_inc(s("pos"), 1)
            pool.wait_ge(s("pos"), 1)

            def send(t):
                u = t.slot(4)
                if not t.early(4):
                    pool.wait_ge(moved[u], t.turn(4) * 16 * K4)
                    pool.sem_inc(s("issuing"), 1)
                pool.tensor_copy(at[:, u, :], c.s["index"][:, bass.ds(t.g, 1), LAST, :].rearrange("p o k -> p (o k)"))\
                    .then_inc(s("at"), 1)
                pool.tensor_copy(row[:, u, :], pos[:, bass.ds(t.g, 1), :].rearrange("p o k -> p (o k)")).then_inc(s("at"), 1)
                pool.wait_ge(s("at"), t.g * 2 + 2)
                pool.sem_inc(s("issuing"), 1)
                for k in range(K4):
                    pool.indirect_dma_start(c.place_dram[:, :], bass.IndirectOffsetOnAxis(ap=at[:, u, k:k + 1], axis=0),
                                            row[:, u, k:k + 1], None, bounds_check=N - 1, oob_is_err=False).then_inc(moved[u], 16)
            skewed(pool, GROUPS, [(0, send)])
            for u in range(4):
                pool.wait_ge(moved[u], len(range(u, GROUPS, 4)) * 16 * K4)

        @block.vector
        def _(dve):
            def measure(t):
                dve.wait_ge(loaded[t.slot(4)], 16 * (t.turn(4) + 1))
                dve.tensor_tensor(x[:, t.slot(4), :, :], x[:, t.slot(4), :, :], over_tiles(c.c0[:, :]), ALU.add)\
                   .then_inc(s("shifted"), 1)
                dve.wait_ge(s("shifted"), t.g + 1)
                if not t.early(2):
                    dve.wait_ge(s("x_shift"), t.g - 1)
                row_stats(dve, x[:, t.slot(4)], stats[:, t.slot(2)], mv[:, t.slot(2)], s, "x", t.g)

            def shift(t):
                if not t.early(2):
                    dve.wait_ge(s("y_done"), t.g - 1)
                row_shift(dve, off[:, t.slot(2), :], mv[:, t.slot(2)], rs[:, t.slot(2), :], s, "x", t.g)
            skewed(dve, NG, [(0, measure), (1, shift)])

        @block.scalar
        def _(act):
            log_exp_tables(nc, act)
            def apply(t):
                u, v = t.slot(2), t.slot(4)
                if not t.early(4):
                    act.wait_ge(stored[v], 16 * t.turn(4))
                row_apply_act(act, y[:, v], x[:, v], off[:, u], rs[:, u], s, "x", t.g, "y_done")
            skewed(act, NG, [(1, apply), (0, lambda t: row_scale(act, c, mv[:, t.slot(2)], rs[:, t.slot(2), :], s, "x", t.g,
                                                                 c.consts[:, 1:2]))])


def cosine_phase(c):
    nc = c.nc
    with c.phase() as ctx:
        half = c.sb("co_half", [P, T], ctx=ctx)
        s = signals(c, "co_")
        block = ctx.enter_context(nc.Block())
        rounder = 1.5 * 2.0 ** 23
        w = c.d["w"]

        @block.vector
        def _(dve):
            dve.tensor_scalar(half[:, :], w[:, :], 0.5, rounder, ALU.mult, ALU.add).then_inc(s("step"), 1)
            dve.wait_ge(s("step"), 1)
            dve.tensor_scalar(half[:, :], half[:, :], rounder, -2.0, ALU.subtract, ALU.mult).then_inc(s("step"), 1)
            dve.wait_ge(s("step"), 2)
            dve.tensor_tensor(half[:, :], half[:, :], w[:, :], ALU.add).then_inc(s("reduced"), 1)
            dve.wait_ge(s("sine"), 1)
            dve.tensor_scalar(c.cutoff[:, :], half[:, :], 1.0, 0.25, ALU.add, ALU.mult)

        @block.scalar
        def _(act):
            act.wait_ge(s("reduced"), 1)
            act.activation(half[:, :], half[:, :], ACT.Abs).then_inc(s("abs"), 1)
            act.wait_ge(s("abs"), 1)
            act.activation(half[:, :], half[:, :], ACT.Sin, bias=c.consts[:, 3:4], scale=-math.pi).then_inc(s("sine"), 1)


def load_keys(sp, dram, to, t, lo, n, slots, used, keyed, parts=P):
    if not t.early(slots):
        sp.wait_ge(used, t.g - (slots - 1))
    sp.dma_start(to, dram[bass.ds(t.g * ROWS + lo, n)].rearrange("(o n) -> o n", o=1).to_broadcast([parts, n]))\
      .then_inc(keyed[t.slot(slots)], 16)


def filter_layer(c, a):
    nc = c.nc
    side = c.d
    with c.phase() as ctx:
        sb = lambda n, shape, dt=F32: c.sb("l0_" + n, shape, dt, ctx=ctx)
        xs, xd = sb("xs", [P, 2, K4, D]), sb("xd", [P, 4, K4, D])
        ea, keys = sb("ea", [P, 2, K4, BASIS]), sb("keys", [P, 2, ROWS + 1])
        at, at_last = sb("at", [P, 4, 4, K4], I32), sb("at_last", [P, 4, K4], I32)
        eaT, xsT = sb("eaT", [BASIS, ROWS]), sb("xsT", [P, 2, ROWS])
        pre, log, soft = (sb(n, [P, 2, 2, ROWS]) for n in ("pre", "log", "soft"))
        filt, msg = sb("filt", [P, K4, D]), sb("msg", [P, K4, D])
        same, cont = sb("same", [P, 2, K4, P]), sb("cont", [P, 2, K4, P])
        agg, y = sb("agg", [P, 2, ROWS]), sb("y", [P, 4, K4, D])
        stats, mv, rs = sb("stats", [P, K4, 6]), sb("mv", [P, K4, 2]), sb("rs", [P, K4])
        ps_x, ps_z, ps_o, ps_a = (c.ps("l0_p" + n, [P, 2, 512], ctx=ctx) for n in "xzoa")
        tiles_of = lambda p: p[:, :, :].rearrange("p b (j d) -> p (b j) d", d=D)
        s = signals(c, "l0_")
        got_s, got_e, keyed = ([s(f"{n}{u}") for u in range(2)] for n in ("got_s", "got_e", "keyed"))
        got_d, sent = ([s(f"{n}{u}") for u in range(4)] for n in ("got_d", "sent"))
        at_place, row = sb("at_place", [P, 2, K4], I32), sb("row", [P, 2, K4], I32)
        looked = [s("looked0"), s("looked1")]
        block = ctx.enter_context(nc.Block())

        @block.gpsimd
        def _(pool):
            def gather(t):
                u, v = t.slot(2), t.slot(4)
                if not t.early(2):
                    pool.wait_ge(s("xsT"), t.g - 1)
                    pool.wait_ge(s("eaT"), t.g - 1)
                if not t.early(4):
                    pool.wait_ge(s("summed"), t.g - 3)
                    pool.sem_inc(s("issuing"), 1)
                pool.tensor_copy(at[:, v, :, :], side["index"][:, bass.ds(t.g, 1), :, :].rearrange("p o n k -> p (o n) k"))\
                    .then_inc(s("at"), 1)
                pool.wait_ge(s("at"), t.g + 1)
                pool.sem_inc(s("issuing"), 1)
                for to, frm, kind, got in ((ea[:, u], a["ea"], EDGE, got_e[u]), (xs[:, u], a["x"], OTHER, got_s[u]),
                                           (xd[:, v], a["x"], OWN, got_d[v])):
                    for k in range(K4):
                        pool.indirect_dma_start(to[:, k, :], None, frm[:, :],
                                                bass.IndirectOffsetOnAxis(ap=at[:, v, kind, k:k + 1], axis=0)).then_inc(got, 16)

            def scatter(t):
                v = t.slot(4)
                if not t.early(4):
                    pool.wait_ge(sent[v], t.turn(4) * 16 * K4)
                pool.tensor_copy(at_last[:, v, :], side["index"][:, bass.ds(t.g, 1), LAST, :].rearrange("p o k -> p (o k)"))\
                    .then_inc(s("at_last"), 1)
                pool.wait_ge(s("at_last"), t.g + 1)
                pool.wait_ge(s("y_done"), t.g + 1)
                pool.sem_inc(s("issuing"), 1)
                for k in range(K4):
                    pool.indirect_dma_start(c.a_dram[:, :], bass.IndirectOffsetOnAxis(ap=at_last[:, v, k:k + 1], axis=0),
                                            y[:, v, k, :], None, bounds_check=N - 1, oob_is_err=False).then_inc(sent[v], 16)

            def look(t):
                u = t.slot(2)
                if not t.early(2):
                    pool.wait_ge(s("kept"), t.g - 1)
                    pool.sem_inc(s("issuing"), 1)
                pool.tensor_copy(at_place[:, u, :], c.s["index"][:, bass.ds(t.g, 1), OTHER, :].rearrange("p o k -> p (o k)"))\
                    .then_inc(s("at_place"), 1)
                pool.wait_ge(s("at_place"), t.g + 1)
                pool.sem_inc(s("issuing"), 1)
                for k in range(K4):
                    pool.indirect_dma_start(row[:, u, k:k + 1], None, c.place_dram[:, :],
                                            bass.IndirectOffsetOnAxis(ap=at_place[:, u, k:k + 1], axis=0)).then_inc(looked[u], 16)

            def keep(t):
                u = t.slot(2)
                pool.wait_ge(looked[u], (t.turn(2) + 1) * 16 * K4)
                pool.sem_inc(s("issuing"), 1)
                pool.tensor_copy(c.s_place[:, bass.ds(t.g, 1), :].rearrange("p o k -> p (o k)"), row[:, u, :]).then_inc(s("kept"), 1)
            skewed(pool, GROUPS, [(0, gather), (1, keep), (0, look), (3, scatter)])
            for v in range(4):
                pool.wait_ge(sent[v], len(range(v, GROUPS, 4)) * 16 * K4)

        @block.sync
        def _(sp):
            skewed(sp, GROUPS, [(0, lambda t: load_keys(sp, side["keys"], keys[:, t.slot(2), :], t, 0, ROWS + 1, 2,
                                                        s("masked"), keyed))])

        @block.tensor
        def _(pe):
            def turn(t):
                u = t.slot(2)
                pe.wait_ge(got_e[u], (t.turn(2) + 1) * 16 * K4)
                pe.wait_ge(s("filt"), t.g)
                pe.sem_inc(s("held"), 1)
                for k in range(K4):
                    last = pe.transpose(ps_z[0:BASIS, 0, k * P:(k + 1) * P], ea[:, u, k, :], c.ident[:, :])
                last.then_inc(s("eaT"), 1)
                pe.wait_ge(got_s[u], (t.turn(2) + 1) * 16 * K4)
                pe.wait_ge(s("msg"), t.g)
                for f in range(2):
                    for k in range(K4):
                        last = pe.transpose(ps_x[:, f, k * P:(k + 1) * P], xs[:, u, k, f * P:(f + 1) * P], c.ident[:, :])
                last.then_inc(s("xsT"), 1)
                pe.wait_ge(s("eaT_sb"), t.g + 1)
                for f in range(2):
                    last = pe.matmul(ps_z[:, f, :], c.fw1T[:, f * P:(f + 1) * P], eaT[:, :], start=True, stop=True)
                last.then_inc(s("hidden"), 1)

            def first_out(t):
                pe.wait_ge(s("agg"), (t.g + 1) * K4)
                pe.wait_ge(s("pre1"), t.g)
                for o in range(2):
                    for f in range(2):
                        last = pe.matmul(ps_o[:, o, :], c.w2T[:, f, o * P:(o + 1) * P], agg[:, f, :],
                                         start=(f == 0), stop=(f == 1))
                last.then_inc(s("o1"), 1)

            def messages(t):
                pe.wait_ge(s("xsT_sb"), t.g + 1)
                for k in range(K4):
                    for f in range(2):
                        last = pe.matmul(tiles_of(ps_x)[:, k, :], xsT[:, f, k * P:(k + 1) * P], c.w1T[:, f, :],
                                         start=(f == 0), stop=(f == 1))
                last.then_inc(s("h"), 1)
                pe.wait_ge(s("soft0"), t.g + 1)
                for k in range(K4):
                    for f in range(2):
                        last = pe.matmul(tiles_of(ps_z)[:, k, :], soft[:, 0, f, k * P:(k + 1) * P], c.fw2T[:, f, :],
                                         start=(f == 0), stop=(f == 1))
                last.then_inc(s("filter"), 1)

            def second_out(t):
                pe.wait_ge(s("soft1"), t.g + 1)
                for k in range(K4):
                    for o in range(2):
                        last = pe.matmul(tiles_of(ps_a)[:, k, :], soft[:, 1, o, k * P:(k + 1) * P], c.w3T[:, o, :],
                                         start=(o == 0), stop=(o == 1))
                last.then_inc(s("o2"), 1)

            def runs(t):
                pe.wait_ge(s("msg"), t.g + 1)
                pe.wait_ge(s("masked"), t.g + 1)
                pe.wait_ge(s("summed"), t.g)
                for f in range(2):
                    for k in range(K4):
                        last = pe.matmul(ps_a[:, f, k * P:(k + 1) * P], msg[:, k, f * P:(f + 1) * P], same[:, t.slot(2), k, :],
                                         start=True, stop=True)
                last.then_inc(s("runs"), 1)
            skewed(pe, GROUPS, [(0, turn), (1, first_out), (0, messages), (1, second_out), (0, runs)])

        @block.scalar
        def _(act):
            log_exp_tables(nc, act)
            def copies(t):
                act.wait_ge(s("eaT"), t.g + 1)
                act.activation(eaT[:, :], ps_z[0:BASIS, 0, :], ACT.Copy).then_inc(s("eaT_sb"), 1)
                act.wait_ge(s("xsT"), t.g + 1)
                act.wait_ge(s("h"), t.g)
                act.activation(xsT[:, :, :], ps_x[:, :, :], ACT.Copy).then_inc(s("xsT_sb"), 1)

            def softplus(t, n, ps, ready, bias):
                act.wait_ge(s(ready), t.g + 1)
                act.wait_ge(s(f"soft{n}"), t.g)
                for f in range(2):
                    last = act.activation(pre[:, n, f, :], ps[:, f, :], ACT.Identity, bias=bias[:, f:f + 1])
                last.then_inc(s(f"pre{n}"), 1)
                act.wait_ge(s(f"pre{n}"), t.g + 1)
                act.activation(log[:, n, :, :], pre[:, n, :, :], ACT.Abs).then_inc(s(f"abs{n}"), 1)
                act.wait_ge(s(f"abs{n}"), t.g + 1)
                act.activation(log[:, n, :, :], log[:, n, :, :], ACT.Exp, scale=-1.0).then_inc(s(f"exp{n}"), 1)
                act.wait_ge(s(f"exp{n}"), t.g + 1)
                act.activation(log[:, n, :, :], log[:, n, :, :], ACT.Ln, bias=c.consts[:, 4:5], scale=0.5).then_inc(s(f"log{n}"), 1)
            skewed(act, GROUPS, [(0, copies), (0, lambda t: softplus(t, 0, ps_z, "hidden", c.fb1)),
                                 (1, lambda t: softplus(t, 1, ps_o, "o1", c.b2)),
                                 (1, lambda t: row_scale(act, c, mv, rs[:, :], s, "x", t.g, c.consts[:, 1:2]))])

        @block.vector
        def _(dve):
            dve.memset(agg[:, :, :], 0.0).then_inc(s("agg_clear"), 1)

            def softplus(t, n, used):
                dve.wait_ge(s(f"log{n}"), t.g + 1)
                dve.wait_ge(s(used), t.g)
                dve.scalar_tensor_tensor(out=soft[:, n, :, :], in0=pre[:, n, :, :], scalar=0.0, in1=log[:, n, :, :],
                                         op0=ALU.max, op1=ALU.add).then_inc(s(f"soft{n}"), 1)

            def carry_on(t):
                dve.wait_ge(s("runs"), t.g + 1)
                dve.wait_ge(s("o1"), t.g)
                for k in range(K4):
                    if t.early(1) and k == 0:
                        dve.wait_ge(s("agg_clear"), 1)
                    else:
                        dve.wait_ge(s("agg"), t.g * K4 + k)
                    before = (k * P - 1) % ROWS
                    for f in range(2):
                        last = dve.scalar_tensor_tensor(
                            out=agg[:, f, k * P:(k + 1) * P], in0=cont[:, t.slot(2), k, :], scalar=agg[:, f, before:before + 1],
                            in1=ps_a[:, f, k * P:(k + 1) * P], op0=ALU.mult, op1=ALU.add)
                    last.then_inc(s("agg"), 1)

            def masks(t):
                u = t.slot(2)
                dve.wait_ge(keyed[u], 16 * (t.turn(2) + 1))
                if not t.early(2):
                    dve.wait_ge(s("runs"), t.g - 1)
                rows = keys[:, u, 1:ROWS + 1].rearrange("p (k j) -> p k j", k=K4)
                dve.tensor_tensor(same[:, u, :, :], rows, along(side["key"][:, bass.ds(t.g * K4 + 1, K4)]), ALU.is_equal)
                dve.tensor_tensor(cont[:, u, :, :], rows, along(keys[:, u, 0:ROWS:P]), ALU.is_equal).then_inc(s("masked"), 1)

            def messages(t):
                dve.wait_ge(s("filter"), t.g + 1)
                dve.tensor_tensor(filt[:, :, :], tiles_of(ps_z), over_tiles(c.fb2[:, :]), ALU.add).then_inc(s("filt"), 1)
                dve.wait_ge(s("filt"), t.g + 1)
                dve.wait_ge(s("h"), t.g + 1)
                dve.wait_ge(s("runs"), t.g)
                for k in range(K4):
                    last = dve.scalar_tensor_tensor(out=msg[:, k, :], in0=filt[:, k, :], scalar=c.cutoff[:, bass.ds(t.g * K4 + k, 1)],
                                                    in1=tiles_of(ps_x)[:, k, :], op0=ALU.mult, op1=ALU.mult)
                last.then_inc(s("msg"), 1)

            def add_bias(t):
                v = t.slot(4)
                dve.wait_ge(got_d[v], (t.turn(4) + 1) * 16 * K4)
                dve.tensor_tensor(xd[:, v, :, :], xd[:, v, :, :], over_tiles(c.b3[:, :]), ALU.add).then_inc(s("xd"), 1)

            def finish(t):
                v = t.slot(4)
                dve.wait_ge(s("xd"), t.g + 1)
                dve.wait_ge(s("o2"), t.g + 1)
                if not t.early(4):
                    dve.wait_ge(sent[v], t.turn(4) * 16 * K4)
                dve.tensor_tensor(y[:, v, :, :], tiles_of(ps_a), xd[:, v, :, :], ALU.add).then_inc(s("summed"), 1)
                dve.wait_ge(s("summed"), t.g + 1)
                row_stats(dve, y[:, v], stats, mv, s, "x", t.g)

            def normalize(t):
                row_apply(dve, y[:, t.slot(4)], y[:, t.slot(4)], mv, rs, s, "x", t.g, "y_done")
            skewed(dve, GROUPS, [(1, carry_on), (2, normalize), (0, masks), (0, add_bias), (0, lambda t: softplus(t, 0, "filter")),
                                 (1, lambda t: softplus(t, 1, "o2")), (0, messages), (1, finish)])


def propagation_round(c, n):
    nc = c.nc
    side = c.s
    table = (c.a_dram, c.h1_dram, c.h2_dram)[n - 1]
    weight = side["w8"] if n == 1 else side["w"]
    with c.phase() as ctx:
        pre = f"l1{n}_"
        sb = lambda m, shape, dt=F32: c.sb(pre + m, shape, dt, ctx=ctx)
        x, keys, at = sb("x", [P, 4, K4, D]), sb("keys", [P, 2, ROWS]), sb("at", [P, 4, K4], I32)
        at_last = sb("at_last", [P, 4, K4], I32)
        same, cont = sb("same", [P, 4, K4, P]), sb("cont", [P, 4, K4, P])
        total, h, square = sb("total", [P, 4, K4, D]), sb("h", [P, 4, K4, D]), sb("square", [P, K4, D])
        ss, rn = sb("ss", [P, 2, K4]), sb("rn", [P, 2, K4])
        old = sb("old", [P, 2, 2, K4, D]) if n == 3 else None
        acc = c.ps(pre + "acc", [P, 2 * K4, 512], ctx=ctx)
        s = signals(c, pre)
        got, sent = ([s(f"{m}{u}") for u in range(4)] for m in ("got", "sent"))
        keyed, older = ([s(f"{m}{u}") for u in range(2)] for m in ("keyed", "older"))
        per_send = 16 * K4 if n == 3 else 16
        block = ctx.enter_context(nc.Block())

        @block.gpsimd
        def _(pool):
            def gather(t):
                u = t.slot(4)
                if not t.early(4):
                    pool.wait_ge(s("opened"), t.g - 3)
                    pool.sem_inc(s("issuing"), 1)
                place = side["index"][:, bass.ds(t.g, 1), OTHER, :] if n == 1 else c.s_place[:, bass.ds(t.g, 1), :]
                pool.tensor_copy(at[:, u, :], place.rearrange("p o k -> p (o k)")).then_inc(s("at"), 1)
                pool.wait_ge(s("at"), t.g + 1)
                pool.sem_inc(s("issuing"), 1)
                for k in range(K4):
                    pool.indirect_dma_start(x[:, u, k, :], None, table[:, :],
                                            bass.IndirectOffsetOnAxis(ap=at[:, u, k:k + 1], axis=0)).then_inc(got[u], 16)

            def scatter(t):
                u = t.slot(4)
                if not t.early(4):
                    pool.wait_ge(sent[u], t.turn(4) * per_send)
                pool.tensor_copy(at_last[:, u, :], side["index"][:, bass.ds(t.g, 1), LAST, :].rearrange("p o k -> p (o k)"))\
                    .then_inc(s("at_last"), 1)
                pool.wait_ge(s("at_last"), t.g + 1)
                pool.wait_ge(s("h_done"), t.g + 1)
                pool.sem_inc(s("issuing"), 1)
                for k in range(K4):
                    pool.indirect_dma_start(c.a_dram[:, :], bass.IndirectOffsetOnAxis(ap=at_last[:, u, k:k + 1], axis=0),
                                            h[:, u, k, :], None, bounds_check=N - 1, oob_is_err=False,
                                            compute_op=ALU.add).then_inc(sent[u], 16)
            skewed(pool, GROUPS, [(0, gather)] + ([(5, scatter)] if n == 3 else []))
            if n == 3:
                for u in range(4):
                    pool.wait_ge(sent[u], len(range(u, GROUPS, 4)) * per_send)

        @block.sync
        def _(sp):
            def load_old(t):
                if not t.early(2):
                    sp.wait_ge(s("h_done"), t.g - 1)
                sp.dma_start(old[:, t.slot(2), 0, :, :], edge_rows(c.h1_dram, t.g)).then_inc(older[t.slot(2)], 16)
                sp.dma_start(old[:, t.slot(2), 1, :, :], edge_rows(c.h2_dram, t.g)).then_inc(older[t.slot(2)], 16)

            def store(t):
                sp.wait_ge(s("h_own"), t.g + 1)
                sp.dma_start(edge_rows((c.h1_dram, c.h2_dram)[n - 1], t.g), h[:, t.slot(4), :, :]).then_inc(sent[t.slot(4)], 16)
            skewed(sp, GROUPS, [(0, lambda t: load_keys(sp, side["keys"], keys[:, t.slot(2), :], t, 1, ROWS, 2, s("masked"), keyed)),
                                (3, load_old) if n == 3 else (5, store)])
            if n < 3:
                for u in range(4):
                    sp.wait_ge(sent[u], len(range(u, GROUPS, 4)) * per_send)

        @block.tensor
        def _(pe):
            def inside(t, k):
                if k == 0:
                    pe.wait_ge(got[t.slot(4)], (t.turn(4) + 1) * 16 * K4)
                    pe.wait_ge(s("masked"), t.g + 1)
                    if not t.early(2):
                        pe.wait_ge(s("total"), (t.g - 1) * K4)
                last = pe.matmul(acc[:, t.slot(2) * K4 + k, 0:D], same[:, t.slot(4), k, :], x[:, t.slot(4), k, :],
                                 start=True, stop=False)
                if k == K4 - 1:
                    last.then_inc(s("opened"), 1)

            def across(t, k):
                if t.early(1) and k == 0:
                    pe.wait_ge(s("total_clear"), 1)
                else:
                    pe.wait_ge(s("total"), t.g * K4 + k)
                before = total[96:P, t.slot(4), k - 1, :] if k else total[96:P, (t.slot(4) - 1) % 4, K4 - 1, :]
                pe.matmul(acc[:, t.slot(2) * K4 + k, 0:D], cont[96:P, t.slot(4), k, :], before,
                          start=False, stop=True).then_inc(s("acc"), 1)
            skewed(pe, GROUPS, [(lag, lambda t, k=k, fn=fn: fn(t, k)) for k in range(K4) for lag, fn in ((2, across), (1, inside))])

        @block.scalar
        def _(act):
            log_exp_tables(nc, act)
            def norms(t):
                act.wait_ge(s("squared"), t.g + 1)
                inverse_norm(act, c, ss[:, t.slot(2), :], rn[:, t.slot(2), :], rn[:, t.slot(2), :], s, t.g, c.consts[:, 5:6] if n == 3 else c.consts[:, 2:3])

            def totals(t):
                for k in range(K4):
                    act.wait_ge(s("acc"), t.g * K4 + k + 1)
                    if k == 0 and not t.early(4):
                        act.wait_ge(s("h_own"), t.g - 3)
                    act.activation(total[:, t.slot(4), k, :], acc[:, t.slot(2) * K4 + k, 0:D], ACT.Copy).then_inc(s("total"), 1)
            skewed(act, GROUPS, [(2, totals), (3, norms)])

        @block.vector
        def _(dve):
            dve.memset(total[:, 3, K4 - 1, :], 0.0).then_inc(s("total_clear"), 1)

            def masks(t):
                u, v = t.slot(2), t.slot(4)
                dve.wait_ge(keyed[u], 16 * (t.turn(2) + 1))
                if not t.early(4):
                    dve.wait_ge(s("acc"), (t.g - 3) * K4)
                for k in range(K4):
                    dve.tensor_scalar(same[:, v, k, :], keys[:, u, k * P:(k + 1) * P], side["key"][:, bass.ds(t.g * K4 + k + 1, 1)],
                                      weight[:, bass.ds(t.g * K4 + k, 1)], ALU.is_equal, ALU.mult)
                dve.tensor_tensor(cont[96:P, v, :, :], keys[96:P, u, :].rearrange("p (k j) -> p k j", k=K4),
                                  along(side["key_end"][96:P, bass.ds(t.g * K4, K4)]), ALU.is_equal).then_inc(s("masked"), 1)

            def squares(t):
                dve.wait_ge(s("total"), (t.g + 1) * K4)
                if not t.early(2):
                    dve.wait_ge(s("rn_guard"), t.g - 1)
                if not t.early(1):
                    dve.wait_ge(s("squared"), t.g)
                for k in range(K4):
                    last = dve.scalar_tensor_tensor(out=square[:, k, :], in0=total[:, t.slot(4), k, :], scalar=1.0,
                                                    in1=total[:, t.slot(4), k, :], op0=ALU.mult, op1=ALU.mult,
                                                    accum_out=ss[:, t.slot(2), k:k + 1])
                last.then_inc(s("squared"), 1)

            def scale(t):
                u, v = t.slot(2), t.slot(4)
                dve.wait_ge(s("rn"), t.g + 1)
                if not t.early(4):
                    dve.wait_ge(sent[v], t.turn(4) * per_send)
                for k in range(K4):
                    last = dve.tensor_scalar(h[:, v, k, :], total[:, v, k, :], rn[:, u, k:k + 1], None, ALU.mult)
                last.then_inc(s("h_own"), 1)
                if n < 3:
                    return
                dve.wait_ge(older[u], (t.turn(2) + 1) * 32)
                dve.wait_ge(s("h_own"), t.g + 1)
                dve.scalar_tensor_tensor(out=h[:, v, :, :], in0=old[:, u, 0, :, :], scalar=0.25, in1=h[:, v, :, :],
                                         op0=ALU.mult, op1=ALU.add).then_inc(s("h_first"), 1)
                dve.wait_ge(s("h_first"), t.g + 1)
                dve.scalar_tensor_tensor(out=h[:, v, :, :], in0=old[:, u, 1, :, :], scalar=0.25, in1=h[:, v, :, :],
                                         op0=ALU.mult, op1=ALU.add).then_inc(s("h_done"), 1)
            skewed(dve, GROUPS, [(3, squares), (0, masks), (4, scale)])


def node_pass_two(c):
    nc = c.nc
    with c.phase() as ctx:
        sb = lambda n, shape, dt=F32: c.sb("n2_" + n, shape, dt, ctx=ctx)
        x, x3, y = sb("x", [P, 6, K4, D]), sb("x3", [P, 3, K4, D]), sb("y", [P, 3, K4, D])
        xT, h, square = sb("xT", [P, 2, 2, ROWS]), sb("h", [P, 2, K4, D]), sb("square", [P, K4, D])
        stats, mv, rs = sb("stats", [P, 2, K4, 6]), sb("mv", [P, 2, 2, K4, 2]), sb("rs", [P, 2, K4])
        log, fac = sb("log", [P, 2, 2, K4]), sb("fac", [P, 2, 3, K4])
        ss, rn, guarded, off = (sb(n, [P, 2, K4]) for n in ("ss", "rn", "guarded", "off"))
        work = sb("work", [P, 3, K4])
        turn = c.ps("n2_turn", [P, 4, 512], ctx=ctx)
        prod = c.ps("n2_prod", [P, 4, 512], ctx=ctx)
        s = signals(c, "n2_")
        loaded, sent2 = ([s(f"{n}{u}") for u in range(6)] for n in ("loaded", "sent2_"))
        sent3, senty = ([s(f"{n}{u}") for u in range(3)] for n in ("sent3_", "senty"))
        tiles = lambda t: prod[:, 2 * t.slot(2):2 * t.slot(2) + 2, :].rearrange("p b (j d) -> p (b j) d", d=D)
        block = ctx.enter_context(nc.Block())

        @block.sync
        def _(sp):
            def load(t):
                if not t.early(6):
                    sp.wait_ge(s("z"), t.g - 5)
                    sp.sem_inc(s("loading"), 1)
                    sp.wait_ge(sent2[t.slot(6)], 16 * t.turn(6))
                sp.dma_start(x[:, t.slot(6), :, :], node_rows(c.a_dram, t.g)).then_inc(loaded[t.slot(6)], 16)

            def store(t, dram, buf, slots, done, sent):
                if t.last(NG):
                    sp.wait_ge(sent[(NG - 2) % slots], 16 * ((NG - 2) // slots + 1))
                sp.wait_ge(s(done), t.g + 1)
                sp.dma_start(node_rows(dram, t.g), buf[:, t.slot(slots), :, :]).then_inc(sent[t.slot(slots)], 16)
            skewed(sp, NG, [(0, load), (3, lambda t: store(t, c.x2_dram, x, 6, "x2", sent2)),
                            (7, lambda t: store(t, c.x3_dram, x3, 3, "x3_done", sent3)),
                            (8, lambda t: store(t, c.out, y, 3, "y_done", senty))], 6)
            for u in range(6):
                sp.wait_ge(sent2[u], 16 * len(range(u, NG, 6)))
            for u in range(3):
                sp.wait_ge(sent3[u], 16 * len(range(u, NG, 3)))
                sp.wait_ge(senty[u], 16 * len(range(u, NG, 3)))

        @block.vector
        def _(dve):
            def sum_up(t):
                v = t.slot(3)
                dve.wait_ge(s("n_newton"), 3 * t.g + 3)
                if not t.early(3):
                    dve.wait_ge(sent3[v], 16 * t.turn(3))
                    dve.wait_ge(s("y_done"), t.g - 2)
                for k in range(K4):
                    last = dve.scalar_tensor_tensor(out=x3[:, v, k, :], in0=h[:, t.slot(2), k, :], scalar=rn[:, t.slot(2), k:k + 1],
                                                    in1=x[:, t.slot(6), k, :], op0=ALU.mult, op1=ALU.add)
                last.then_inc(s("z"), 1)
                dve.wait_ge(s("z"), t.g + 1)
                row_stats(dve, x3[:, v], stats[:, 1], mv[:, 1, t.slot(2)], s, "b", t.g)

            def measure(t):
                dve.wait_ge(loaded[t.slot(6)], 16 * (t.turn(6) + 1))
                row_stats(dve, x[:, t.slot(6)], stats[:, 0], mv[:, 0, t.slot(2)], s, "a", t.g)

            def out(t):
                dve.wait_ge(s("b_newton"), 3 * t.g + 3)
                row_apply(dve, x3[:, t.slot(3)], x3[:, t.slot(3)], mv[:, 1, t.slot(2)], fac[:, t.slot(2), 0, :], s, "b", t.g,
                          "x3_done")

            def shift(t):
                u = t.slot(2)
                if not t.early(2):
                    dve.wait_ge(s("x2"), t.g - 1)
                dve.wait_ge(s("a_newton"), 3 * t.g + 3)
                row_shift(dve, off[:, u, :], mv[:, 0, u], rs[:, u, :], s, "a", t.g)
            def a_root(t, n):
                if n == 0:
                    dve.wait_ge(s("a_scale"), t.g + 1)
                newton_part(dve, n, *variance_root(rs[:, t.slot(2), :], mv[:, 0, t.slot(2)], work[:, 0, :]), s("a_newton"), t.g)

            def b_root(t, n):
                if n == 0:
                    dve.wait_ge(s("b_scale"), t.g + 1)
                newton_part(dve, n, *variance_root(fac[:, t.slot(2), 0, :], mv[:, 1, t.slot(2)], work[:, 1, :]), s("b_newton"), t.g)

            def n_root(t, n):
                if n == 0:
                    dve.wait_ge(s("rn"), t.g + 1)
                newton_part(dve, n, *norm_root(rn[:, t.slot(2), :], guarded[:, t.slot(2), :], work[:, 2, :]), s("n_newton"), t.g)
            roots = [(lag, lambda t, fn=fn, n=n: fn(t, n)) for n in range(3) for lag, fn in ((5, n_root), (6, b_root), (2, a_root))]
            skewed(dve, NG, roots + [(5, sum_up), (2, shift), (1, measure), (6, out)], 6)

        @block.gpsimd
        def _(pool):
            def twice(t):
                pool.wait_ge(s("x3_done"), t.g + 1)
                if not t.early(3):
                    pool.wait_ge(senty[t.slot(3)], 16 * t.turn(3))
                pool.sem_inc(s("held"), 1)
                for k in range(K4):
                    last = pool.tensor_scalar(y[:, t.slot(3), k, :], x3[:, t.slot(3), k, :], fac[:, t.slot(2), 1, k:k + 1],
                                              fac[:, t.slot(2), 2, k:k + 1], ALU.mult, ALU.mult)
                last.then_inc(s("y_done"), 1)
            skewed(pool, NG, [(7, twice)], 6)

        @block.scalar
        def _(act):
            log_exp_tables(nc, act)
            def scales(t):
                u = t.slot(2)
                act.wait_ge(s("b_var"), t.g + 1)
                if not t.early(2):
                    act.wait_ge(s("y_done"), t.g - 1)
                act.activation(log[:, u, 0, :], mv[:, 1, u, :, 1], ACT.Ln, bias=c.consts[:, 0:1])
                act.activation(log[:, u, 1, :], mv[:, 1, u, :, 1], ACT.Ln, bias=c.consts[:, 8:9], scale=1.0 + LN_EPS)\
                   .then_inc(s("b_log"), 1)
                act.wait_ge(s("b_log"), t.g + 1)
                act.activation(fac[:, u, 1, :], log[:, u, 0, :], ACT.Exp, scale=0.5)
                act.activation(fac[:, u, 2, :], log[:, u, 1, :], ACT.Exp, scale=-0.5)
                act.activation(fac[:, u, 0, :], log[:, u, 0, :], ACT.Exp, scale=-0.5).then_inc(s("b_scale"), 1)

            def norm(t):
                u = t.slot(2)
                act.wait_ge(s("prod"), t.g + 1)
                if not t.early(2):
                    act.wait_ge(s("z"), t.g - 1)
                act.activation(h[:, u, :, :], tiles(t), ACT.Relu).then_inc(s("relu"), 1)
                act.wait_ge(s("relu"), t.g + 1)
                if not t.early(1):
                    act.wait_ge(s("squared"), t.g)
                for k in range(K4):
                    last = act.activation(square[:, k, :], h[:, u, k, :], ACT.Square, accum_out=ss[:, u, k:k + 1])
                last.then_inc(s("squared"), 1)
                act.wait_ge(s("squared"), t.g + 1)
                inverse_norm(act, c, ss[:, u, :], guarded[:, u, :], rn[:, u, :], s, t.g, c.consts[:, 2:3])

            def copy(t):
                u = t.slot(2)
                act.wait_ge(s("xT"), t.g + 1)
                if not t.early(2):
                    act.wait_ge(s("prod"), t.g - 1)
                act.activation(xT[:, u, :, :], turn[:, 2 * u:2 * u + 2, :], ACT.Copy).then_inc(s("xT_sb"), 1)
            def apply(t):
                v = t.slot(6)
                row_apply_act(act, x[:, v], x[:, v], off[:, t.slot(2)], rs[:, t.slot(2)], s, "a", t.g, "x2")
            skewed(act, NG, [(3, copy), (4, norm), (2, apply), (5, scales),
                             (1, lambda t: row_scale(act, c, mv[:, 0, t.slot(2)], rs[:, t.slot(2), :], s, "a", t.g))], 6)

        @block.tensor
        def _(pe):
            def turn_x(t):
                u = t.slot(2)
                pe.wait_ge(s("x2"), t.g + 1)
                if not t.early(2):
                    pe.wait_ge(s("xT_sb"), t.g - 1)
                for f in range(2):
                    for k in range(K4):
                        last = pe.transpose(turn[:, 2 * u + f, k * P:(k + 1) * P], x[:, t.slot(6), k, f * P:(f + 1) * P], c.ident[:, :])
                last.then_inc(s("xT"), 1)

            def product(t):
                u = t.slot(2)
                if not t.early(2):
                    pe.wait_ge(s("relu"), t.g - 1)
                for b in range(2):
                    pe.matmul(prod[:, 2 * u + b, :], c.ones[0:3, :], c.bias_parts[:, :], start=True, stop=False)
                pe.wait_ge(s("xT_sb"), t.g + 1)
                for k in range(K4):
                    for f in range(2):
                        last = pe.matmul(tiles(t)[:, k, :], xT[:, u, f, k * P:(k + 1) * P], c.wg[:, f, 0:D],
                                         start=False, stop=(f == 1 and k % 2 == 1))
                last.then_inc(s("prod"), 1)
            skewed(pe, NG, [(3, product), (2, turn_x)], 6)


def attention_layer(c, layer):
    nc = c.nc
    side = c.d
    two = layer == 2
    H = H2 if two else H3
    W = D + H
    kinds = 2 if two else 1
    source = c.x2_dram if two else c.x3_dram
    target = c.x3_dram if two else c.out
    with c.phase() as ctx:
        pre = f"l{layer}_"
        sb = lambda n, shape, dt=F32: c.sb(pre + n, shape, dt, ctx=ctx)
        xs, xd = sb("xs", [P, 3, K4, D]), sb("xd", [P, 6, K4, D])
        at, at_last = sb("at", [P, 6, 2, K4], I32), sb("at_last", [P, 3, K4], I32)
        keys, cuts = sb("keys", [P, 2, ROWS]), sb("cuts", [H3, 2, ROWS + 1])
        same, cont = sb("same", [P, 3, K4, P]), sb("cont", [P, 3, K4, P])
        xT = sb("xT", [P, 2, 2, ROWS])
        hs, hd = (sb("hs", [P, 2, K4, D]), sb("hd", [P, 6, K4, D])) if two else (None, None)
        score, e = sb("score", [P, 2, 2, K4, 2 * H2]), sb("e", [P, 2, 2, K4, H])
        esc, top = sb("esc", [P, K4, H]), sb("top", [P, 2, K4, H])
        run_max, seg_max = sb("run_max", [H3, 2, ROWS]), sb("seg_max", [H3, ROWS])
        prob, fade = sb("prob", [P, 3, 2, K4, H]), sb("fade", [P, 2, H])
        msg, total, carry = sb("msg", [P, 2, K4, W]), sb("total", [P, 2, K4, W]), sb("carry", [P, W])
        den, r, y = sb("den", [P, K4, H]), sb("r", [P, 2, K4, D]), sb("y", [P, 3, K4, D])
        square = sb("square", [P, K4, D]) if two else None
        stats, mv, rs = sb("stats", [P, K4, 6]), sb("mv", [P, K4, 2]), sb("rs", [P, K4])
        ss, rn, guarded = (sb(n, [P, 2, K4]) for n in ("ss", "rn", "guarded"))
        work = sb("work", [P, K4])
        ps_turn = c.ps(pre + "ps_turn", [P, 2, 512], ctx=ctx)
        ps_h = c.ps(pre + "ps_h", [P, K4, D], ctx=ctx) if two else None
        ps_acc = c.ps(pre + "ps_acc", [P, 2, 512], ctx=ctx)
        ps_score = c.ps(pre + "ps_score", [P, 512], ctx=ctx)
        ps_max = c.ps(pre + "ps_max", [P, 512], ctx=ctx)
        raw = ps_score[:, 0:2 * K4 * 2 * H2].rearrange("p (o k h) -> p o k h", o=2, k=K4)
        back = ps_max[:, 0:K4 * H].rearrange("p (k h) -> p k h", k=K4)
        head_of = ps_max[:, 256:256 + H]
        s = signals(c, pre)
        keyed = [s(f"keyed{u}") for u in range(2)]
        got_s, sent = ([s(f"{n}{u}") for u in range(3)] for n in ("got_s", "sent"))
        got_d = [s(f"got_d{u}") for u in range(6)]
        if two:
            split = lambda v: v.rearrange("p k (h d) -> p k h d", h=H)
            spread = lambda v: v.rearrange("p k (h o) -> p k h o", o=1).to_broadcast([v.shape[0], v.shape[1], H, D // H])
        else:
            split = lambda v: v.rearrange("p k (d h) -> p k d h", h=H)
            spread = lambda v: v.rearrange("p k (o h) -> p k o h", o=1).to_broadcast([v.shape[0], v.shape[1], D // H, H])
        one = lambda v: v.rearrange("p (o d) -> p o d", o=1)
        block = ctx.enter_context(nc.Block())

        @block.gpsimd
        def _(pool):
            def gather(t):
                u, v = t.slot(3), t.slot(6)
                if not t.early(3):
                    if two:
                        pool.wait_ge(s("xT"), 2 * (t.g - 2))
                    else:
                        pool.wait_ge(s("msg"), t.g - 2)
                if not t.early(6):
                    pool.wait_ge(s("summed"), t.g - 5)
                    pool.sem_inc(s("issuing"), 1)
                pool.tensor_copy(at[:, v, :, :], side["index"][:, bass.ds(t.g, 1), 0:2, :].rearrange("p o n k -> p (o n) k"))\
                    .then_inc(s("at"), 1)
                pool.wait_ge(s("at"), t.g + 1)
                pool.sem_inc(s("issuing"), 1)
                for to, kind, got in ((xs[:, u], OTHER, got_s[u]), (xd[:, v], OWN, got_d[v])):
                    for k in range(K4):
                        pool.indirect_dma_start(to[:, k, :], None, source[:, :],
                                                bass.IndirectOffsetOnAxis(ap=at[:, v, kind, k:k + 1], axis=0)).then_inc(got, 16)

            def scatter(t):
                v = t.slot(3)
                if not t.early(3):
                    pool.wait_ge(sent[v], t.turn(3) * 16 * K4)
                pool.tensor_copy(at_last[:, v, :], side["index"][:, bass.ds(t.g, 1), LAST, :].rearrange("p o k -> p (o k)"))\
                    .then_inc(s("at_last"), 1)
                pool.wait_ge(s("at_last"), t.g + 1)
                pool.wait_ge(s("y_done"), t.g + 1)
                pool.sem_inc(s("issuing"), 1)
                for k in range(K4):
                    pool.indirect_dma_start(target[:, :], bass.IndirectOffsetOnAxis(ap=at_last[:, v, k:k + 1], axis=0),
                                            y[:, v, k, :], None, bounds_check=N - 1, oob_is_err=False).then_inc(sent[v], 16)
            skewed(pool, GROUPS, [(0, gather), (7, scatter)], 6)
            for v in range(3):
                pool.wait_ge(sent[v], len(range(v, GROUPS, 3)) * 16 * K4)

        @block.sync
        def _(sp):
            def load(t):
                if not t.early(2):
                    sp.wait_ge(s("masked"), t.g - 1)
                load_keys(sp, side["keys"], keys[:, t.slot(2), :], t, 1, ROWS, 2, s("seg_max"), keyed)
                sp.dma_start(cuts[0:H, t.slot(2), :], side["cuts"][bass.ds(t.g * ROWS, ROWS + 1)].rearrange("(o n) -> o n", o=1)
                             .to_broadcast([H, ROWS + 1])).then_inc(keyed[t.slot(2)], 16)
            skewed(sp, GROUPS, [(0, load)], 6)

        @block.tensor
        def _(pe):
            def scores_across(t):
                pe.wait_ge(s("esc"), t.g + 1)
                pe.wait_ge(s("fade_sub"), t.g)
                for k in range(K4):
                    last = pe.matmul(ps_max[0:H, k * P:(k + 1) * P], esc[:, k, :], c.ident[:, :], start=True, stop=True)
                last.then_inc(s("escT"), 1)

            def accumulate(t, k):
                u, v = t.slot(2), t.slot(3)
                if k == 0:
                    pe.wait_ge(s("msg"), t.g + 1)
                    pe.wait_ge(s("masked"), t.g + 1)
                    pe.wait_ge(s("carry"), t.g + 1)
                    pe.wait_ge(s("total"), t.g * K4)
                pe.matmul(ps_acc[:, k % 2, 0:W], same[:, v, k, :], msg[:, u, k, :], start=True, stop=False)
                if k:
                    pe.wait_ge(s("total"), t.g * K4 + k)
                rest = carry[96:P, :] if k == 0 else total[96:P, u, k - 1, :]
                pe.matmul(ps_acc[:, k % 2, 0:W], cont[96:P, v, k, :], rest, start=False, stop=True).then_inc(s("acc"), 1)

            def turn(t, n):
                x, got, i = ((xs[:, t.slot(3)], got_s[t.slot(3)], t.turn(3)), (xd[:, t.slot(6)], got_d[t.slot(6)], t.turn(6)))[n]
                pe.wait_ge(got, (i + 1) * 16 * K4)
                pe.wait_ge(s("xT_sb"), 2 * t.g + n)
                for f in range(2):
                    for k in range(K4):
                        last = pe.transpose(ps_turn[:, f, k * P:(k + 1) * P], x[:, k, f * P:(f + 1) * P], c.ident[:, :])
                last.then_inc(s("xT"), 1)

            def project(t, n):
                pe.wait_ge(s("xT_sb"), 2 * t.g + n + 1)
                if two:
                    pe.wait_ge(s("h_sb"), 2 * t.g + n)
                    for k in range(K4):
                        for f in range(2):
                            last = pe.matmul(ps_h[:, k, :], xT[:, n, f, k * P:(k + 1) * P], c.wg[:, f, 0:D],
                                             start=(f == 0), stop=(f == 1))
                    last.then_inc(s("h"), 1)

            def raw_scores(t):
                pe.wait_ge(s("score"), t.g)
                for n in range(2):
                    for k in range(K4):
                        for f in range(2):
                            vec = c.wg[:, f, D:D + 2 * H2] if two else c.wuv[:, f, n * H3:(n + 1) * H3]
                            last = pe.matmul(raw[:, n, k, :], xT[:, n, f, k * P:(k + 1) * P], vec, start=(f == 0), stop=(f == 1))
                last.then_inc(s("raw"), 1)

            def maxima_back(t):
                pe.wait_ge(s("seg_max"), t.g + 1)
                for k in range(K4):
                    last = pe.matmul(back[:, k, :], seg_max[0:H, k * P:(k + 1) * P], c.ident[0:H, 0:H], start=True, stop=True)
                last.then_inc(s("back"), 1)

            def first_maximum(t):
                pe.wait_ge(s("top"), t.g + 1)
                pe.matmul(head_of, c.first[:, :], top[:, t.slot(2), 0, :], start=True, stop=True).then_inc(s("head_of"), 1)

            at_ = lambda fn, *args: (lambda t: fn(t, *args))
            skewed(pe, GROUPS, [(1, at_(turn, 0)), (2, scores_across), (3, at_(accumulate, 0)), (3, at_(accumulate, 1)),
                                (1, at_(project, 0)), (2, maxima_back), (3, at_(accumulate, 2)), (1, at_(turn, 1)),
                                (3, at_(accumulate, 3)), (2, first_maximum), (1, at_(project, 1)), (1, raw_scores)], 6)

        @block.scalar
        def _(act):
            log_exp_tables(nc, act)
            def totals(t, k):
                act.wait_ge(s("acc"), t.g * K4 + k + 1)
                if k == 0 and not t.early(2):
                    act.wait_ge(s("total_used"), t.g - 1)
                if k == K4 - 1:
                    act.wait_ge(s("carry"), t.g + 1)
                act.activation(total[:, t.slot(2), k, :], ps_acc[:, k % 2, 0:W], ACT.Copy).then_inc(s("total"), 1)

            def copy(t, n):
                act.wait_ge(s("xT"), 2 * t.g + n + 1)
                act.wait_ge(s("raw"), t.g)
                act.activation(xT[:, n, :, :], ps_turn[:, :, :], ACT.Copy).then_inc(s("xT_sb"), 1)

            def features(t, n):
                if two:
                    act.wait_ge(s("h"), 2 * t.g + n + 1)
                    if n == 0 and not t.early(2):
                        act.wait_ge(s("msg"), t.g - 1)
                    if n == 1 and not t.early(6):
                        act.wait_ge(s("own_used"), t.g - 5)
                    act.activation((hs[:, t.slot(2)], hd[:, t.slot(6)])[n], ps_h[:, :, :], ACT.Copy).then_inc(s("h_sb"), 1)

            def exp_prob(t):
                act.wait_ge(s("below"), t.g + 1)
                act.activation(prob[:, t.slot(3), 0:kinds, :, :], prob[:, t.slot(3), 0:kinds, :, :], ACT.Exp).then_inc(s("prob"), 1)

            def exp_fade(t):
                act.wait_ge(s("fade_in"), t.g + 1)
                act.activation(fade[96:P, t.slot(2), :], fade[96:P, t.slot(2), :], ACT.Exp).then_inc(s("fade"), 1)

            def scores(t):
                act.wait_ge(s("raw"), t.g + 1)
                act.activation(score[:, t.slot(2), :, :, :], raw, ACT.Copy).then_inc(s("score"), 1)

            def norm(t):
                u = t.slot(2)
                act.wait_ge(s("biased"), t.g + 1)
                act.activation(r[:, u, :, :], r[:, u, :, :], ACT.Relu).then_inc(s("relu"), 1)
                act.wait_ge(s("relu"), t.g + 1)
                if not t.early(1):
                    act.wait_ge(s("squared"), t.g)
                for k in range(K4):
                    last = act.activation(square[:, k, :], r[:, u, k, :], ACT.Square, accum_out=ss[:, u, k:k + 1])
                last.then_inc(s("squared"), 1)
                act.wait_ge(s("squared"), t.g + 1)
                inverse_norm(act, c, ss[:, u, :], guarded[:, u, :], rn[:, u, :], s, t.g, c.consts[:, 2:3])

            at_ = lambda fn, *args: (lambda t: fn(t, *args))
            stages = [(1, at_(copy, 0)), (3, at_(totals, 0)), (3, at_(totals, 1)), (1, at_(features, 0)), (3, at_(totals, 2)),
                      (1, at_(copy, 1)), (2, exp_prob), (3, at_(totals, 3)), (2, exp_fade)]
            if two:
                stages.append((4, norm))
            stages += [(1, at_(features, 1)), (1, scores), (5, lambda t: row_scale(act, c, mv, rs[:, :], s, "b", t.g))]
            skewed(act, GROUPS, stages, 6)

        @block.vector
        def _(dve):
            def chained(name, ins, g):
                ins.then_inc(s(name), 1)
                dve.wait_ge(s(name), g + 1)

            dve.memset(total[:, 1, K4 - 1, :], 0.0).then_inc(s("clear"), 1)
            dve.memset(top[:, 1, :, :], 0.0).then_inc(s("clear"), 1)
            dve.memset(run_max[0:H, 1, :], LOW).then_inc(s("clear"), 1)
            dve.wait_ge(s("clear"), 3)

            def carry_in(t):
                u = t.slot(2)
                dve.wait_ge(s("fade"), t.g + 1)
                dve.wait_ge(s("total"), t.g * K4)
                if not t.early(1):
                    dve.wait_ge(s("acc"), (t.g - 1) * K4 + 1)
                before, f = total[96:P, 1 - u, K4 - 1:K4, :], fade[96:P, u, :]
                dve.tensor_tensor(split(one(carry[96:P, 0:D])), split(before[:, :, 0:D]), spread(one(f)), ALU.mult)
                dve.tensor_tensor(carry[96:P, D:W], total[96:P, 1 - u, K4 - 1, D:W], f, ALU.mult).then_inc(s("carry"), 1)

            def edge_scores(t):
                u = t.slot(2)
                dve.wait_ge(s("score"), t.g + 1)
                if two:
                    for n in range(2):
                        last = dve.tensor_tensor(e[:, u, n, :, :], score[:, u, n, :, 0:H], score[:, u, 1, :, H:2 * H], ALU.add)
                else:
                    chained("e_sum", dve.tensor_tensor(e[:, u, 0, :, :], score[:, u, 0, :, :], score[:, u, 1, :, :], ALU.add), t.g)
                    last = dve.tensor_tensor(e[:, u, 0, :, :], e[:, u, 0, :, :], over_tiles(c.bu[:, :]), ALU.add)
                chained("e_raw", last, t.g)
                last = dve.scalar_tensor_tensor(out=e[:, u, 0:kinds, :, :], in0=e[:, u, 0:kinds, :, :], scalar=0.2,
                                                in1=e[:, u, 0:kinds, :, :], op0=ALU.mult, op1=ALU.max)
                chained("e_leaky", last, t.g)
                dve.wait_ge(s("escT"), t.g)
                dve.tensor_tensor(esc[:, :, :], e[:, u, 0, :, :], e[:, u, kinds - 1, :, :], ALU.max).then_inc(s("esc"), 1)

            def masks(t):
                u, v = t.slot(2), t.slot(3)
                dve.wait_ge(keyed[u], 32 * (t.turn(2) + 1))
                if not t.early(3):
                    dve.wait_ge(s("acc"), (t.g - 2) * K4)
                rows = keys[:, u, :].rearrange("p (k j) -> p k j", k=K4)
                dve.tensor_tensor(same[:, v, :, :], rows, along(side["key"][:, bass.ds(t.g * K4 + 1, K4)]), ALU.is_equal)
                dve.tensor_tensor(cont[96:P, v, :, :], rows[96:P, :, :], along(side["key_end"][96:P, bass.ds(t.g * K4, K4)]),
                                  ALU.is_equal).then_inc(s("masked"), 1)

            def scans(t):
                u = t.slot(2)
                dve.wait_ge(s("escT"), t.g + 1)
                dve.wait_ge(keyed[u], 32 * (t.turn(2) + 1))
                chained("run_max", dve.tensor_tensor_scan(run_max[0:H, u, :], cuts[0:H, u, 0:ROWS], ps_max[0:H, :],
                                                          run_max[0:H, 1 - u, ROWS - 1:ROWS], ALU.add, ALU.max), t.g)
                dve.wait_ge(s("back"), t.g)
                dve.tensor_tensor_scan(seg_max[0:H, :][:, ::-1], cuts[0:H, u, 1:ROWS + 1][:, ::-1], run_max[0:H, u, :][:, ::-1],
                                       LOW, ALU.add, ALU.max).then_inc(s("seg_max"), 1)

            def subtract_max(t):
                u, v = t.slot(2), t.slot(3)
                dve.wait_ge(s("back"), t.g + 1)
                chained("top", dve.tensor_copy(top[:, u, :, :], back), t.g)
                if not t.early(3):
                    dve.wait_ge(s("own_used"), t.g - 2)
                for n in range(kinds):
                    last = dve.tensor_tensor(prob[:, v, n, :, :], e[:, u, n, :, :], top[:, u, :, :], ALU.subtract)
                last.then_inc(s("below"), 1)

            def fade_out(t):
                u = t.slot(2)
                dve.wait_ge(s("head_of"), t.g + 1)
                chained("fade_sub", dve.tensor_tensor(fade[96:P, u, :], top[96:P, 1 - u, K4 - 1, :], head_of[96:P, :], ALU.subtract), t.g)
                dve.tensor_scalar(fade[96:P, u, :], fade[96:P, u, :], 0.0, None, ALU.min).then_inc(s("fade_in"), 1)

            def messages(t):
                u = t.slot(2)
                dve.wait_ge(s("prob"), t.g + 1)
                if not t.early(2):
                    dve.wait_ge(s("acc"), (t.g - 1) * K4)
                p = prob[:, t.slot(3), 0, :, :]
                dve.tensor_copy(msg[:, u, :, D:W], p)
                last = dve.tensor_tensor(split(msg[:, u, :, 0:D]), split(hs[:, u, :, :] if two else xs[:, t.slot(3), :, :]), spread(p), ALU.mult)
                last.then_inc(s("msg"), 1)

            def own_loop(t):
                if two:
                    dve.wait_ge(s("total"), (t.g + 1) * K4)
                    if not t.early(2):
                        dve.wait_ge(s("summed"), t.g - 1)
                    p = prob[:, t.slot(3), 1, :, :]
                    dve.tensor_tensor(den[:, :, :], total[:, t.slot(2), :, D:W], p, ALU.add)
                    chained("own_used", dve.tensor_tensor(split(r[:, t.slot(2), :, :]), split(hd[:, t.slot(6), :, :]), spread(p), ALU.mult), t.g)
                    dve.tensor_tensor(r[:, t.slot(2), :, :], r[:, t.slot(2), :, :], total[:, t.slot(2), :, 0:D], ALU.add).then_inc(s("total_used"), 1)
                    chained("den", dve.reciprocal(den[:, :, :], den[:, :, :]), t.g)

            def divide(t):
                v = t.slot(4)
                if two:
                    chained("divided", dve.tensor_tensor(split(r[:, t.slot(2), :, :]), split(r[:, t.slot(2), :, :]), spread(den[:, :, :]), ALU.mult), t.g)
                    dve.tensor_tensor(r[:, t.slot(2), :, :], r[:, t.slot(2), :, :], over_tiles(c.bias[:, :]), ALU.add).then_inc(s("biased"), 1)
                else:
                    dve.wait_ge(s("total"), (t.g + 1) * K4)
                    chained("den", dve.reciprocal(den[:, :, :], total[:, t.slot(2), :, D:W]), t.g)
                    last = dve.tensor_tensor(split(r[:, t.slot(2), :, :]), split(total[:, t.slot(2), :, 0:D]), spread(den[:, :, :]), ALU.mult)
                    chained("total_used", last, t.g)
                    dve.sem_inc(s("own_used"), 1)

            def finish(t):
                v = t.slot(3)
                if not t.early(3):
                    dve.wait_ge(sent[v], t.turn(3) * 16 * K4)
                dve.wait_ge(got_d[t.slot(6)], (t.turn(6) + 1) * 16 * K4)
                own = xd[:, t.slot(6)]
                if two:
                    dve.wait_ge(s("rn"), t.g + 1)
                    newton(dve, norm_root(rn[:, t.slot(2), :], guarded[:, t.slot(2), :], work[:, :]), s("rn_newton"), t.g)
                    for k in range(K4):
                        last = dve.scalar_tensor_tensor(out=y[:, v, k, :], in0=r[:, t.slot(2), k, :], scalar=rn[:, t.slot(2), k:k + 1],
                                                        in1=own[:, k, :], op0=ALU.mult, op1=ALU.add)
                else:
                    last = dve.tensor_tensor(y[:, v, :, :], r[:, t.slot(2), :, :], own, ALU.add)
                chained("summed", last, t.g)
                row_stats(dve, y[:, v], stats, mv, s, "b", t.g)

            def normalize(t):
                row_apply(dve, y[:, t.slot(3)], y[:, t.slot(3)], mv, rs[:, :], s, "b", t.g, "y_done", work[:, :])
            skewed(dve, GROUPS, ([(2, edge_scores), (3, carry_in), (4, own_loop), (2, scans), (4, divide), (2, subtract_max), (6, normalize),
                                  (2, fade_out), (2, messages), (5, finish), (1, masks)] if two else
                                 [(3, carry_in), (2, edge_scores), (6, normalize), (2, scans), (5, finish), (1, masks),
                                  (4, own_loop), (2, subtract_max), (4, divide), (2, fade_out), (2, messages)]), 6)


_NAMES = {"x": "x", "src": "src", "dst": "dst", "ea": "edge_attr_64", "ew": "edge_weight", "fw1": "L0_gnn_fw1",
          "fb1": "L0_gnn_fb1", "fw2": "L0_gnn_fw2", "fb2": "L0_gnn_fb2", "w1": "L0_gnn_w1", "w2": "L0_gnn_w2",
          "b2": "L0_gnn_b2", "w3": "L0_gnn_w3", "b3": "L0_gnn_b3", "W": "L2_gnn_W", "att_src": "L2_gnn_att_src",
          "att_dst": "L2_gnn_att_dst", "bias": "L2_gnn_bias", "W_u": "L3_gnn_W_u", "b_u": "L3_gnn_b_u",
          "W_v": "L3_gnn_W_v"}


def build(nc, a, out, stop=None):
    with ExitStack() as ctx:
        c = Core(nc, ctx)
        c.out = out
        dram = lambda n, shape, dt=F32: nc.dram_tensor(n, shape, dt, kind="Internal").ap()
        c.h1_dram, c.h2_dram = dram("h1_rows", (EP + 1, D)), dram("h2_rows", (EP + 1, D))
        c.place_dram = dram("node_places", (N, 1), I32)
        c.a_dram, c.x3_dram = dram("a_rows", (N, D)), dram("x3_rows", (N, D))
        c.wg = c.sb("wg", [P, 2, D + 2 * H2])
        c.fw2T, c.w1T, c.w2T, c.w3T = (c.sb(n, [P, 2, D]) for n in ("fw2T", "w1T", "w2T", "w3T"))
        c.fw1T, c.wuv = c.sb("fw1T", [BASIS, D]), c.sb("wuv", [P, 2, 16])
        c.fb1, c.b2 = c.sb("fb1", [P, 2]), c.sb("b2", [P, 2])
        c.fb2, c.b3, c.bias, c.c0 = (c.sb(n, [P, D]) for n in ("fb2", "b3", "bias", "c0"))
        c.bu = c.sb("bu", [P, H3])
        c.ident, c.identb, c.first = c.sb("ident", [P, P]), c.sb("identb", [P, P], BF16), c.sb("first", [P, P])
        c.ltri, c.ones = c.sb("ltri", [P, P], BF16), c.sb("ones", [P, P], BF16)
        c.window, c.digits = c.sb("window", [P, 2 * P], BF16), c.sb("digits", [P, 256], BF16)
        c.digits_i, c.end = c.sb("digits_i", [P, 256], I32), c.sb("end", [P, 1])
        c.consts, c.zero_row = c.sb("consts", [P, 16]), c.sb("zero_row", [P, D])
        c.bias_parts = c.sb("bias_parts", [3, 2 * D], BF16)
        c.x2_dram = dram("x2_rows", (N, D))
        c.absent = c.sb("absent", [P, N // 125], I32)
        c.pay_d, c.pay_s = c.sb("pay_d", [P, T, 4], I32), c.sb("pay_s", [P, T, 4], I32)
        sides = {}
        for s, pay in (("d", c.pay_d), ("s", c.pay_s)):
            sides[s] = {"pay": pay, "key": c.sb(s + "_key", [P, T + 1]), "key_end": c.sb(s + "_key_end", [P, T]),
                        "index": c.sb(s + "_index", [P, GROUPS, 4, K4], I32),
                        "keys": dram(s + "_keys", (EP + 2,)), "w": c.sb(s + "_w", [P, T]), "w8": c.sb(s + "_w8", [P, T]),
                        "cuts": dram(s + "_cuts", (EP + 1,)),
                        "rows": dram(s + "_sorted", (EP, 4), I32), "rows0": dram(s + "_half_sorted", (EP, 4), I32)}
            sides[s]["columns"] = [(1, N - 1), (0, N - 1), (3, E - 1)]
        c.d, c.s = sides["d"], sides["s"]
        c.cutoff, c.s_place = c.sb("cutoff", [P, T]), c.sb("s_place", [P, GROUPS, K4], I32)
        setup_phase(c, a)
        if stop == "setup": return c
        payload_phase(c, a)
        for s in ("d", "s"):
            sort_pass(c, s + "0_", sides[s]["pay"], 0, sides[s]["rows0"])
            sort_pass(c, s + "1_", sides[s]["pay"], 8, sides[s]["rows"])
            index_phase(c, s + "_ix_", sides[s])
        if stop == "sort": return c
        node_pass_one(c, a)
        cosine_phase(c)
        if stop == "p1": return c
        filter_layer(c, a)
        if stop == "l0": return c
        propagation_round(c, 1)
        if stop == "l11": return c
        propagation_round(c, 2)
        propagation_round(c, 3)
        if stop == "l1": return c
        node_pass_two(c)
        if stop == "p2": return c
        attention_layer(c, 2)
        attention_layer(c, 3)


_INS = ["x", "src", "dst", "edge_attr_64", "edge_weight", "L0_gnn_fw1", "L0_gnn_fb1", "L0_gnn_fw2", "L0_gnn_fb2",
        "L0_gnn_w1", "L0_gnn_w2", "L0_gnn_b2", "L0_gnn_w3", "L0_gnn_b3", "L2_gnn_W", "L2_gnn_att_src",
        "L2_gnn_att_dst", "L2_gnn_bias", "L3_gnn_W_u", "L3_gnn_b_u", "L3_gnn_W_v"]


def kernel(**inputs):
    import numpy as np
    import concourse.bacc as bacc
    from concourse.bass_utils import run_bass_kernel_spmd

    nc = bacc.Bacc("TRN2", target_bir_lowering=False, num_devices=1)
    arrays, given = {}, {}
    for name in _INS:
        array = np.ascontiguousarray(inputs[name])
        arrays[name + "_in"] = array
        given[name] = nc.dram_tensor(name + "_in", array.shape, mybir.dt.from_np(array.dtype), kind="ExternalInput").ap()
    out = nc.dram_tensor("out", (N, D), F32, kind="ExternalOutput").ap()
    build(nc, {short: given[name] for short, name in _NAMES.items()}, out)
    result = run_bass_kernel_spmd(nc, [arrays], core_ids=[0])
    return result.results[0]["out"]
```
